# Optimizing a Trainium2 kernel written in Bass

```python
import numpy as np
import jax
import jax.numpy as jnp

def _softmax(x, axis=-1):
    return jax.nn.softmax(x, axis=axis)

def _gelu(x):
    return jax.nn.gelu(x, approximate=True)

def _silu(x):
    return jax.nn.silu(x)

def _sigmoid(x):
    return jax.nn.sigmoid(x)

def _layernorm(x, axis=-1, eps=1e-05):
    m = jnp.mean(x, axis=axis, keepdims=True)
    v = jnp.var(x, axis=axis, keepdims=True)
    return (x - m) / jnp.sqrt(v + eps)

def _scatter_add(tgt, idx, src, axis=0):
    return tgt.at[idx].add(src)

def _segment_sum(src, seg, n):
    return jax.ops.segment_sum(src, seg, n)
kernel_name = 'mk_flamingo_gated_d2_seqx_r4_4e20e2'

def setup_inputs(seed: int=0):
    np.random.seed(seed)
    _w = jnp.asarray

    def _rec_inputs():
        import jax
        import jax.numpy as jnp
        _rk = jax.random.key(seed)
        x = 7.22e-05 + 1 * jax.random.normal(jax.random.fold_in(_rk, 1), (16, 256, 512), jnp.float32)
        _lenS = 256 - jax.random.randint(jax.random.fold_in(_rk, 7), (16,), 0, max(1, 256 // 4) + 1, jnp.int32)
        _lenS2 = 256 - jax.random.randint(jax.random.fold_in(_rk, 8), (16,), 0, max(1, 256 // 4) + 1, jnp.int32)
        _ctx_2048P = jax.random.normal(jax.random.fold_in(_rk, 11), (16, 16, 512), jnp.float32)
        _ctx_2048c = jax.random.dirichlet(jax.random.fold_in(_rk, 511), 0.3 * jnp.ones((16,), jnp.float32), (16, 256))
        _ctx_2048t = jnp.einsum('bsk,bkd->bsd', _ctx_2048c, _ctx_2048P)
        _ctx_2048t = _ctx_2048t * jax.lax.rsqrt(jnp.mean(jnp.square(_ctx_2048t)) + 1e-12) * 0.953939
        ctx_2048 = 4.13588e-05 + 0.999923 * (_ctx_2048t + 0.3 * jax.random.normal(jax.random.fold_in(_rk, 611), (16, 256, 512), jnp.float32))
        _validS = jnp.arange(256)[None, :] < _lenS[:, None]
        _validS2 = jnp.arange(256)[None, :] < _lenS2[:, None]
        _causal = jnp.tril(jnp.ones((256, 256), dtype=bool))
        mask_BxS2_bk0 = jnp.logical_not(jnp.broadcast_to(_validS2[:, :], (16, 256)))
        _g = jax.random.normal(jax.random.fold_in(_rk, 9001), (2, 2), jnp.float32)
        _g = jnp.sign(_g) * jnp.maximum(jnp.abs(_g), 1.0) + (_g == 0) * 1.0
        g_xattn = _g[0]
        g_ffn = _g[1]
        return (x, ctx_2048, mask_BxS2_bk0, g_xattn, g_ffn)
    x, ctx_2048, mask_BxS2_bk0, g_xattn, g_ffn = _rec_inputs()

    def _L0_xattn_setup():
        import jax, jax.numpy as jnp
        import numpy as np
        N_HEAD = 8
        key = jax.random.key(seed)
        k1, k2, k3 = jax.random.split(key, 3)
        b, d, m = (4, 256, 512)
        c, n = (256, 512)
        q = jax.random.normal(k1, (b, d, m), dtype=jnp.float32)
        k = jax.random.normal(k2, (d // d * b, d, n), dtype=jnp.float32).reshape(b, d, n)
        v = jax.random.normal(k3, (b, c, n), dtype=jnp.float32)
        return {'q': q, 'k': k, 'v': v}
    _L0_xattn_all = _L0_xattn_setup()
    _L0_xattn_in = {k: v for k, v in _L0_xattn_all.items() if k in ()}
    del _L0_xattn_all

    def _L0_ffn_setup():
        import jax, jax.numpy as jnp
        import numpy as np
        DIM = 512
        N_EXPERTS = 8
        TOP_K = 2
        key = jax.random.key(seed)
        ks = jax.random.split(key, 5)
        x = jax.random.normal(ks[0], (4, 1024, DIM), dtype=jnp.float32)
        W_up = jax.random.normal(ks[1], (DIM, DIM), dtype=jnp.float32) * (1.0 / np.sqrt(DIM))
        W_down = jax.random.normal(ks[2], (DIM, DIM), dtype=jnp.float32) * (1.0 / np.sqrt(DIM))
        W_gate = jax.random.normal(ks[3], (N_EXPERTS, DIM), dtype=jnp.float32) * (1.0 / np.sqrt(DIM))
        W_expert = jax.random.normal(ks[4], (DIM, DIM), dtype=jnp.float32) * (1.0 / np.sqrt(DIM))
        return {'x': x, 'W_up': W_up, 'W_down': W_down, 'W_gate': W_gate, 'W_expert': W_expert}
    _L0_ffn_all = _L0_ffn_setup()
    _L0_ffn_in = {k: v for k, v in _L0_ffn_all.items() if k in ('W_up', 'W_down', 'W_gate', 'W_expert')}
    del _L0_ffn_all

    def _L1_xattn_setup():
        import jax, jax.numpy as jnp
        import numpy as np
        key = jax.random.key(seed)
        k1, k2, k3 = jax.random.split(key, 3)
        B, S, D, M = (8, 512, 512, 128)
        hidden_states = jax.random.normal(k1, (B, S, D), dtype=jnp.float32)
        memory_tokens = jax.random.normal(k2, (B, M, D), dtype=jnp.float32)
        memory_mask = jax.random.randint(k3, (B, M), 0, 2).astype(jnp.bool_)
        return {'hidden_states': hidden_states, 'memory_tokens': memory_tokens, 'memory_mask': memory_mask}
    _L1_xattn_all = _L1_xattn_setup()
    _L1_xattn_in = {k: v for k, v in _L1_xattn_all.items() if k in ()}
    del _L1_xattn_all

    def _L1_ffn_setup():
        import jax, jax.numpy as jnp
        import numpy as np
        B, T, D, E, H = (4, 512, 512, 4, 2048)
        TOPK = 2
        CAPACITY_FACTOR = 1
        key = jax.random.key(seed)
        k0, k1, k2, k3 = jax.random.split(key, 4)
        x = jax.random.normal(k0, (B, T, D), dtype=jnp.float32)
        Wg = jax.random.normal(k1, (D, E), dtype=jnp.float32) * 0.02
        bg = jnp.zeros((E,), dtype=jnp.float32)
        W1 = jax.random.normal(k2, (E, D, H), dtype=jnp.float32) * (1.0 / np.sqrt(D))
        W2 = jax.random.normal(k3, (E, H, D), dtype=jnp.float32) * (1.0 / np.sqrt(H))
        return {'x': x, 'Wg': Wg, 'bg': bg, 'W1': W1, 'W2': W2}
    _L1_ffn_all = _L1_ffn_setup()
    _L1_ffn_in = {k: v for k, v in _L1_ffn_all.items() if k in ('Wg', 'bg', 'W1', 'W2')}
    del _L1_ffn_all
    return {'x': x, 'ctx_2048': ctx_2048, 'mask_BxS2_bk0': mask_BxS2_bk0, 'g_xattn': g_xattn, 'g_ffn': g_ffn, 'L0_ffn_W_up': _L0_ffn_in['W_up'], 'L0_ffn_W_down': _L0_ffn_in['W_down'], 'L0_ffn_W_gate': _L0_ffn_in['W_gate'], 'L0_ffn_W_expert': _L0_ffn_in['W_expert'], 'L1_ffn_Wg': _L1_ffn_in['Wg'], 'L1_ffn_bg': _L1_ffn_in['bg'], 'L1_ffn_W1': _L1_ffn_in['W1'], 'L1_ffn_W2': _L1_ffn_in['W2']}

def reference(x, ctx_2048, mask_BxS2_bk0, g_xattn, g_ffn, L0_ffn_W_up, L0_ffn_W_down, L0_ffn_W_gate, L0_ffn_W_expert, L1_ffn_Wg, L1_ffn_bg, L1_ffn_W1, L1_ffn_W2):
    import jax
    import jax.numpy as jnp

    def _L0_xattn_ref(q, k, v):
        import jax, jax.numpy as jnp
        import numpy as np
        N_HEAD = 8
        b, d, m = q.shape
        c = v.shape[1]
        h = N_HEAD
        qh = q.reshape(b * h, d // h, m)
        kh = k.reshape(b * h, d // h, -1)
        vh = v.reshape(b * h, c // h, -1)
        scale = 1.0 / jnp.sqrt(jnp.asarray(d // h, dtype=q.dtype))
        qk = jnp.einsum('bdm,bdn->bmn', qh, kh) * scale
        sm = jax.nn.softmax(qk, axis=-1)
        ret = jnp.einsum('bmn,bcn->bcm', sm, vh)
        return ret.reshape(b, c, m)

    def _L0_ffn_ref(x, W_up, W_down, W_gate, W_expert):
        import jax, jax.numpy as jnp
        import numpy as np
        DIM = 512
        N_EXPERTS = 8
        TOP_K = 2
        logits = jnp.einsum('bsd,ed->bse', x, W_gate)
        routing_weights, selected_experts = jax.lax.top_k(logits, TOP_K)
        shared_out = jnp.einsum('bsd,od->bso', jax.nn.relu(jnp.einsum('bsd,od->bso', x, W_up)), W_down)
        rw = jax.nn.softmax(routing_weights, axis=-1)
        expert_out = jnp.einsum('bsd,do->bso', x, W_expert)
        moe_out = jnp.sum(rw, axis=-1, keepdims=True) * expert_out
        return shared_out + moe_out

    def _L1_xattn_ref(hidden_states, memory_tokens, memory_mask):
        import jax, jax.numpy as jnp
        import numpy as np
        B, S, D = hidden_states.shape
        scale = 1.0 / jnp.sqrt(jnp.asarray(D, hidden_states.dtype))
        scores = jnp.einsum('bsd,bmd->bsm', hidden_states, memory_tokens) * scale
        neg_inf = jnp.asarray(-1e+30, scores.dtype)
        scores = jnp.where(memory_mask[:, None, :], scores, neg_inf)
        attn = jax.nn.softmax(scores, axis=-1)
        readout = jnp.einsum('bsm,bmd->bsd', attn, memory_tokens)
        valid_b = jnp.any(memory_mask, axis=-1)
        out = jnp.where(valid_b[:, None, None], readout, jnp.zeros_like(readout))
        return out

    def _L1_ffn_ref(x, Wg, bg, W1, W2):
        import jax, jax.numpy as jnp
        import numpy as np
        B, T, D, E, H = (4, 512, 512, 4, 2048)
        TOPK = 2
        CAPACITY_FACTOR = 1
        Bq, Tq, Dq = x.shape
        N = Bq * Tq
        capacity = int(N * CAPACITY_FACTOR / E)
        flat_x = x.reshape(N, Dq)
        logits = flat_x @ Wg + bg
        top_vals, top_idx = jax.lax.top_k(logits, TOPK)
        sparse = jnp.full_like(logits, -jnp.inf)
        sparse = sparse.at[jnp.arange(N)[:, None], top_idx].set(top_vals)
        probs = jax.nn.softmax(sparse, axis=-1)
        out = jnp.zeros_like(flat_x)
        for i in range(E):
            assigned = (top_idx == i).any(axis=-1)
            score = jnp.where(assigned, probs[:, i], -jnp.inf)
            sel_p, sel_idx = jax.lax.top_k(score, capacity)
            p = jnp.where(jnp.isfinite(sel_p), sel_p, 0.0)[:, None]
            tok = flat_x[sel_idx]
            h = jax.nn.gelu(tok @ W1[i], approximate=False)
            y = h @ W2[i] * p
            out = out.at[sel_idx].add(y)
        return out.reshape(Bq, Tq, Dq)
    x = x + jnp.tanh(g_xattn[0]) * _L0_xattn_ref(_layernorm(x, axis=-1), ctx_2048, ctx_2048)
    x = x + jnp.tanh(g_ffn[0]) * _L0_ffn_ref(_layernorm(x, axis=-1), L0_ffn_W_up, L0_ffn_W_down, L0_ffn_W_gate, L0_ffn_W_expert)
    x = x + jnp.tanh(g_xattn[1]) * _L1_xattn_ref(_layernorm(x, axis=-1), ctx_2048, mask_BxS2_bk0)
    x = x + jnp.tanh(g_ffn[1]) * _L1_ffn_ref(_layernorm(x, axis=-1), L1_ffn_Wg, L1_ffn_bg, L1_ffn_W1, L1_ffn_W2)
    return x

_drawn_inputs = setup_inputs


def setup_inputs(seed=0):
    import zlib

    import numpy as np

    out = dict(_drawn_inputs(seed))
    spreads = {'g_ffn': (-1.0, 0.6), 'L1_ffn_bg': (0.0, 0.1)}
    factors = {'L0_ffn_W_gate': 8.0}
    for name, (base, spread) in spreads.items():
        noise = np.random.default_rng([zlib.crc32(name.encode()), seed]).standard_normal(out[name].shape)
        drawn = base * np.exp(spread * noise) if base else spread * noise
        out[name] = jnp.asarray(drawn.astype(out[name].dtype))
    for name, factor in factors.items():
        out[name] = (out[name] * factor).astype(out[name].dtype)
    return out
```

```python
from contextlib import ExitStack

import numpy as np

import concourse.bass as bass
from concourse import mybir

P = 128
F32 = mybir.dt.float32
F32R = mybir.dt.float32r
I32 = mybir.dt.int32
U32 = mybir.dt.uint32
U8 = mybir.dt.uint8
ALU = mybir.AluOpType
ACT = mybir.ActivationFunctionType
AX = mybir.AxisListType.X
EPS = 1e-5


def wait(eng, sem, value):
    if isinstance(value, int) and value <= 0:
        return
    eng.wait_ge(sem, value)


RSQRT_STEPS = 12


def inverse_sqrt(nc, dve, y, var, tmp, step, base):
    nc.vector.tensor_scalar(tmp[0], var, EPS, None, ALU.add).then_inc(step, 1)
    dve.wait_ge(step, base + 1)
    nc.vector.tensor_scalar(tmp[1].bitcast(I32), tmp[0].bitcast(I32), 1, None,
                            ALU.logical_shift_right).then_inc(step, 1)
    dve.wait_ge(step, base + 2)
    nc.vector.tensor_scalar(y.bitcast(I32), tmp[1].bitcast(I32), -1.0, float(0x5F3759DF),
                            ALU.mult, ALU.add).then_inc(step, 1)
    for n in range(3):
        done = base + 3 + 3 * n
        dve.wait_ge(step, done)
        nc.vector.tensor_tensor(tmp[1], y, y, ALU.mult).then_inc(step, 1)
        dve.wait_ge(step, done + 1)
        nc.vector.scalar_tensor_tensor(out=tmp[2], in0=tmp[1], scalar=-0.5, in1=tmp[0],
                                       op0=ALU.mult, op1=ALU.mult).then_inc(step, 1)
        dve.wait_ge(step, done + 2)
        nc.vector.scalar_tensor_tensor(out=y, in0=tmp[2], scalar=1.5, in1=y,
                                       op0=ALU.add, op1=ALU.mult).then_inc(step, 1)


def row_major(t):
    return t.rearrange("b s d -> (b s) d")


def build_constants(nc, ctx, g_xattn, g_ffn):
    def sb(name, shape, dt):
        return ctx.enter_context(nc.sbuf_tensor(name, shape, dt))

    c = {
        "ident": sb("ident", [P, P], F32),
        "neg_ident": sb("neg_ident", [P, P], F32),
        "ones": sb("ones", [P, P], F32),
        "ones_r": sb("ones_r", [P, P], F32R),
        "gates": sb("gates", [P, 4], F32),
        "gates_raw": sb("gates_raw", [P, 4], F32),
    }
    with nc.semaphore("gates_loaded") as gates_loaded, nc.semaphore("cleared") as cleared, \
            nc.semaphore("const_step") as const_step, nc.Block() as block:
        @block.sync
        def _(sp):
            for n, g in enumerate((g_xattn, g_ffn)):
                sp.dma_start(c["gates_raw"][:, 2 * n:2 * n + 2],
                             bass.AP(tensor=g.tensor, offset=0, ap=[[0, P], [1, 2]])).then_inc(gates_loaded, 16)
            sp.wait_ge(gates_loaded, 32)

        @block.scalar
        def _(act):
            act.wait_ge(gates_loaded, 32)
            nc.scalar.activation(c["gates"][:], c["gates_raw"][:], ACT.Tanh).then_inc(const_step, 1)
            act.wait_ge(const_step, 1)

        @block.gpsimd
        def _(pool):
            nc.gpsimd.memset(c["ident"][:], 0.0).then_inc(cleared, 1)
            nc.gpsimd.memset(c["ones"][:], 1.0).then_inc(cleared, 1)
            nc.gpsimd.memset(c["neg_ident"][:], 0.0).then_inc(cleared, 1)
            pool.wait_ge(cleared, 3)
            for name, v in (("ident", 1.0), ("neg_ident", -1.0)):
                nc.gpsimd.affine_select(out=c[name][:], in_=c[name][:], compare_op=ALU.not_equal, fill=v,
                                        base=0, pattern=[[-1, P]], channel_multiplier=1).then_inc(cleared, 1)
            nc.gpsimd.tensor_copy(c["ones_r"][:], c["ones"][:]).then_inc(cleared, 1)
            pool.wait_ge(cleared, 6)
    return c


def column_attention(nc, c, x_in, ctx_in, xhat_d, x_res):
    D = x_in.shape[2]
    TOK = x_in.shape[0] * x_in.shape[1]
    TILES = TOK // P
    BATCHES = TILES // 2
    HEADS = 4
    ROWS = P // HEADS
    NT = D // P
    SCALE = float(np.float32(1.0) / np.sqrt(np.float32(ROWS)))
    NORM_STEPS = 4 + RSQRT_STEPS
    ORDER = (0, 2, 1, 3)
    x_t = row_major(x_in).rearrange("(t p) d -> p t d", p=P)
    ctx_t = row_major(ctx_in).rearrange("(t p) d -> t p d", p=P)
    ctx_h = row_major(ctx_in).rearrange("(t h r) d -> t r h d", h=HEADS, r=ROWS)
    xhat_t = xhat_d.rearrange("(t p) d -> t p d", p=P)
    xhat_h = xhat_d.rearrange("(t h r) d -> t r h d", h=HEADS, r=ROWS)
    NEG_IDENT4 = c["neg_ident"][:].unsqueeze(1).broadcast_to([P, NT, P])

    with ExitStack() as ctx:
        def sb(name, shape, dt=F32):
            return ctx.enter_context(nc.sbuf_tensor(name, shape, dt))

        def sem(name):
            return ctx.enter_context(nc.semaphore(name))

        ctx_nat = sb("ctx_nat", [P, 2, D])
        k_raw = sb("k_raw", [P, 2, HEADS, D])
        q_raw = sb("q_raw", [P, 2, HEADS, D])
        k_stack = sb("k_stack", [P, 2, HEADS, D], F32R)
        q_stack = sb("q_stack", [P, 2, HEADS, D], F32R)
        v_ones = sb("v_ones", [P, 2, NT, HEADS, 2 * ROWS])
        probs = sb("probs", [P, 2, NT, D])
        maxima = sb("maxima", [P, 2, NT])
        neg_max_diag = sb("neg_max_diag", [P, 2, NT, P], F32R)
        xhat = sb("xhat", [P, 2, D])
        stats = sb("stats", [P, 2, 6])
        mean_var = sb("mean_var", [P, 2, 2])
        rstd = sb("rstd", [P, 2])
        fence = sb("fence", [P, 1])
        tmp3 = sb("tmp3", [P, 3, 2])
        outputs = sb("outputs", [P, D])
        denominators = sb("denominators", [P, D])
        recip = sb("recip", [P, D])
        gated = sb("gated", [P, 2, D])
        ps_s = [ctx.enter_context(nc.psum_tensor(f"ps_s{n}", [P, D], F32)) for n in range(2)]
        ps_st = [ctx.enter_context(nc.psum_tensor(f"ps_st{n}", [P, D], F32)) for n in range(2)]
        ps_od = [ctx.enter_context(nc.psum_tensor(f"ps_od{n}", [P, D], F32)) for n in range(2)]
        ps_v = ctx.enter_context(nc.psum_tensor("ps_v", [P, NT, P], F32))

        x_loaded = sem("x_loaded")
        ctx_loaded = [sem(f"ctx_loaded{u}") for u in range(2)]
        k_loaded = [sem(f"k_loaded{u}") for u in range(2)]
        q_loaded = [sem(f"q_loaded{u}") for u in range(2)]
        xhat_stored = sem("xhat_stored")
        ln_step = sem("ln_step")
        xhat_ready = sem("xhat_ready")
        hi_ready = sem("hi_ready")
        lo_ready = sem("lo_ready")
        ones_ready = sem("ones_ready")
        v_transposed = sem("v_transposed")
        v_ready = sem("v_ready")
        s_done = sem("s_done")
        reduced = sem("reduced")
        diag_ready = sem("diag_ready")
        st_done = sem("st_done")
        exp_done = sem("exp_done")
        pv_done = sem("pv_done")
        evacuated = sem("evacuated")
        recip_done = sem("recip_done")
        gated_done = sem("gated_done")
        x_added = sem("x_added")

        block = ctx.enter_context(nc.Block())

        def batches(eng, body):
            body(0)
            with eng.Fori(1, BATCHES - 1) as i:
                body(i)
            body(BATCHES - 1)

        def is_last(i):
            return isinstance(i, int) and i == BATCHES - 1

        @block.sync
        def _(sp):
            sp.dma_start(x_res[:, 0:2, :], x_t[:, 0:2, :]).then_inc(x_loaded, 16)

            def body(i):
                sp.wait_ge(x_loaded, 16 * i + 16)
                if not is_last(i):
                    sp.dma_start(x_res[:, bass.ds(2 * i + 2, 2), :],
                                 x_t[:, bass.ds(2 * i + 2, 2), :]).then_inc(x_loaded, 16)
                for u in range(2):
                    t = 2 * i + u
                    wait(sp, lo_ready, 12 * t - 12)
                    for r in range(4):
                        sp.dma_start(k_raw[ROWS * r:ROWS * r + ROWS, u, :, :],
                                     ctx_h[bass.ds(t, 1)].rearrange("o r h d -> (o r) h d")).then_inc(k_loaded[u], 16)
                    wait(sp, v_transposed, t - 1)
                    sp.dma_start(ctx_nat[:, u, :],
                                 ctx_t[bass.ds(t, 1)].rearrange("o p d -> (o p) d")).then_inc(ctx_loaded[u], 16)
                    sp.wait_ge(xhat_ready, t + 1)
                    sp.dma_start(xhat_t[bass.ds(t, 1)].rearrange("o p d -> (o p) d"),
                                 xhat[:, u, :]).then_inc(xhat_stored, 16)
                    sp.wait_ge(xhat_stored, 16 * t + 16)
                    for r in range(4):
                        sp.dma_start(q_raw[ROWS * r:ROWS * r + ROWS, u, :, :],
                                     xhat_h[bass.ds(t, 1)].rearrange("o r h d -> (o r) h d")).then_inc(q_loaded[u], 16)

            batches(sp, body)

        @block.gpsimd
        def _(pool):
            nc.gpsimd.memset(v_ones[:], 1.0).then_inc(ones_ready, 1)

            def split(i, u, g, prologue=False):
                t = 2 * i + u
                h, n = ORDER[g], 4 * t + g
                if prologue:
                    pool.wait_ge(ones_ready, 1)
                    wait(pool, lo_ready, 3 * n)
                else:
                    pool.wait_ge(diag_ready, n - 2)
                    if g == 1:
                        wait(pool, x_added, t - 1)
                pool.wait_ge(hi_ready, 2 * n + 1)
                nc.gpsimd.tensor_tensor(k_stack[64:P, u, h, :], k_raw[64:P, u, h, :], k_stack[64:P, u, h, :],
                                        ALU.subtract).then_inc(lo_ready, 1)
                pool.wait_ge(hi_ready, 2 * n + 2)
                for m, low in enumerate((slice(32, 64), slice(96, P))):
                    pool.wait_ge(lo_ready, 3 * n + 1 + m)
                    nc.gpsimd.tensor_tensor(q_stack[low, u, h, :], q_raw[low, u, h, :],
                                            q_stack[low, u, h, :], ALU.subtract).then_inc(lo_ready, 1)

            def diag(i, u, g, splits):
                n = 4 * (2 * i + u) + g
                pool.wait_ge(reduced, 4 * n + 4)
                pool.wait_ge(lo_ready, 3 * splits)
                wait(pool, st_done, 4 * n - 4)
                nc.gpsimd.tensor_tensor(
                    neg_max_diag[:, g % 2], NEG_IDENT4,
                    maxima[:, g % 2, :].unsqueeze(2).broadcast_to([P, NT, P]), ALU.mult).then_inc(diag_ready, 1)

            def add(i, u):
                t = 2 * i + u
                pool.wait_ge(gated_done, t + 1)
                xt = x_res[:, bass.ds(t, 1), :].rearrange("p o d -> p (o d)")
                nc.gpsimd.tensor_tensor(xt, gated[:, u, :], xt, ALU.add).then_inc(x_added, 1)

            for g in range(HEADS):
                split(0, 0, g, prologue=True)
            diag(0, 0, 0, HEADS)

            def body(i):
                for u in range(2):
                    for g in range(HEADS):
                        last_tile = is_last(i) and u == 1
                        n_next = 4 * (2 * i + u + 1) + g
                        splits = 4 * TILES if last_tile else n_next
                        if g < 3:
                            diag(i, u, g + 1, splits)
                        elif not last_tile:
                            diag(i + u, 1 - u, 0, splits)
                        if g == 1:
                            if u == 1:
                                add(i, 0)
                            elif not (isinstance(i, int) and i == 0):
                                add(i - 1, 1)
                        if not last_tile:
                            split(i + u, 1 - u, g)

            batches(pool, body)
            add(BATCHES - 1, 1)

        @block.scalar
        def _(act):
            def hi(i, u, g):
                h, t = ORDER[g], 2 * i + u
                act.wait_ge(k_loaded[u], 64 * i + 64)
                wait(act, st_done, 16 * t + 4 * g - 28)
                nc.scalar.activation(k_stack[:, u, h, :], k_raw[:, u, h, :], ACT.Copy).then_inc(hi_ready, 1)
                act.wait_ge(q_loaded[u], 64 * i + 64)
                nc.scalar.activation(q_stack[:, u, h, :], q_raw[:, u, h, :], ACT.Copy).then_inc(hi_ready, 1)

            def exps(i, u, g, ks):
                n = 4 * (2 * i + u) + g
                for k in ks:
                    act.wait_ge(st_done, 4 * n + k + 1)
                    wait(act, pv_done, 4 * n + k - 7)
                    nc.scalar.activation(probs[:, g % 2, k, :], ps_st[k % 2][:, :], ACT.Exp,
                                         scale=SCALE).then_inc(exp_done, 1)

            def evacuate(i, u, bank):
                t = 2 * i + u
                n = 2 * t + bank
                act.wait_ge(pv_done, 8 * n + 8)
                wait(act, gated_done, t)
                for h in (bank, bank + 2):
                    own, other = 32 * h, 32 * (h ^ 1)
                    nc.scalar.activation(outputs[own:own + 32, :], ps_od[bank][own:own + 32, :],
                                         ACT.Copy).then_inc(evacuated, 1)
                    nc.scalar.activation(denominators[own:own + 32, :], ps_od[bank][other:other + 32, :],
                                         ACT.Copy).then_inc(evacuated, 1)

            for g in range(HEADS):
                hi(0, 0, g)

            def body(i):
                for u in range(2):
                    for g in range(HEADS):
                        exps(i, u, g, (0, 1))
                        if g == 1:
                            if u == 1:
                                evacuate(i, 0, 1)
                            elif not (isinstance(i, int) and i == 0):
                                evacuate(i - 1, 1, 1)
                        if g == 3:
                            evacuate(i, u, 0)
                        if not (is_last(i) and u == 1):
                            hi(i + u, 1 - u, g)
                        exps(i, u, g, (2, 3))

            batches(act, body)
            evacuate(BATCHES - 1, 1, 1)

        @block.vector
        def _(dve):
            def statistics(i):
                base = NORM_STEPS * i
                dve.wait_ge(x_loaded, 16 * i + 16)
                for u in range(2):
                    xt = x_res[:, bass.ds(2 * i + u, 1), :].rearrange("p o d -> p (o d)")
                    nc.vector.bn_stats(stats[:, u, :], xt).then_inc(ln_step, 1)
                wait(dve, xhat_ready, 2 * i)
                dve.wait_ge(ln_step, base + 2)
                nc.vector.memset(fence[:], 0.0)
                for u in range(2):
                    nc.vector.bn_aggr(mean_var[:, u, :], stats[:, u, :]).then_inc(ln_step, 1)
                dve.wait_ge(ln_step, base + 4)
                inverse_sqrt(nc, dve, rstd[:], mean_var[:, :, 1], [tmp3[:, n, :] for n in range(3)],
                             ln_step, base + 4)

            def norm(i, u):
                t = 2 * i + u
                xt = x_res[:, bass.ds(t, 1), :].rearrange("p o d -> p (o d)")
                dve.wait_ge(ln_step, NORM_STEPS * i + NORM_STEPS)
                wait(dve, xhat_stored, 16 * t - 16)
                nc.vector.tensor_scalar(xhat[:, u, :], xt, mean_var[:, u, 0:1], rstd[:, u:u + 1],
                                        ALU.subtract, ALU.mult).then_inc(xhat_ready, 1)

            def v_copy(i, u):
                t = 2 * i + u
                dve.wait_ge(v_transposed, t + 1)
                wait(dve, pv_done, 16 * t - 16)
                src = ps_v[:].rearrange("p n (h r) -> p n h r", h=HEADS)
                for odd in range(2):
                    nc.vector.tensor_copy(v_ones[:, u, :, odd:HEADS:2, ROWS * odd:ROWS * odd + ROWS],
                                          src[:, :, odd:HEADS:2, :]).then_inc(v_ready, 1)

            def maxes(i, u, g):
                n = 4 * (2 * i + u) + g
                wait(dve, diag_ready, n - 1)
                for k in range(NT):
                    dve.wait_ge(s_done, 4 * n + k + 1)
                    nc.vector.tensor_reduce(maxima[:, g % 2, k:k + 1], ps_s[k % 2][:, :], AX,
                                            ALU.max).then_inc(reduced, 1)

            def divide(i, u):
                t = 2 * i + u
                dve.wait_ge(evacuated, 8 * t + 8)
                wait(dve, gated_done, t)
                nc.vector.reciprocal(recip[:], denominators[:]).then_inc(recip_done, 1)
                dve.wait_ge(recip_done, t + 1)
                wait(dve, x_added, t - 1)
                nc.vector.scalar_tensor_tensor(
                    out=gated[:, u, :], in0=outputs[:], scalar=c["gates"][:, 0:1], in1=recip[:],
                    op0=ALU.mult, op1=ALU.mult).then_inc(gated_done, 1)

            statistics(0)
            norm(0, 0)
            norm(0, 1)
            dve.wait_ge(ones_ready, 1)
            v_copy(0, 0)
            maxes(0, 0, 0)

            def body(i):
                for u in range(2):
                    last_tile = is_last(i) and u == 1
                    for g in range(HEADS):
                        if g < 3:
                            maxes(i, u, g + 1)
                        elif not last_tile:
                            maxes(i + u, 1 - u, 0)
                        if g == 0 and u == 0 and not is_last(i):
                            statistics(i + 1)
                        if g == 1 and not is_last(i):
                            norm(i + 1, u)
                        if g == 1:
                            if u == 1:
                                divide(i, 0)
                            elif not (isinstance(i, int) and i == 0):
                                divide(i - 1, 1)
                        if g == 2 and not last_tile:
                            v_copy(i + u, 1 - u)

            batches(dve, body)
            divide(BATCHES - 1, 1)

        @block.tensor
        def _(pe):
            def v_transpose(i, u):
                pe.wait_ge(ctx_loaded[u], 16 * i + 16)
                wait(pe, v_ready, 4 * i + 2 * u)
                for k in range(NT):
                    mm = nc.tensor.transpose(ps_v[:, k, :], ctx_nat[:, u, P * k:P * k + P], c["ident"][:])
                mm.then_inc(v_transposed, 1)

            def scores(i, u, g, k):
                h, n = ORDER[g], 4 * (2 * i + u) + g
                if k == 0:
                    pe.wait_ge(lo_ready, 3 * n + 3)
                wait(pe, reduced, 4 * n + k - 1)
                nc.tensor.matmul(ps_s[k % 2][:, :], q_stack[:, u, h, P * k:P * k + P], k_stack[:, u, h, :],
                                 start=True, stop=True).then_inc(s_done, 1)

            def scores_t(i, u, g, k):
                h, n = ORDER[g], 4 * (2 * i + u) + g
                if k == 0:
                    pe.wait_ge(diag_ready, n + 1)
                wait(pe, exp_done, 4 * n + k - 1)
                nc.tensor.matmul(ps_st[k % 2][:, :], k_stack[:, u, h, P * k:P * k + P], q_stack[:, u, h, :],
                                 start=True, stop=False)
                nc.tensor.matmul(ps_st[k % 2][:, :], c["ones_r"][:], neg_max_diag[:, g % 2],
                                 start=False, stop=True).then_inc(st_done, 1)

            def values(i, u, g, k):
                h, n = ORDER[g], 4 * (2 * i + u) + g
                t = 2 * i + u
                if k == 0 and g == 0:
                    pe.wait_ge(v_ready, 2 * t + 2)
                    wait(pe, evacuated, 8 * t - 4)
                if k == 0 and g == 2:
                    wait(pe, evacuated, 8 * t)
                pe.wait_ge(exp_done, 4 * n + k + 1)
                col = 64 * (h // 2)
                nc.tensor.matmul(ps_od[h % 2][col:col + 64, :], v_ones[:, u, k, h, :], probs[:, g % 2, k, :],
                                 start=(k == 0), stop=(k == NT - 1)).then_inc(pv_done, 1)

            v_transpose(0, 0)
            for k in range(NT):
                scores(0, 0, 0, k)

            def body(i):
                for u in range(2):
                    last_tile = is_last(i) and u == 1
                    for g in range(HEADS):
                        for k in range(NT):
                            if k < 2:
                                for kk in (2 * k, 2 * k + 1):
                                    if g < 3:
                                        scores(i, u, g + 1, kk)
                                    elif not last_tile:
                                        scores(i + u, 1 - u, 0, kk)
                            scores_t(i, u, g, k)
                            if g > 0:
                                values(i, u, g - 1, k)
                            elif u == 1:
                                values(i, 0, 3, k)
                            elif not (isinstance(i, int) and i == 0):
                                values(i - 1, 1, 3, k)
                        if g == 1 and not last_tile:
                            v_transpose(i + u, 1 - u)

            batches(pe, body)
            for k in range(NT):
                values(BATCHES - 1, 1, 3, k)


def split_weights(nc, c, t, w):
    D = t["L0_ffn_W_up"].shape[0]
    K = D // P
    E = t["L0_ffn_W_gate"].shape[0]
    with ExitStack() as ctx:
        raw = {n: ctx.enter_context(nc.sbuf_tensor(f"raw_{n}", [P, K, D], F32)) for n in ("up", "down", "expert")}
        raw_gate = ctx.enter_context(nc.sbuf_tensor("raw_gate", [E, D], F32))
        ps_w = ctx.enter_context(nc.psum_tensor("ps_w", [P, 8, D], F32))
        w_loaded = {n: ctx.enter_context(nc.semaphore(f"w_loaded_{n}"))
                    for n in ("up", "down", "expert", "gate", "route")}
        w_transposed = ctx.enter_context(nc.semaphore("w_transposed"))
        gate_transposed = ctx.enter_context(nc.semaphore("gate_transposed"))
        w_hi = ctx.enter_context(nc.semaphore("w_hi"))
        w_lo = ctx.enter_context(nc.semaphore("w_lo"))
        block = ctx.enter_context(nc.Block())

        @block.sync
        def _(sp):
            for n in ("up", "down", "expert"):
                sp.dma_start(raw[n][:], t[f"L0_ffn_W_{n}"].rearrange("(k p) n -> p k n", p=P)).then_inc(w_loaded[n], 16)
            sp.dma_start(raw_gate[:], t["L0_ffn_W_gate"]).then_inc(w_loaded["gate"], 16)
            sp.dma_start(w["route"][:], t["L1_ffn_Wg"].rearrange("(k p) n -> p k n", p=P)).then_inc(w_loaded["route"], 16)
            sp.dma_start(w["route_bias"][:], bass.AP(tensor=t["L1_ffn_bg"].tensor, offset=0,
                                                     ap=[[0, P], [1, 4]])).then_inc(w_loaded["route"], 16)
            sp.wait_ge(w_loaded["route"], 32)

        @block.tensor
        def _(pe):
            for m, n in enumerate(("up", "down")):
                pe.wait_ge(w_loaded[n], 16)
                for k in range(K):
                    for o in range(K):
                        mm = nc.tensor.transpose(ps_w[:, 4 * m + k, P * o:P * o + P], raw[n][:, o, P * k:P * k + P],
                                                 c["ident"][:])
                    mm.then_inc(w_transposed, 1)
            pe.wait_ge(w_loaded["gate"], 16)
            pe.wait_ge(w_lo, 2)
            for k in range(K):
                mm = nc.tensor.transpose(ps_w[:, 0, E * k:E * k + E], raw_gate[:, P * k:P * k + P],
                                         c["ident"][0:E, 0:E])
            mm.then_inc(gate_transposed, 1)

        def parts():
            out = []
            for m, n in enumerate(("up", "down")):
                for k in range(K):
                    out.append((w[n + "_hi"][:, k, :], w[n + "_lo"][:, k, :], ps_w[:, 4 * m + k, :],
                                w_transposed, 4 * m + k + 1))
            out.append((w["expert_hi"][:], w["expert_lo"][:], raw["expert"][:], w_loaded["expert"], 16))
            out.append((w["gate_hi"][:], w["gate_lo"][:],
                        ps_w[:, 0, 0:E * K].rearrange("p (k e) -> p k e", k=K), gate_transposed, 1))
            return out

        @block.scalar
        def _(act):
            for hi, lo, src, s, count in parts():
                act.wait_ge(s, count)
                nc.scalar.activation(hi, src, ACT.Copy).then_inc(w_hi, 1)

        @block.vector
        def _(dve):
            for n, (hi, lo, src, s, count) in enumerate(parts()):
                dve.wait_ge(w_hi, n + 1)
                nc.vector.tensor_tensor(lo, src, hi, ALU.subtract).then_inc(w_lo, 1)


def dense_and_memory(nc, c, w, t, x_res, xhat_d, out, logits):
    ctx_in, mask_in = t["ctx_2048"], t["mask_BxS2_bk0"]
    B, S, D = ctx_in.shape
    K = D // P
    U = S // P
    E = t["L0_ffn_W_gate"].shape[0]
    R = t["L1_ffn_Wg"].shape[1]
    SCALE = float(np.float32(1.0) / np.sqrt(np.float32(D)))
    NEG = 1e30
    CHAIN = 2 * U + RSQRT_STEPS
    RW = 8
    ctx_t = row_major(ctx_in).rearrange("(b u p) d -> b p u d", u=U, p=P)
    xhat_t = xhat_d.rearrange("(b u p) d -> b p u d", u=U, p=P)
    out_t = row_major(out).rearrange("(b u p) d -> b p u d", u=U, p=P)

    with ExitStack() as ctx:
        def sb(name, shape, dt=F32):
            return ctx.enter_context(nc.sbuf_tensor(name, shape, dt))

        def sem(name):
            return ctx.enter_context(nc.semaphore(name))

        def pair(name, shape):
            return sb(name + "_hi", shape, F32R), sb(name + "_lo", shape, F32R)

        xhat1 = sb("xhat1", [P, U, D])
        xhat2 = sb("xhat2", [P, U, D])
        xhat3 = sb("xhat3", [P, U, D])
        xt1 = pair("xt1", [P, K, S])
        xt2 = pair("xt2", [P, K, S])
        xt3 = sb("xt3", [P, K, S])
        hid = pair("hid", [P, K, S])
        mem_raw = sb("mem_raw", [P, U, D])
        mem = pair("mem", [P, U, D])
        mem_t = pair("mem_t", [P, K, S])
        masked = sb("masked", [P, U, S])
        probs = sb("mem_probs", [P, U, S])
        probs_t = pair("probs_t", [P, U, S])
        mask_u8 = sb("mask_u8", [P, B, S], U8)
        mask_f = sb("mask_f", [P, S])
        mask_add = sb("mask_add", [P, S])
        valid_gate = sb("valid_gate", [P, 2])
        row_max = sb("row_max", [P, U])
        neg_max = sb("neg_max", [P, U])
        row_sum = sb("row_sum", [P, U])
        row_scale = sb("row_scale", [P, 2, U])
        top_in = sb("top_in", [P, U, E])
        top = sb("top", [P, U, 8])
        rw = sb("rw", [P, 6, U])
        ln = {n: dict(stats=sb(f"st{n}", [P, U, 6]), mv=sb(f"mv{n}", [P, U, 2]), rstd=sb(f"rs{n}", [P, U]),
                      tmp=sb(f"tm{n}", [P, 3, U]), step=sem(f"ln{n}_step")) for n in (1, 2, 3)}
        fence = {n: sb(f"fence_{n}", [P, 1]) for n in ("top", "ln1a", "ln1b", "ln2a", "ln2b", "ln3a", "ln3b")}
        ps = ctx.enter_context(nc.psum_tensor("ps_b", [P, 8, 512], F32))
        halves = lambda bank: ps[:, bank, :].rearrange("p (k s) -> p k s", s=S)

        mem_loaded, mask_loaded = sem("mem_loaded"), sem("mask_loaded")
        xhat1_ready, xhat2_ready, xhat3_ready = sem("xhat1_ready"), sem("xhat2_ready"), sem("xhat3_ready")
        xt1_ps, xt1_hi, xt1_lo = sem("xt1_ps"), sem("xt1_hi"), sem("xt1_lo")
        xt2_ps, xt2_hi, xt2_lo = sem("xt2_ps"), sem("xt2_hi"), sem("xt2_lo")
        memt_ps, memt_hi, memt_lo = sem("memt_ps"), sem("memt_hi"), sem("memt_lo")
        mem_hi, mem_lo = sem("mem_hi"), sem("mem_lo")
        gate_ps, gate_copied = sem("gate_ps"), sem("gate_copied")
        rw_step, rw_exp = sem("rw_step"), sem("rw_exp")
        up_ps, hid_hi, hid_lo = sem("up_ps"), sem("hid_hi"), sem("hid_lo")
        down_ps, x1_step = sem("down_ps"), sem("x1_step")
        scores_ps = sem("scores_ps")
        mask_ready, valid_ready = sem("mask_ready"), sem("valid_ready")
        sm_step, exp_done = sem("sm_step"), sem("mem_exp_done")
        pt_ps, pt_hi, pt_lo = sem("pt_ps"), sem("pt_hi"), sem("pt_lo")
        read_ps, scale_step, x2_ready = sem("read_ps"), sem("scale_step"), sem("x2_ready")
        xt3_ps, xt3_ready = sem("xt3_ps"), sem("xt3_ready")
        route_ps, logits_ready = sem("route_ps"), sem("logits_ready")
        xhat_stored, x_stored = sem("xhat3_stored"), sem("x_stored")

        block = ctx.enter_context(nc.Block())

        def iterations(eng, body):
            for s in range(3):
                body(s, s < B, s >= 1, s >= 2, True)
            with eng.Fori(3, B - 1) as s:
                body(s, True, True, True, True)
            body(B - 1, True, True, True, False)
            body(B, False, True, True, False)
            body(B + 1, False, False, True, False)

        def x_tile(b, u):
            return x_res[:, bass.ds(U * b + u, 1), :].rearrange("p o d -> p (o d)")

        @block.sync
        def _(sp):
            sp.dma_start(mask_u8[:], bass.AP(tensor=mask_in.tensor, offset=0, ap=[[0, P], [S, B], [1, S]])
                         ).then_inc(mask_loaded, 16)

            def body(s, f, a, r, more):
                if f:
                    wait(sp, memt_ps, 2 * s)
                    wait(sp, mem_lo, s)
                    sp.dma_start(mem_raw[:], ctx_t[bass.ds(s, 1)].rearrange("o p u d -> (o p) u d")
                                 ).then_inc(mem_loaded, 16)

            iterations(sp, body)

        @block.gpsimd
        def _(pool):
            def body(s, f, a, r, more):
                if not a:
                    return
                b = s - 1
                pool.wait_ge(mem_hi, b + 1)
                wait(pool, read_ps, U * b)
                nc.gpsimd.tensor_tensor(mem[1][:], mem_raw[:], mem[0][:], ALU.subtract).then_inc(mem_lo, 1)

            iterations(pool, body)

        @block.scalar
        def _(act):
            def body(s, f, a, r, more):
                b = s - 1
                if r:
                    q = s - 2
                    act.wait_ge(xhat3_ready, U * q + U)
                    act.dma_start(xhat_t[bass.ds(q, 1)].rearrange("o p u d -> (o p) u d"),
                                  xhat3[:]).then_inc(xhat_stored, 16)
                    act.dma_start(out_t[bass.ds(q, 1)].rearrange("o p u d -> (o p) u d"),
                                  x_res[:, bass.ds(U * q, U), :]).then_inc(x_stored, 16)
                if f:
                    wait(act, down_ps, U * s)
                    for n in range(2):
                        act.wait_ge(xt1_ps, 2 * s + n + 1)
                        nc.scalar.activation(xt1[0][:, 2 * n:2 * n + 2, :], halves(n), ACT.Copy).then_inc(xt1_hi, 1)
                if a:
                    wait(act, scores_ps, b)
                    for n in range(2):
                        act.wait_ge(xt2_ps, 2 * b + n + 1)
                        nc.scalar.activation(xt2[0][:, 2 * n:2 * n + 2, :], halves(4 + n), ACT.Copy
                                             ).then_inc(xt2_hi, 1)
                    for n in range(2):
                        act.wait_ge(memt_ps, 2 * b + n + 1)
                        nc.scalar.activation(mem_t[0][:, 2 * n:2 * n + 2, :], halves(6 + n), ACT.Copy
                                             ).then_inc(memt_hi, 1)
                    act.wait_ge(mem_loaded, 16 * b + 16)
                    wait(act, read_ps, U * b)
                    wait(act, mem_lo, b)
                    nc.scalar.activation(mem[0][:], mem_raw[:], ACT.Copy).then_inc(mem_hi, 1)
                if f:
                    act.wait_ge(rw_step, RW * s + 3)
                    nc.scalar.activation(rw[:, 1, :], rw[:, 0, :], ACT.Exp).then_inc(rw_exp, 1)
                    for n in range(2):
                        act.wait_ge(up_ps, 2 * s + n + 1)
                        nc.scalar.activation(hid[0][:, 2 * n:2 * n + 2, :], halves(2 + n), ACT.Relu
                                             ).then_inc(hid_hi, 1)
                if r:
                    q = s - 2
                    wait(act, route_ps, q)
                    for n in range(2):
                        act.wait_ge(xt3_ps, 2 * q + n + 1)
                        nc.scalar.activation(xt3[:, 2 * n:2 * n + 2, :], halves(4 + n), ACT.Copy
                                             ).then_inc(xt3_ready, 1)
                if a:
                    act.wait_ge(sm_step, 4 * b + 4)
                    wait(act, pt_ps, b)
                    wait(act, scale_step, 2 * b)
                    for u in range(U):
                        nc.scalar.activation(probs[:, u, :], masked[:, u, :], ACT.Exp, bias=neg_max[:, u:u + 1],
                                             accum_out=row_sum[:, u:u + 1]).then_inc(exp_done, 1)
                    act.wait_ge(pt_ps, b + 1)
                    nc.scalar.activation(probs_t[0][:], halves(7), ACT.Copy).then_inc(pt_hi, 1)

            iterations(act, body)
            act.wait_ge(xhat_stored, 16 * B)
            act.wait_ge(x_stored, 16 * B)

        @block.vector
        def _(dve):
            def layer_norm(n, b, dst, ready, free_sem, free_count):
                L = ln[n]
                base = CHAIN * b
                nc.vector.memset(fence[f"ln{n}a"][:], 0.0)
                for u in range(U):
                    nc.vector.bn_stats(L["stats"][:, u, :], x_tile(b, u)).then_inc(L["step"], 1)
                dve.wait_ge(L["step"], base + U)
                wait(dve, ready, U * b)
                nc.vector.memset(fence[f"ln{n}b"][:], 0.0)
                for u in range(U):
                    nc.vector.bn_aggr(L["mv"][:, u, :], L["stats"][:, u, :]).then_inc(L["step"], 1)
                dve.wait_ge(L["step"], base + 2 * U)
                inverse_sqrt(nc, dve, L["rstd"][:], L["mv"][:, :, 1], [L["tmp"][:, m, :] for m in range(3)],
                             L["step"], base + 2 * U)
                dve.wait_ge(L["step"], base + CHAIN)
                wait(dve, free_sem, free_count)
                for u in range(U):
                    nc.vector.tensor_scalar(dst[:, u, :], x_tile(b, u), L["mv"][:, u, 0:1], L["rstd"][:, u:u + 1],
                                            ALU.subtract, ALU.mult).then_inc(ready, 1)

            def lo_part(dst, bank, n, hi, hi_sem, count, lo_sem):
                dve.wait_ge(hi_sem, count)
                nc.vector.tensor_tensor(dst[1][:, 2 * n:2 * n + 2, :], halves(bank), hi[:, 2 * n:2 * n + 2, :],
                                        ALU.subtract).then_inc(lo_sem, 1)

            layer_norm(1, 0, xhat1, xhat1_ready, xt1_ps, 0)

            def body(s, f, a, r, more):
                b = s - 1
                if f:
                    for n in range(2):
                        lo_part(xt1, n, n, xt1[0], xt1_hi, 2 * s + n + 1, xt1_lo)
                if a:
                    for n in range(2):
                        lo_part(xt2, 4 + n, n, xt2[0], xt2_hi, 2 * b + n + 1, xt2_lo)
                    for n in range(2):
                        lo_part(mem_t, 6 + n, n, mem_t[0], memt_hi, 2 * b + n + 1, memt_lo)
                if f:
                    base = RW * s
                    dve.wait_ge(gate_ps, s + 1)
                    nc.vector.tensor_copy(top_in[:], ps[:, 3, 0:U * E].rearrange("p (u e) -> p u e", u=U)
                                          ).then_inc(gate_copied, 1)
                    dve.wait_ge(gate_copied, s + 1)
                    nc.vector.memset(fence["top"][:], 0.0)
                    for u in range(U):
                        nc.vector.max(top[:, u, :], top_in[:, u, :]).then_inc(rw_step, 1)
                    dve.wait_ge(rw_step, base + 2)
                    nc.vector.tensor_tensor(rw[:, 0, :], top[:, :, 1], top[:, :, 0], ALU.subtract).then_inc(rw_step, 1)
                    dve.wait_ge(rw_exp, s + 1)
                    nc.vector.tensor_scalar(rw[:, 2, :], rw[:, 1, :], 1.0, None, ALU.add).then_inc(rw_step, 1)
                    dve.wait_ge(rw_step, base + 4)
                    nc.vector.reciprocal(rw[:, 3, :], rw[:, 2, :]).then_inc(rw_step, 1)
                    dve.wait_ge(rw_step, base + 5)
                    nc.vector.tensor_tensor(rw[:, 4, :], rw[:, 1, :], rw[:, 3, :], ALU.mult).then_inc(rw_step, 1)
                    dve.wait_ge(rw_step, base + 6)
                    nc.vector.tensor_tensor(rw[:, 2, :], rw[:, 3, :], rw[:, 4, :], ALU.add).then_inc(rw_step, 1)
                    dve.wait_ge(rw_step, base + 7)
                    nc.vector.tensor_scalar(rw[:, 5, :], rw[:, 2, :], c["gates"][:, 2:3], None, ALU.mult
                                            ).then_inc(rw_step, 1)
                    for n in range(2):
                        dve.wait_ge(hid_hi, 2 * s + n + 1)
                        nc.vector.scalar_tensor_tensor(
                            out=hid[1][:, 2 * n:2 * n + 2, :], in0=halves(2 + n), scalar=0.0,
                            in1=hid[0][:, 2 * n:2 * n + 2, :], op0=ALU.max, op1=ALU.subtract).then_inc(hid_lo, 1)
                if a:
                    dve.wait_ge(mask_loaded, 16)
                    nc.vector.tensor_copy(mask_f[:].unsqueeze(1), mask_u8[:, bass.ds(b, 1), :]).then_inc(mask_ready, 1)
                    dve.wait_ge(mask_ready, 2 * b + 1)
                    nc.vector.tensor_scalar(mask_add[:], mask_f[:], 1.0, NEG, ALU.subtract, ALU.mult
                                            ).then_inc(mask_ready, 1)
                    dve.wait_ge(mask_ready, 2 * b + 2)
                    dve.wait_ge(scores_ps, b + 1)
                    wait(dve, exp_done, U * b)
                    nc.vector.scalar_tensor_tensor(
                        out=masked[:], in0=halves(6), scalar=SCALE,
                        in1=mask_f[:].unsqueeze(1).broadcast_to([P, U, S]), op0=ALU.mult, op1=ALU.mult
                    ).then_inc(sm_step, 1)
                    dve.wait_ge(sm_step, 4 * b + 1)
                    nc.vector.tensor_tensor(masked[:], masked[:], mask_add[:].unsqueeze(1).broadcast_to([P, U, S]),
                                            ALU.add).then_inc(sm_step, 1)
                    dve.wait_ge(sm_step, 4 * b + 2)
                    nc.vector.tensor_reduce(row_max[:], masked[:], AX, ALU.max).then_inc(sm_step, 1)
                    dve.wait_ge(sm_step, 4 * b + 3)
                    nc.vector.tensor_scalar(neg_max[:], row_max[:], -1.0, None, ALU.mult).then_inc(sm_step, 1)
                    wait(dve, scale_step, 2 * b)
                    nc.vector.tensor_reduce(valid_gate[:, 0:1], mask_f[:], AX, ALU.max).then_inc(valid_ready, 1)
                    dve.wait_ge(valid_ready, 2 * b + 1)
                    nc.vector.tensor_scalar(valid_gate[:, 1:2], valid_gate[:, 0:1], c["gates"][:, 1:2], None,
                                            ALU.mult).then_inc(valid_ready, 1)
                if f and more:
                    layer_norm(1, s + 1, xhat1, xhat1_ready, xt1_ps, 2 * s + 2)

                def first_ffn(u):
                    n = 2 * (U * s + u)
                    dve.wait_ge(down_ps, U * s + u + 1)
                    xt = x_tile(s, u)
                    nc.vector.scalar_tensor_tensor(out=xt, in0=ps[:, 2 * u, :], scalar=c["gates"][:, 2:3], in1=xt,
                                                   op0=ALU.mult, op1=ALU.add).then_inc(x1_step, 1)
                    dve.wait_ge(x1_step, n + 1)
                    dve.wait_ge(rw_step, RW * s + RW)
                    nc.vector.scalar_tensor_tensor(out=xt, in0=ps[:, 2 * u + 1, :], scalar=rw[:, 5, u:u + 1], in1=xt,
                                                   op0=ALU.mult, op1=ALU.add).then_inc(x1_step, 1)

                if f:
                    first_ffn(0)
                if r:
                    q = s - 2
                    dve.wait_ge(route_ps, q + 1)
                    nc.vector.tensor_tensor(
                        logits[:, bass.ds(U * q, U), :], ps[:, 5, 0:U * R].rearrange("p (u e) -> p u e", u=U),
                        w["route_bias"][:].unsqueeze(1).broadcast_to([P, U, R]), ALU.add).then_inc(logits_ready, 1)
                if a:
                    dve.wait_ge(pt_hi, b + 1)
                    nc.vector.tensor_tensor(probs_t[1][:], halves(7), probs_t[0][:], ALU.subtract).then_inc(pt_lo, 1)
                if f:
                    first_ffn(1)
                    dve.wait_ge(x1_step, 2 * U * s + 2 * U)
                    layer_norm(2, s, xhat2, xhat2_ready, xt2_ps, 2 * s)
                if a:
                    dve.wait_ge(exp_done, U * b + U)
                    nc.vector.reciprocal(row_scale[:, 0, :], row_sum[:]).then_inc(scale_step, 1)
                    dve.wait_ge(scale_step, 2 * b + 1)
                    wait(dve, x2_ready, U * b)
                    nc.vector.tensor_scalar(row_scale[:, 1, :], row_scale[:, 0, :], valid_gate[:, 1:2], None,
                                            ALU.mult).then_inc(scale_step, 1)
                    dve.wait_ge(scale_step, 2 * b + 2)
                    for u in range(U):
                        dve.wait_ge(read_ps, U * b + u + 1)
                        xt = x_tile(b, u)
                        nc.vector.scalar_tensor_tensor(out=xt, in0=ps[:, 4 + u, :], scalar=row_scale[:, 1, u:u + 1],
                                                       in1=xt, op0=ALU.mult, op1=ALU.add).then_inc(x2_ready, 1)
                    dve.wait_ge(x2_ready, U * b + U)
                    wait(dve, xhat_stored, 16 * b)
                    layer_norm(3, b, xhat3, xhat3_ready, xt3_ps, 2 * b)

            iterations(dve, body)

        @block.tensor
        def _(pe):
            def transposes(src, bank, done):
                for n in range(2):
                    for k in (2 * n, 2 * n + 1):
                        for u in range(U):
                            mm = nc.tensor.transpose(halves(bank + n)[:, k % 2, P * u:P * u + P],
                                                     src[:, u, P * k:P * k + P], c["ident"][:])
                    mm.then_inc(done, 1)

            def product(dst, lhs, rhs):
                n = len(lhs)
                for k in range(n):
                    for a_, b_ in ((0, 0), (0, 1), (1, 0)):
                        mm = nc.tensor.matmul(dst, lhs[k][a_], rhs[k][b_], start=(k == 0 and a_ == b_),
                                              stop=(k == n - 1 and a_ == 1))
                return mm

            def chunks(pair_, cols):
                return [[x[:, k, cols] for x in pair_] for k in range(K)]

            everything = slice(None)

            def down(s, u):
                tok = slice(P * u, P * u + P)
                product(ps[:, 2 * u, :], chunks(hid, tok), chunks((w["down_hi"], w["down_lo"]), everything))
                product(ps[:, 2 * u + 1, :], chunks(xt1, tok), chunks((w["expert_hi"], w["expert_lo"]), everything)
                        ).then_inc(down_ps, 1)

            def body(s, f, a, r, more):
                b = s - 1
                if f:
                    pe.wait_ge(xhat1_ready, U * s + U)
                    wait(pe, x1_step, 2 * U * s - 2)
                    transposes(xhat1, 0, xt1_ps)
                if a:
                    pe.wait_ge(xhat2_ready, U * b + U)
                    wait(pe, x2_ready, U * b)
                    transposes(xhat2, 4, xt2_ps)
                    pe.wait_ge(mem_loaded, 16 * b + 16)
                    wait(pe, pt_lo, b)
                    wait(pe, sm_step, 4 * b)
                    transposes(mem_raw, 6, memt_ps)
                if f:
                    pe.wait_ge(xt1_lo, 2 * s + 2)
                    wait(pe, x1_step, 2 * U * s)
                    for u in range(U):
                        mm = product(ps[:, 3, E * u:E * u + E], chunks(xt1, slice(P * u, P * u + P)),
                                     chunks((w["gate_hi"], w["gate_lo"]), everything))
                    mm.then_inc(gate_ps, 1)
                    for n in range(2):
                        if n == 1:
                            pe.wait_ge(gate_copied, s + 1)
                        for o in (2 * n, 2 * n + 1):
                            mm = product(halves(2 + n)[:, o % 2, :],
                                         chunks((w["up_hi"], w["up_lo"]), slice(P * o, P * o + P)),
                                         chunks(xt1, everything))
                        mm.then_inc(up_ps, 1)
                if r:
                    q = s - 2
                    pe.wait_ge(xhat3_ready, U * q + U)
                    if a:
                        pe.wait_ge(xt2_lo, 2 * b + 2)
                    else:
                        pe.wait_ge(x2_ready, U * q + U)
                    transposes(xhat3, 4, xt3_ps)
                if a:
                    pe.wait_ge(xt2_lo, 2 * b + 2)
                    pe.wait_ge(memt_lo, 2 * b + 2)
                    for u in range(U):
                        mm = product(halves(6)[:, u, :], chunks(xt2, slice(P * u, P * u + P)),
                                     chunks(mem_t, everything))
                    mm.then_inc(scores_ps, 1)
                if f:
                    pe.wait_ge(hid_lo, 2 * s + 2)
                    down(s, 0)
                if r:
                    q = s - 2
                    pe.wait_ge(xt3_ready, 2 * q + 2)
                    for u in range(U):
                        for k in range(K):
                            mm = nc.tensor.matmul(ps[:, 5, R * u:R * u + R], xt3[:, k, P * u:P * u + P],
                                                  w["route"][:, k, :], start=(k == 0), stop=(k == K - 1))
                    mm.then_inc(route_ps, 1)
                if a:
                    pe.wait_ge(exp_done, U * b + U)
                    for m in range(U):
                        for u in range(U):
                            mm = nc.tensor.transpose(halves(7)[:, m, P * u:P * u + P],
                                                     probs[:, u, P * m:P * m + P], c["ident"][:])
                    mm.then_inc(pt_ps, 1)
                if f:
                    down(s, 1)
                if a:
                    if r:
                        pe.wait_ge(logits_ready, s - 1)
                    pe.wait_ge(pt_lo, b + 1)
                    pe.wait_ge(mem_lo, b + 1)
                    for u in range(U):
                        product(ps[:, 4 + u, :], [[x[:, m, P * u:P * u + P] for x in probs_t] for m in range(U)],
                                [[x[:, m, :] for x in mem] for m in range(U)]).then_inc(read_ps, 1)

            iterations(pe, body)


def route(nc, c, logits, capacity, slot_token, slot_weight):
    T, E = logits.shape[1], logits.shape[2]
    B = capacity // P
    DIGIT = 3
    RADIX = 1 << DIGIT
    ROUNDS = 10
    BF16 = mybir.dt.bfloat16
    COLS = 5
    with ExitStack() as ctx:
        def sb(name, shape, dt=F32):
            return ctx.enter_context(nc.sbuf_tensor(name, shape, dt))

        def psum(name, shape):
            return ctx.enter_context(nc.psum_tensor(name, shape, F32))

        def sem(name):
            return ctx.enter_context(nc.semaphore(name))

        digit_i = sb("digit_i", [P, RADIX], I32)
        digits = sb("digits", [P, ROUNDS, RADIX], I32)
        before = sb("before", [P, P])
        token_i, token = sb("token_i", [P, T], I32), sb("token", [P, T])
        tile_i, row_i = sb("tile_i", [P, T], I32), sb("row_i", [P, T], I32)
        hi_iota_i, hi_iota = sb("hi_iota_i", [P, P], I32), sb("hi_iota", [P, P], BF16)
        lo_iota = sb("lo_iota", [P, B], BF16)
        restart = sb("restart", [P, 2 * E, T])
        beats = sb("beats", [P, T, E, E])
        rank = sb("rank", [P, T, E])
        assigned = sb("assigned", [P, T, E])
        best = sb("best", [P, T])
        shifted, expo = sb("shifted", [P, T, E]), sb("expo", [P, T, E])
        total, inv = sb("total", [P, T]), sb("inv", [P, T])
        prob = sb("prob", [P, T, E])
        unassigned = sb("unassigned", [P, T, E])
        score = sb("score", [P, E, T])
        kth = sb("kth", [P, E])
        cand = sb("cand", [P, E, RADIX])
        at_least = sb("at_least", [P, E, RADIX, T])
        part_count = sb("part_count", [P, E, RADIX])
        kept = sb("kept", [P, E, RADIX])
        flags = sb("flags", [P, 2, E, T])
        running = sb("running", [P, 2, E, T])
        earlier = sb("earlier", [P, 2, E, T])
        wanted = sb("wanted", [P, E])
        ties = sb("ties", [P, E])
        chosen_n = sb("chosen_n", [P, E])
        fits = sb("fits", [P, E, T])
        chosen = sb("chosen", [P, E, T])
        taken = sb("taken", [P, E, T])
        other = sb("other", [P, E, T])
        slot = sb("slot", [P, E, T])
        slot_i, slot_hi_i, slot_lo_i = (sb(n, [P, E, T], I32) for n in ("slot_i", "slot_hi_i", "slot_lo_i"))
        slot_hi, slot_lo = sb("slot_hi", [P, E, T], BF16), sb("slot_lo", [P, E, T], BF16)
        hot_hi = sb("hot_hi", [P, E, T, P], BF16)
        hot_lo = sb("hot_lo", [P, E, T, B], BF16)
        value = sb("value", [P, E, T, COLS], BF16)
        weight = sb("weight", [P, 3, E, T])
        placed = sb("placed", [P, E, T, COLS, B], BF16)
        w_sum = sb("w_sum", [P, E, B])
        slot_parts = sb("slot_parts", [P, E, COLS, B])
        ps_count = psum("ps_count", [P, 512])
        ps_before = psum("ps_before", [P, 512])
        ps_slot = psum("ps_slot", [P, E, 512])
        tables = sem("tables")
        cs = sem("cs")
        logits_shifted, exped = sem("logits_shifted"), sem("exped")
        counted, count_ps = sem("counted"), sem("count_ps")
        flags_ready, prefix_ps = sem("flags_ready"), sem("prefix_ps")
        placed_ready, slot_ps = sem("placed_ready"), sem("slot_ps")
        block = ctx.enter_context(nc.Block())

        @block.gpsimd
        def _(pool):
            nc.gpsimd.iota(digit_i[:], pattern=[[1, RADIX]], base=0, channel_multiplier=0).then_inc(tables, 1)
            nc.gpsimd.iota(token_i[:], pattern=[[P, T]], base=0, channel_multiplier=1).then_inc(tables, 1)
            nc.gpsimd.iota(tile_i[:], pattern=[[1, T]], base=0, channel_multiplier=0).then_inc(tables, 1)
            nc.gpsimd.iota(row_i[:], pattern=[[0, T]], base=0, channel_multiplier=1).then_inc(tables, 1)
            nc.gpsimd.iota(hi_iota_i[:], pattern=[[1, P]], base=0, channel_multiplier=0).then_inc(tables, 1)
            nc.gpsimd.memset(restart[:], 1.0).then_inc(tables, 1)
            pool.wait_ge(tables, 6)
            nc.gpsimd.memset(restart[:, :, 0:1], 0.0).then_inc(tables, 1)
            nc.gpsimd.affine_select(out=before[:], in_=c["ones"][:], compare_op=ALU.is_gt, fill=0.0, base=0,
                                    pattern=[[1, P]], channel_multiplier=-1).then_inc(tables, 1)

        @block.scalar
        def _(act):
            act.wait_ge(logits_shifted, 1)
            nc.scalar.activation(expo[:], shifted[:], ACT.Exp).then_inc(exped, 1)

        @block.tensor
        def _(pe):
            with pe.Fori(0, ROUNDS) as r:
                pe.wait_ge(counted, r + 1)
                nc.tensor.matmul(ps_count[:, 0:E * RADIX], c["ones"][:], part_count[:].rearrange("p e j -> p (e j)"),
                                 start=True, stop=True).then_inc(count_ps, 1)
            pe.wait_ge(tables, 8)
            pe.wait_ge(flags_ready, 2)
            f = flags[:].rearrange("p f e t -> p (f e t)")
            nc.tensor.matmul(ps_before[:, 0:2 * E * T], before[:], f, start=True, stop=True)
            nc.tensor.matmul(ps_count[:, 0:2 * E * T], c["ones"][:], f, start=True, stop=True).then_inc(prefix_ps, 1)
            for e in range(E):
                pe.wait_ge(placed_ready, e + 1)
                for t_ in range(T):
                    mm = nc.tensor.matmul(ps_slot[:, e, 0:COLS * B], hot_hi[:, e, t_, :],
                                          placed[:, e, t_].rearrange("p c b -> p (c b)"),
                                          start=(t_ == 0), stop=(t_ == T - 1))
                mm.then_inc(slot_ps, 1)

        @block.vector
        def _(dve):
            steps = [0]

            def link(ins):
                steps[0] += 1
                ins.then_inc(cs, 1)
                dve.wait_ge(cs, steps[0])

            V = nc.vector

            def per_expert(ap):
                return ap.unsqueeze(2).broadcast_to([P, E, T])

            dve.wait_ge(tables, 8)
            for r in range(ROUNDS):
                link(V.tensor_scalar(digits[:, r, :], digit_i[:], DIGIT * (ROUNDS - 1 - r), None,
                                     ALU.logical_shift_left))
            link(V.tensor_copy(token[:], token_i[:]))
            link(V.tensor_copy(hi_iota[:], hi_iota_i[:]))
            link(V.tensor_copy(lo_iota[:], digit_i[:, 0:B]))
            for e in range(E):
                link(V.tensor_copy(value[:, e, :, 0], tile_i[:]))
                link(V.tensor_copy(value[:, e, :, 1], row_i[:]))

            link(V.memset(beats[:], 0.0))
            for e in range(E):
                for js, op in ((slice(0, e), ALU.is_ge), (slice(e + 1, E), ALU.is_gt)):
                    n = js.stop - js.start
                    if n:
                        link(V.tensor_tensor(beats[:, :, e, js], logits[:, :, js],
                                             logits[:, :, e:e + 1].broadcast_to([P, T, n]), op))
            link(V.tensor_reduce(rank[:], beats[:], AX, ALU.add))
            link(V.tensor_scalar(assigned[:], rank[:], 2.0, None, ALU.is_lt))
            link(V.tensor_reduce(best[:], logits[:], AX, ALU.max))
            V.tensor_tensor(shifted[:], logits[:], best[:].unsqueeze(2).broadcast_to([P, T, E]),
                            ALU.subtract).then_inc(logits_shifted, 1)
            dve.wait_ge(exped, 1)
            link(V.tensor_tensor(expo[:], expo[:], assigned[:], ALU.mult))
            link(V.tensor_reduce(total[:], expo[:], AX, ALU.add))
            link(V.reciprocal(inv[:], total[:]))
            link(V.tensor_tensor(prob[:], expo[:], inv[:].unsqueeze(2).broadcast_to([P, T, E]), ALU.mult))
            link(V.tensor_scalar(unassigned[:], assigned[:], 1.0, None, ALU.subtract))
            link(V.tensor_tensor(score[:].rearrange("p e t -> p t e"), prob[:], unassigned[:], ALU.add))
            link(V.memset(kth[:], 0.0))

            base = steps[0]
            with dve.Fori(0, ROUNDS) as r:
                V.tensor_tensor(cand[:].bitcast(I32), kth[:].bitcast(I32).unsqueeze(2).broadcast_to([P, E, RADIX]),
                                digits[:, bass.ds(r, 1), :].broadcast_to([P, E, RADIX]),
                                ALU.bitwise_or).then_inc(cs, 1)
                dve.wait_ge(cs, 4 * r + base + 1)
                V.tensor_tensor(at_least[:], score[:].unsqueeze(2).broadcast_to([P, E, RADIX, T]),
                                cand[:].unsqueeze(3).broadcast_to([P, E, RADIX, T]), ALU.is_ge).then_inc(cs, 1)
                dve.wait_ge(cs, 4 * r + base + 2)
                V.tensor_reduce(part_count[:], at_least[:], AX, ALU.add).then_inc(counted, 1)
                dve.wait_ge(count_ps, r + 1)
                V.scalar_tensor_tensor(out=kept[:], in0=ps_count[:, 0:E * RADIX].rearrange("p (e j) -> p e j", e=E),
                                       scalar=float(capacity), in1=cand[:], op0=ALU.is_ge,
                                       op1=ALU.mult).then_inc(cs, 1)
                dve.wait_ge(cs, 4 * r + base + 3)
                V.tensor_reduce(kth[:], kept[:], AX, ALU.max).then_inc(cs, 1)
                dve.wait_ge(cs, 4 * r + base + 4)
            steps[0] += 4 * ROUNDS

            for n, op in enumerate((ALU.is_gt, ALU.is_equal)):
                V.tensor_tensor(flags[:, n], score[:], per_expert(kth[:]), op).then_inc(flags_ready, 1)
            dve.wait_ge(prefix_ps, 1)
            flat = lambda ap: ap[:].rearrange("p f e t -> p (f e t)")
            link(V.tensor_tensor_scan(flat(running), restart[:].rearrange("p f t -> p (f t)"),
                                      ps_count[:, 0:2 * E * T], 0.0, ALU.mult, ALU.add))
            link(V.tensor_tensor(flat(earlier), flat(running), ps_count[:, 0:2 * E * T], ALU.subtract))
            link(V.tensor_tensor(flat(earlier), flat(earlier), ps_before[:, 0:2 * E * T], ALU.add))
            link(V.tensor_scalar(wanted[:], running[:, 0, :, T - 1], -1.0, float(capacity), ALU.mult, ALU.add))
            link(V.tensor_tensor(ties[:], wanted[:], running[:, 1, :, T - 1], ALU.min))
            link(V.tensor_tensor(chosen_n[:], ties[:], running[:, 0, :, T - 1], ALU.add))
            link(V.tensor_tensor(fits[:], earlier[:, 1], per_expert(wanted[:]), ALU.is_lt))
            link(V.tensor_tensor(fits[:], fits[:], flags[:, 1], ALU.mult))
            link(V.tensor_tensor(chosen[:], flags[:, 0], fits[:], ALU.add))
            link(V.tensor_tensor(taken[:], earlier[:, 1], per_expert(wanted[:]), ALU.min))
            link(V.tensor_tensor(taken[:], taken[:], earlier[:, 0], ALU.add))
            link(V.tensor_tensor(other[:], token[:].unsqueeze(1).broadcast_to([P, E, T]), taken[:], ALU.subtract))
            link(V.tensor_tensor(other[:], other[:], per_expert(chosen_n[:]), ALU.add))
            link(V.tensor_tensor(slot[:], taken[:], other[:], ALU.subtract))
            link(V.tensor_tensor(slot[:], slot[:], chosen[:], ALU.mult))
            link(V.tensor_tensor(slot_i[:], slot[:], other[:], ALU.add))
            link(V.tensor_scalar(slot_hi_i[:], slot_i[:], DIGIT, None, ALU.logical_shift_right))
            link(V.tensor_scalar(slot_lo_i[:], slot_i[:], RADIX - 1, None, ALU.bitwise_and))
            link(V.tensor_copy(slot_hi[:], slot_hi_i[:]))
            link(V.tensor_copy(slot_lo[:], slot_lo_i[:]))
            link(V.tensor_tensor(weight[:, 0], chosen[:], prob[:].rearrange("p t e -> p e t"), ALU.mult))
            for n in range(3):
                link(V.tensor_copy(value[:, :, :, 2 + n], weight[:, n]))
                if n < 2:
                    link(V.tensor_tensor(weight[:, n + 1], weight[:, n], value[:, :, :, 2 + n], ALU.subtract))
            link(V.tensor_tensor(hot_lo[:], slot_lo[:].unsqueeze(3).broadcast_to([P, E, T, B]),
                                 lo_iota[:].unsqueeze(1).unsqueeze(1).broadcast_to([P, E, T, B]), ALU.is_equal))
            for e in range(E):
                link(V.tensor_tensor(placed[:, e], hot_lo[:, e].unsqueeze(2).broadcast_to([P, T, COLS, B]),
                                     value[:, e].unsqueeze(3).broadcast_to([P, T, COLS, B]), ALU.mult))
                V.tensor_tensor(hot_hi[:, e], slot_hi[:, e].unsqueeze(2).broadcast_to([P, T, P]),
                                hi_iota[:].unsqueeze(1).broadcast_to([P, T, P]), ALU.is_equal).then_inc(placed_ready, 1)
            for e in range(E):
                dve.wait_ge(slot_ps, e + 1)
                link(V.tensor_copy(slot_parts[:, e].rearrange("p c b -> p (c b)"), ps_slot[:, e, 0:COLS * B]))
            link(V.scalar_tensor_tensor(out=slot_token[:], in0=slot_parts[:, :, 0, :], scalar=float(P),
                                        in1=slot_parts[:, :, 1, :], op0=ALU.mult, op1=ALU.add))
            link(V.tensor_tensor(w_sum[:], slot_parts[:, :, 2, :], slot_parts[:, :, 3, :], ALU.add))
            link(V.tensor_tensor(w_sum[:], w_sum[:], slot_parts[:, :, 4, :], ALU.add))
            link(V.tensor_scalar(slot_weight[:], w_sum[:], c["gates"][:, 3:4], None, ALU.mult))


def experts(nc, c, w1, w2, slot_token, slot_weight, xhat_d, out):
    E, D, H = w1.shape
    K = D // P
    HT = H // P
    SLOTS = slot_token.shape[2]
    I = SLOTS // 2
    GROUP = 4
    RING = 4
    AHEAD = 2
    rows_out = row_major(out)
    w1_t = w1.rearrange("e (k p) h -> e p k h", p=P)
    w2_t = w2.rearrange("e (t p) d -> e p t d", p=P)
    with ExitStack() as ctx:
        def sb(name, shape, dt=F32):
            return ctx.enter_context(nc.sbuf_tensor(name, shape, dt))

        def sem(name):
            return ctx.enter_context(nc.semaphore(name))

        w1_raw = sb("w1_raw", [P, 2, K, GROUP * P])
        w2_raw = sb("w2_raw", [P, 2, GROUP, D])
        w1_s = [sb("w1_hi", [P, RING, K, P], F32R), sb("w1_lo", [P, RING, K, P], F32R)]
        w2_s = [sb("w2_hi", [P, RING, D], F32R), sb("w2_lo", [P, RING, D], F32R)]
        rows = sb("rows", [P, I, D])
        rows_t = [sb("rows_t_hi", [P, 2, K, D], F32R), sb("rows_t_lo", [P, 2, K, D], F32R)]
        hidden = sb("hidden", [P, 2, D])
        hid = [sb("hidden_hi", [P, 2, D], F32R), sb("hidden_lo", [P, 2, D], F32R)]
        scaled = sb("scaled", [P, I, D])
        gather_index = sb("gather_index", [P, I], U32)
        scatter_index = sb("scatter_index", [P, I], U32)
        factor = sb("factor", [P, I])
        ps_y = ctx.enter_context(nc.psum_tensor("ps_y", [P, I, 512], F32))
        ps_h = ctx.enter_context(nc.psum_tensor("ps_h", [P, 2, 512], F32))
        ps_t = ctx.enter_context(nc.psum_tensor("ps_t", [P, 2, I, P], F32))

        w_loaded = [sem(f"w_loaded{n}") for n in range(2)]
        w_hi, w_lo = sem("w_hi"), sem("w_lo")
        index_ready = sem("index_ready")
        factor_ready = sem("factor_ready")
        gathered = [sem(f"gathered{i}") for i in range(I)]
        rows_ps = sem("rows_ps")
        rows_hi, rows_lo = sem("rows_hi"), sem("rows_lo")
        h_ps, gelu_done = sem("h_ps"), sem("gelu_done")
        h_hi, h_lo = sem("h_hi"), sem("h_lo")
        y_done = sem("y_done")
        y_out = sem("y_out")
        scattered = sem("scattered")
        block = ctx.enter_context(nc.Block())
        STEPS = 2 * HT

        def all_experts(eng, body):
            body(0, True)
            with eng.Fori(1, E - 1) as e:
                body(e, True)
            body(E - 1, False)

        def first(e, half):
            return isinstance(e, int) and e == 0 and half == 0

        @block.sync
        def _(sp):
            def body(e, more):
                for half in range(2):
                    for q in range(HT // GROUP):
                        n, par = 8 * e + 4 * half + q, q % 2
                        wait(sp, w_lo, 2 * GROUP * (n - 1))
                        cols = slice(GROUP * P * q, GROUP * P * (q + 1))
                        sp.dma_start(w1_raw[:, par], w1_t[bass.ds(e, 1), :, :, cols].rearrange("o p k h -> (o p) k h")
                                     ).then_inc(w_loaded[par], 16)
                        sp.dma_start(w2_raw[:, par], w2_t[bass.ds(e, 1), :, GROUP * q:GROUP * q + GROUP, :]
                                     .rearrange("o p t d -> (o p) t d")).then_inc(w_loaded[par], 16)

            all_experts(sp, body)

        def gather_wait(e, half):
            n = 2 * e + half
            nc.gpsimd.wait_ge(index_ready, n + 1)
            wait(nc.gpsimd, rows_ps, K * n)

        def gather():
            for i in range(I):
                nc.gpsimd.indirect_dma_start(
                    out=rows[:, i, :], out_offset=None, in_=xhat_d,
                    in_offset=bass.IndirectOffsetOnAxis(ap=gather_index[:, i:i + 1], axis=0)
                ).then_inc(gathered[i], 16)

        @block.gpsimd
        def _(pool):
            def split(e, half, t):
                g, par, r = STEPS * e + HT * half + t, (t // GROUP) % 2, t % RING
                j = t % GROUP
                pool.wait_ge(w_hi, 2 * g + 1)
                nc.gpsimd.tensor_tensor(w1_s[1][:, r], w1_raw[:, par, :, P * j:P * j + P], w1_s[0][:, r],
                                        ALU.subtract).then_inc(w_lo, 1)
                pool.wait_ge(w_hi, 2 * g + 2)
                nc.gpsimd.tensor_tensor(w2_s[1][:, r], w2_raw[:, par, j, :], w2_s[0][:, r],
                                        ALU.subtract).then_inc(w_lo, 1)

            def scatter_wait(e, half, i):
                n = I * (2 * e + half) + i
                pool.wait_ge(y_out, n + 1)
                wait(pool, scattered, 16 * n)

            def scatter(i):
                nc.gpsimd.indirect_dma_start(
                    out=rows_out, out_offset=bass.IndirectOffsetOnAxis(
                        ap=scatter_index[:, i:i + 1], axis=0),
                    in_=scaled[:, i, :], in_offset=None, compute_op=ALU.add).then_inc(scattered, 16)

            gather_wait(0, 0)
            gather()
            for t in range(AHEAD):
                split(0, 0, t)

            def body(e, more):
                for half in range(2):
                    for t in range(HT):
                        i = (t - 3) // 2 if t in range(3, 3 + 2 * I, 2) and not first(e, half) else None
                        gathers = t == 1 and (half == 0 or more)
                        if i is not None:
                            scatter_wait(e if half else e - 1, 1 - half, i)
                        if gathers:
                            gather_wait(e + half, 1 - half)
                        if t + AHEAD < HT:
                            split(e, half, t + AHEAD)
                        elif half == 0:
                            split(e, 1, t + AHEAD - HT)
                        elif more:
                            split(e + 1, 0, t + AHEAD - HT)
                        if i is not None:
                            scatter(i)
                        if gathers:
                            gather()

            all_experts(pool, body)
            for i in range(I):
                scatter_wait(E - 1, 1, i)
                scatter(i)
            pool.wait_ge(scattered, 16 * 2 * E * I)

        @block.scalar
        def _(act):
            def split(e, half, t):
                g, par, r = STEPS * e + HT * half + t, (t // GROUP) % 2, t % RING
                j = t % GROUP
                act.wait_ge(w_loaded[par], 32 * (4 * e + 2 * half + t // (2 * GROUP) + 1))
                wait(act, y_done, I * (g - RING + 1))
                nc.scalar.activation(w1_s[0][:, r], w1_raw[:, par, :, P * j:P * j + P], ACT.Copy).then_inc(w_hi, 1)
                nc.scalar.activation(w2_s[0][:, r], w2_raw[:, par, j, :], ACT.Copy).then_inc(w_hi, 1)

            def rows_part(e, half, k):
                n = K * (2 * e + half) + k
                act.wait_ge(rows_ps, n + 1)
                nc.scalar.activation(rows_t[0][:, half, k, :], ps_t[:, k % 2].rearrange("p i s -> p (i s)"),
                                     ACT.Copy).then_inc(rows_hi, 1)

            def gelu(e, half, t):
                g = STEPS * e + HT * half + t
                act.wait_ge(h_ps, g + 1)
                wait(act, h_lo, g - 1)
                nc.scalar.activation(hidden[:, t % 2, :], ps_h[:, t % 2, :], ACT.Gelu).then_inc(gelu_done, 1)

            for t in range(AHEAD):
                split(0, 0, t)
            for k in range(K):
                rows_part(0, 0, k)

            def body(e, more):
                for half in range(2):
                    for t in range(HT):
                        gelu(e, half, t)
                        if t + AHEAD < HT:
                            split(e, half, t + AHEAD)
                        elif half == 0:
                            split(e, 1, t + AHEAD - HT)
                        elif more:
                            split(e + 1, 0, t + AHEAD - HT)
                        if 8 <= t < 8 + K:
                            if half == 0:
                                rows_part(e, 1, t - 8)
                            elif more:
                                rows_part(e + 1, 0, t - 8)

            all_experts(act, body)

        @block.vector
        def _(dve):
            def rows_part(e, half, k):
                n = K * (2 * e + half) + k
                dve.wait_ge(rows_hi, n + 1)
                nc.vector.tensor_tensor(rows_t[1][:, half, k, :], ps_t[:, k % 2].rearrange("p i s -> p (i s)"),
                                        rows_t[0][:, half, k, :], ALU.subtract).then_inc(rows_lo, 1)

            def outputs(e, half):
                blk = 2 * e + half
                wait(dve, scattered, 16 * I * blk)
                cols = slice(I * half, I * half + I)
                nc.vector.tensor_copy(scatter_index[:].unsqueeze(1), slot_token[:, bass.ds(e, 1), cols]
                                      ).then_inc(factor_ready, 1)
                nc.vector.tensor_copy(factor[:].unsqueeze(1), slot_weight[:, bass.ds(e, 1), cols]
                                      ).then_inc(factor_ready, 1)
                dve.wait_ge(factor_ready, 2 * blk + 2)
                for i in range(I):
                    dve.wait_ge(y_done, I * (HT * (blk + 1) - 1) + i + 1)
                    nc.vector.tensor_scalar(scaled[:, i, :], ps_y[:, i, :], factor[:, i:i + 1], None,
                                            ALU.mult).then_inc(y_out, 1)

            def hidden_parts(e, half, t):
                g = STEPS * e + HT * half + t
                dve.wait_ge(gelu_done, g + 1)
                wait(dve, y_done, I * (g - 1))
                nc.vector.tensor_copy(hid[0][:, t % 2, :], hidden[:, t % 2, :]).then_inc(h_hi, 1)
                dve.wait_ge(h_hi, g + 1)
                nc.vector.tensor_tensor(hid[1][:, t % 2, :], hidden[:, t % 2, :], hid[0][:, t % 2, :],
                                        ALU.subtract).then_inc(h_lo, 1)

            def pick(e, half):
                n = 2 * e + half
                wait(dve, rows_ps, K * n)
                nc.vector.tensor_copy(gather_index[:].unsqueeze(1),
                                      slot_token[:, bass.ds(e, 1), I * half:I * half + I]).then_inc(index_ready, 1)

            pick(0, 0)
            for k in range(K):
                rows_part(0, 0, k)

            def body(e, more):
                for half in range(2):
                    if half == 1:
                        outputs(e, 0)
                    elif not first(e, half):
                        outputs(e - 1, 1)
                    for t in range(HT):
                        if t == 0:
                            if half == 0:
                                pick(e, 1)
                            elif more:
                                pick(e + 1, 0)
                        hidden_parts(e, half, t)
                        if 8 <= t < 8 + K:
                            if half == 0:
                                rows_part(e, 1, t - 8)
                            elif more:
                                rows_part(e + 1, 0, t - 8)

            all_experts(dve, body)
            outputs(E - 1, 1)

        @block.tensor
        def _(pe):
            def transposes(e, half, k):
                n = K * (2 * e + half) + k
                if k == 0:
                    for i in range(I):
                        pe.wait_ge(gathered[i], 16 * (2 * e + half + 1))
                wait(pe, rows_lo, n - 1)
                for i in range(I):
                    mm = nc.tensor.transpose(ps_t[:, k % 2, i, :], rows[:, i, P * k:P * k + P], c["ident"][:])
                mm.then_inc(rows_ps, 1)

            def hidden_product(e, half, t):
                g, r = STEPS * e + HT * half + t, t % RING
                if t == 0:
                    pe.wait_ge(rows_lo, K * (2 * e + half) + K)
                pe.wait_ge(w_lo, 2 * g + 2)
                wait(pe, gelu_done, g - 1)
                for k in range(K):
                    for a, b in ((0, 0), (0, 1), (1, 0)):
                        mm = nc.tensor.matmul(ps_h[:, t % 2, :], w1_s[a][:, r, k, :], rows_t[b][:, half, k, :],
                                              start=(k == 0 and a == b), stop=(k == K - 1 and a == 1))
                mm.then_inc(h_ps, 1)

            def output_product(e, half, t):
                g, r = STEPS * e + HT * half + t, t % RING
                pe.wait_ge(h_lo, g + 1)
                for i in range(I):
                    n = I * (2 * e + half) + i
                    if t == 0:
                        wait(pe, y_out, n - I + 1)
                    tok = slice(P * i, P * i + P)
                    for a, b in ((0, 0), (0, 1), (1, 0)):
                        mm = nc.tensor.matmul(ps_y[:, i, :], hid[a][:, t % 2, tok], w2_s[b][:, r],
                                              start=(t == 0 and a == b), stop=(t == HT - 1 and a == 1))
                    mm.then_inc(y_done, 1)

            for k in range(K):
                transposes(0, 0, k)

            def body(e, more):
                for half in range(2):
                    for t in range(HT):
                        hidden_product(e, half, t)
                        if t > 0:
                            output_product(e, half, t - 1)
                        if 8 <= t < 8 + K:
                            if half == 0:
                                transposes(e, 1, t - 8)
                            elif more:
                                transposes(e + 1, 0, t - 8)
                    output_product(e, half, HT - 1)

            all_experts(pe, body)


def program(nc, t, out):
    with ExitStack() as ctx:
        def sb(name, shape, dt=F32):
            return ctx.enter_context(nc.sbuf_tensor(name, shape, dt))

        B, S, D = t["x"].shape
        TOK, K = B * S, D // P
        E = t["L1_ffn_W1"].shape[0]
        CAPACITY = TOK // E
        logits = sb("logits", [P, TOK // P, E])
        slot_token = sb("slot_token", [P, E, CAPACITY // P], U32)
        slot_weight = sb("slot_weight", [P, E, CAPACITY // P])
        xhat_d = nc.dram_tensor("xhat_d", (TOK, D), F32).ap()
        c = build_constants(nc, ctx, t["g_xattn"], t["g_ffn"])
        with ExitStack() as xctx:
            x_res = xctx.enter_context(nc.sbuf_tensor("x_res", [P, TOK // P, D], F32))
            column_attention(nc, c, t["x"], t["ctx_2048"], xhat_d, x_res)
            w = {n + part: xctx.enter_context(nc.sbuf_tensor("w_" + n + part, [P, K, cols], F32R))
                 for n, cols in (("up", D), ("down", D), ("expert", D), ("gate", 8)) for part in ("_hi", "_lo")}
            w["route"] = xctx.enter_context(nc.sbuf_tensor("w_route", [P, K, E], F32))
            w["route_bias"] = xctx.enter_context(nc.sbuf_tensor("w_route_bias", [P, E], F32))
            split_weights(nc, c, t, w)
            dense_and_memory(nc, c, w, t, x_res, xhat_d, out, logits)
        route(nc, c, logits, CAPACITY, slot_token, slot_weight)
        experts(nc, c, t["L1_ffn_W1"], t["L1_ffn_W2"], slot_token, slot_weight, xhat_d, out)


_INS = ["x", "ctx_2048", "mask_BxS2_bk0", "g_xattn", "g_ffn", "L0_ffn_W_up", "L0_ffn_W_down", "L0_ffn_W_gate",
        "L0_ffn_W_expert", "L1_ffn_Wg", "L1_ffn_bg", "L1_ffn_W1", "L1_ffn_W2"]


def kernel(**inputs):
    import numpy as _np
    import concourse.bacc as _bacc
    from concourse import mybir as _mybir
    from concourse.bass_utils import run_bass_kernel_spmd as _run

    nc = _bacc.Bacc("TRN2", target_bir_lowering=False, num_devices=1)
    arrays, tensors = {}, {}
    for name in _INS:
        a = _np.ascontiguousarray(inputs[name])
        arrays[f"in_{name}"] = a
        tensors[name] = nc.dram_tensor(f"in_{name}", a.shape, _mybir.dt.from_np(a.dtype), kind="ExternalInput").ap()
    out = nc.dram_tensor("out_x", (16, 256, 512), _mybir.dt.float32, kind="ExternalOutput").ap()
    program(nc, tensors, out)
    r = _run(nc, [arrays], core_ids=[0])
    return r.results[0]["out_x"]
```

```python
from contextlib import ExitStack

import numpy as np

import concourse.bass as bass
from concourse import mybir

P = 128
F32 = mybir.dt.float32
F32R = mybir.dt.float32r
I32 = mybir.dt.int32
U32 = mybir.dt.uint32
U8 = mybir.dt.uint8
ALU = mybir.AluOpType
ACT = mybir.ActivationFunctionType
AX = mybir.AxisListType.X
EPS = 1e-5


def wait(eng, sem, value):
    if isinstance(value, int) and value <= 0:
        return
    eng.wait_ge(sem, value)


RSQRT_STEPS = 12


def inverse_sqrt(nc, dve, y, var, tmp, step, base):
    rsqrt_guess(nc, dve, y, var, tmp, step, base)
    for n in range(3):
        rsqrt_newton(nc, dve, y, tmp, step, base, n)


def rsqrt_guess(nc, dve, y, var, tmp, step, base):
    nc.vector.tensor_scalar(tmp[0], var, EPS, None, ALU.add).then_inc(step, 1)
    dve.wait_ge(step, base + 1)
    nc.vector.tensor_scalar(tmp[1].bitcast(I32), tmp[0].bitcast(I32), 1, None,
                            ALU.logical_shift_right).then_inc(step, 1)
    dve.wait_ge(step, base + 2)
    nc.vector.tensor_scalar(y.bitcast(I32), tmp[1].bitcast(I32), -1.0, float(0x5F3759DF),
                            ALU.mult, ALU.add).then_inc(step, 1)


def rsqrt_newton(nc, dve, y, tmp, step, base, n):
    done = base + 3 + 3 * n
    dve.wait_ge(step, done)
    nc.vector.tensor_tensor(tmp[1], y, y, ALU.mult).then_inc(step, 1)
    dve.wait_ge(step, done + 1)
    nc.vector.scalar_tensor_tensor(out=tmp[2], in0=tmp[1], scalar=-0.5, in1=tmp[0],
                                   op0=ALU.mult, op1=ALU.mult).then_inc(step, 1)
    dve.wait_ge(step, done + 2)
    nc.vector.scalar_tensor_tensor(out=y, in0=tmp[2], scalar=1.5, in1=y,
                                   op0=ALU.add, op1=ALU.mult).then_inc(step, 1)


def row_major(t):
    return t.rearrange("b s d -> (b s) d")


def build_constants(nc, ctx, g_xattn, g_ffn):
    def sb(name, shape, dt):
        return ctx.enter_context(nc.sbuf_tensor(name, shape, dt))

    c = {
        "ident": sb("ident", [P, P], F32),
        "neg_ident": sb("neg_ident", [P, P], F32),
        "ones": sb("ones", [P, P], F32),
        "ones_r": sb("ones_r", [P, P], F32R),
        "gates": sb("gates", [P, 4], F32),
        "gates_raw": sb("gates_raw", [P, 4], F32),
    }
    with nc.semaphore("gates_loaded") as gates_loaded, nc.semaphore("cleared") as cleared, \
            nc.semaphore("const_step") as const_step, nc.Block() as block:
        @block.sync
        def _(sp):
            for n, g in enumerate((g_xattn, g_ffn)):
                sp.dma_start(c["gates_raw"][:, 2 * n:2 * n + 2],
                             bass.AP(tensor=g.tensor, offset=0, ap=[[0, P], [1, 2]])).then_inc(gates_loaded, 16)
            sp.wait_ge(gates_loaded, 32)

        @block.scalar
        def _(act):
            act.wait_ge(gates_loaded, 32)
            nc.scalar.activation(c["gates"][:], c["gates_raw"][:], ACT.Tanh).then_inc(const_step, 1)
            act.wait_ge(const_step, 1)

        @block.gpsimd
        def _(pool):
            nc.gpsimd.memset(c["ident"][:], 0.0).then_inc(cleared, 1)
            nc.gpsimd.memset(c["ones"][:], 1.0).then_inc(cleared, 1)
            nc.gpsimd.memset(c["neg_ident"][:], 0.0).then_inc(cleared, 1)
            pool.wait_ge(cleared, 3)
            for name, v in (("ident", 1.0), ("neg_ident", -1.0)):
                nc.gpsimd.affine_select(out=c[name][:], in_=c[name][:], compare_op=ALU.not_equal, fill=v,
                                        base=0, pattern=[[-1, P]], channel_multiplier=1).then_inc(cleared, 1)
            nc.gpsimd.tensor_copy(c["ones_r"][:], c["ones"][:]).then_inc(cleared, 1)
            pool.wait_ge(cleared, 6)
    return c


def column_attention(nc, c, x_in, ctx_in, xhat_d, x_res):
    D = x_in.shape[2]
    TOK = x_in.shape[0] * x_in.shape[1]
    TILES = TOK // P
    BATCHES = TILES // 2
    HEADS = 4
    ROWS = P // HEADS
    STACK = 3 * ROWS
    NT = D // P
    SCALE = float(np.float32(1.0) / np.sqrt(np.float32(ROWS)))
    NORM_STEPS = 4 + RSQRT_STEPS
    ORDER = (0, 2, 1, 3)
    x_t = row_major(x_in).rearrange("(t p) d -> p t d", p=P)
    ctx_t = row_major(ctx_in).rearrange("(t p) d -> t p d", p=P)
    ctx_h = row_major(ctx_in).rearrange("(t h r) d -> t r h d", h=HEADS, r=ROWS)
    xhat_t = xhat_d.rearrange("(t p) d -> t p d", p=P)
    xhat_h = xhat_d.rearrange("(t h r) d -> t r h d", h=HEADS, r=ROWS)
    NEG_IDENT4 = c["neg_ident"][:].unsqueeze(1).broadcast_to([P, NT, P])

    with ExitStack() as ctx:
        def sb(name, shape, dt=F32):
            return ctx.enter_context(nc.sbuf_tensor(name, shape, dt))

        def sem(name):
            return ctx.enter_context(nc.semaphore(name))

        ctx_nat = sb("ctx_nat", [P, 2, D])
        k_raw = sb("k_raw", [STACK, 2, HEADS, D])
        q_raw = sb("q_raw", [STACK, 2, HEADS, D])
        k_stack = sb("k_stack", [STACK, 2, HEADS, D], F32R)
        q_stack = sb("q_stack", [STACK, 2, HEADS, D], F32R)
        v_ones = sb("v_ones", [P, 2, NT, HEADS, 2 * ROWS])
        probs = sb("probs", [P, 2, NT, D])
        maxima = sb("maxima", [P, 2, NT])
        neg_max_diag = sb("neg_max_diag", [P, 2, NT, P], F32R)
        xhat = sb("xhat", [P, 2, D])
        stats = sb("stats", [P, 2, 6])
        mean_var = sb("mean_var", [P, 2, 2])
        rstd = sb("rstd", [P, 2])
        fence = sb("fence", [P, 1])
        tmp3 = sb("tmp3", [P, 3, 2])
        outputs = sb("outputs", [P, 2, D])
        denominators = sb("denominators", [P, 2, D])
        recip = sb("recip", [P, D])
        gated = sb("gated", [P, 2, D])
        ps_s = [ctx.enter_context(nc.psum_tensor(f"ps_s{n}", [P, D], F32)) for n in range(NT)]
        ps_st = [ctx.enter_context(nc.psum_tensor(f"ps_st{n}", [P, D], F32)) for n in range(2)]
        ps_od = [ctx.enter_context(nc.psum_tensor(f"ps_od{n}", [P, D], F32)) for n in range(2)]
        ps_v = ps_s[NT - 1][:, :].rearrange("p (n r) -> p n r", n=NT)

        x_loaded = sem("x_loaded")
        ctx_loaded = [sem(f"ctx_loaded{u}") for u in range(2)]
        k_loaded = [sem(f"k_loaded{u}") for u in range(2)]
        q_loaded = [sem(f"q_loaded{u}") for u in range(2)]
        xhat_stored = sem("xhat_stored")
        ln_step = sem("ln_step")
        xhat_ready = sem("xhat_ready")
        hi_ready = sem("hi_ready")
        lo_ready = sem("lo_ready")
        ones_ready = sem("ones_ready")
        v_transposed = sem("v_transposed")
        v_ready = sem("v_ready")
        s_done = sem("s_done")
        reduced = sem("reduced")
        diag_ready = sem("diag_ready")
        st_done = sem("st_done")
        exp_done = sem("exp_done")
        pv_done = sem("pv_done")
        evacuated = sem("evacuated")
        recip_done = sem("recip_done")
        gated_done = sem("gated_done")
        x_added = sem("x_added")

        block = ctx.enter_context(nc.Block())

        def batches(eng, body):
            body(0)
            with eng.Fori(1, BATCHES - 1) as i:
                body(i)
            body(BATCHES - 1)

        def is_last(i):
            return isinstance(i, int) and i == BATCHES - 1

        @block.sync
        def _(sp):
            sp.dma_start(x_res[:, 0:2, :], x_t[:, 0:2, :]).then_inc(x_loaded, 16)

            def body(i):
                sp.wait_ge(x_loaded, 16 * i + 16)
                if not is_last(i):
                    sp.dma_start(x_res[:, bass.ds(2 * i + 2, 2), :],
                                 x_t[:, bass.ds(2 * i + 2, 2), :]).then_inc(x_loaded, 16)
                for u in range(2):
                    t = 2 * i + u
                    wait(sp, lo_ready, 8 * t - 8)
                    for r in range(3):
                        sp.dma_start(k_raw[ROWS * r:ROWS * r + ROWS, u, :, :],
                                     ctx_h[bass.ds(t, 1)].rearrange("o r h d -> (o r) h d")).then_inc(k_loaded[u], 16)
                    wait(sp, v_transposed, t - 1)
                    sp.dma_start(ctx_nat[:, u, :],
                                 ctx_t[bass.ds(t, 1)].rearrange("o p d -> (o p) d")).then_inc(ctx_loaded[u], 16)
                    sp.wait_ge(xhat_ready, t + 1)
                    sp.dma_start(xhat_t[bass.ds(t, 1)].rearrange("o p d -> (o p) d"),
                                 xhat[:, u, :]).then_inc(xhat_stored, 16)
                    sp.wait_ge(xhat_stored, 16 * t + 16)
                    for r in range(3):
                        sp.dma_start(q_raw[ROWS * r:ROWS * r + ROWS, u, :, :],
                                     xhat_h[bass.ds(t, 1)].rearrange("o r h d -> (o r) h d")).then_inc(q_loaded[u], 16)

            batches(sp, body)

        @block.gpsimd
        def _(pool):
            nc.gpsimd.memset(v_ones[:], 1.0).then_inc(ones_ready, 1)

            def split(i, u, g, prologue=False):
                t = 2 * i + u
                h, n = ORDER[g], 4 * t + g
                mid, low = slice(ROWS, 2 * ROWS), slice(2 * ROWS, STACK)
                if prologue:
                    pool.wait_ge(ones_ready, 1)
                    wait(pool, lo_ready, 2 * n)
                else:
                    pool.wait_ge(diag_ready, n - 2)
                    if g == 0:
                        wait(pool, x_added, t - 2)
                pool.wait_ge(hi_ready, 2 * n + 1)
                nc.gpsimd.tensor_tensor(k_stack[mid, u, h, :], k_raw[mid, u, h, :], k_stack[mid, u, h, :],
                                        ALU.subtract).then_inc(lo_ready, 1)
                pool.wait_ge(hi_ready, 2 * n + 2)
                pool.wait_ge(lo_ready, 2 * n + 1)
                nc.gpsimd.tensor_tensor(q_stack[low, u, h, :], q_raw[low, u, h, :], q_stack[low, u, h, :],
                                        ALU.subtract).then_inc(lo_ready, 1)

            def diag(i, u, g, splits):
                n = 4 * (2 * i + u) + g
                pool.wait_ge(reduced, 4 * n + 4)
                pool.wait_ge(lo_ready, 2 * splits)
                wait(pool, st_done, 4 * n - 4)
                nc.gpsimd.tensor_tensor(
                    neg_max_diag[:, g % 2], NEG_IDENT4,
                    maxima[:, g % 2, :].unsqueeze(2).broadcast_to([P, NT, P]), ALU.mult).then_inc(diag_ready, 1)

            def add(i, u, splits):
                t = 2 * i + u
                pool.wait_ge(lo_ready, 2 * splits)
                pool.wait_ge(gated_done, t + 1)
                xt = x_res[:, bass.ds(t, 1), :].rearrange("p o d -> p (o d)")
                nc.gpsimd.tensor_tensor(xt, gated[:, u, :], xt, ALU.add).then_inc(x_added, 1)

            for g in range(HEADS):
                split(0, 0, g, prologue=True)
            diag(0, 0, 0, HEADS)

            def body(i):
                for u in range(2):
                    for g in range(HEADS):
                        last_tile = is_last(i) and u == 1
                        n_next = 4 * (2 * i + u + 1) + g
                        splits = 4 * TILES if last_tile else n_next
                        if g < 3:
                            diag(i, u, g + 1, splits)
                        elif not last_tile:
                            diag(i + u, 1 - u, 0, splits)
                        if not last_tile:
                            split(i + u, 1 - u, g)
                        if g == 3:
                            splits = 4 * TILES if last_tile else n_next + 1
                            if u == 1:
                                add(i, 0, splits)
                            elif not (isinstance(i, int) and i == 0):
                                add(i - 1, 1, splits)

            batches(pool, body)
            add(BATCHES - 1, 1, 4 * TILES)

        @block.scalar
        def _(act):
            def k_hi(i, u, g):
                h, t = ORDER[g], 2 * i + u
                act.wait_ge(k_loaded[u], 48 * i + 48)
                wait(act, st_done, 16 * t + 4 * g - 28)
                nc.scalar.activation(k_stack[:, u, h, :], k_raw[:, u, h, :], ACT.Copy).then_inc(hi_ready, 1)

            def q_hi(i, u, g):
                h = ORDER[g]
                act.wait_ge(q_loaded[u], 48 * i + 48)
                nc.scalar.activation(q_stack[:, u, h, :], q_raw[:, u, h, :], ACT.Copy).then_inc(hi_ready, 1)

            def exps(i, u, g, k):
                n = 4 * (2 * i + u) + g
                act.wait_ge(st_done, 4 * n + k + 1)
                wait(act, pv_done, 4 * n + k - 7)
                nc.scalar.activation(probs[:, g % 2, k, :], ps_st[k % 2][:, :], ACT.Exp,
                                     scale=SCALE).then_inc(exp_done, 1)

            def evacuate(i, u, h):
                t, bank = 2 * i + u, h % 2
                act.wait_ge(pv_done, 8 * (2 * t + bank) + 8)
                wait(act, gated_done, t - 1)
                own, other = 32 * h, 32 * (h ^ 1)
                nc.scalar.activation(outputs[own:own + 32, u, :], ps_od[bank][own:own + 32, :],
                                     ACT.Copy).then_inc(evacuated, 1)
                nc.scalar.activation(denominators[own:own + 32, u, :], ps_od[bank][other:other + 32, :],
                                     ACT.Copy).then_inc(evacuated, 1)

            for g in range(HEADS):
                k_hi(0, 0, g)
                q_hi(0, 0, g)

            def body(i):
                for u in range(2):
                    more = not (is_last(i) and u == 1)
                    for g in range(HEADS):
                        before = (i, 0) if u else (i - 1, 1)
                        if g == 1 and not (isinstance(i, int) and i == 0 and u == 0):
                            leaving = [(*before, 1), (*before, 3)]
                        elif g == 3:
                            leaving = [(i, u, 0), (i, u, 2)]
                        else:
                            leaving = []
                        exps(i, u, g, 0)
                        if more:
                            k_hi(i + u, 1 - u, g)
                        exps(i, u, g, 1)
                        if more:
                            q_hi(i + u, 1 - u, g)
                        exps(i, u, g, 2)
                        if leaving:
                            evacuate(*leaving[0])
                        exps(i, u, g, 3)
                        if leaving:
                            evacuate(*leaving[1])

            batches(act, body)
            evacuate(BATCHES - 1, 1, 1)
            evacuate(BATCHES - 1, 1, 3)

        @block.vector
        def _(dve):
            def statistics(i):
                base = NORM_STEPS * i
                dve.wait_ge(x_loaded, 16 * i + 16)
                for u in range(2):
                    xt = x_res[:, bass.ds(2 * i + u, 1), :].rearrange("p o d -> p (o d)")
                    nc.vector.bn_stats(stats[:, u, :], xt).then_inc(ln_step, 1)
                wait(dve, xhat_ready, 2 * i)
                dve.wait_ge(ln_step, base + 2)
                nc.vector.memset(fence[:], 0.0)
                for u in range(2):
                    nc.vector.bn_aggr(mean_var[:, u, :], stats[:, u, :]).then_inc(ln_step, 1)

            def rstd_guess(i):
                dve.wait_ge(ln_step, NORM_STEPS * i + 4)
                rsqrt_guess(nc, dve, rstd[:], mean_var[:, :, 1], [tmp3[:, n, :] for n in range(3)],
                            ln_step, NORM_STEPS * i + 4)

            def rstd_newton(i, n):
                rsqrt_newton(nc, dve, rstd[:], [tmp3[:, n, :] for n in range(3)], ln_step,
                             NORM_STEPS * i + 4, n)

            def norm(i, u):
                t = 2 * i + u
                xt = x_res[:, bass.ds(t, 1), :].rearrange("p o d -> p (o d)")
                dve.wait_ge(ln_step, NORM_STEPS * i + NORM_STEPS)
                wait(dve, xhat_stored, 16 * t - 16)
                nc.vector.tensor_scalar(xhat[:, u, :], xt, mean_var[:, u, 0:1], rstd[:, u:u + 1],
                                        ALU.subtract, ALU.mult).then_inc(xhat_ready, 1)

            def v_copy(i, u):
                t = 2 * i + u
                dve.wait_ge(v_transposed, t + 1)
                wait(dve, pv_done, 16 * t - 16)
                src = ps_v.rearrange("p n (h r) -> p n h r", h=HEADS)
                for odd in range(2):
                    nc.vector.tensor_copy(v_ones[:, u, :, odd:HEADS:2, ROWS * odd:ROWS * odd + ROWS],
                                          src[:, :, odd:HEADS:2, :]).then_inc(v_ready, 1)

            def maxes(i, u, g, k):
                n = 4 * (2 * i + u) + g
                if k == 0:
                    wait(dve, diag_ready, n - 1)
                dve.wait_ge(s_done, 4 * n + k + 1)
                nc.vector.tensor_reduce(maxima[:, g % 2, k:k + 1], ps_s[k][:, :], AX,
                                        ALU.max).then_inc(reduced, 1)

            def reciprocals(i, u, j):
                t = 2 * i + u
                cols = slice(P * j, P * j + P)
                if j == 0:
                    dve.wait_ge(evacuated, 8 * t + 8)
                    wait(dve, gated_done, t)
                nc.vector.reciprocal(recip[:, cols], denominators[:, u, cols]).then_inc(recip_done, 1)

            def gate(i, u):
                t = 2 * i + u
                dve.wait_ge(recip_done, NT * t + NT)
                wait(dve, x_added, t - 1)
                nc.vector.scalar_tensor_tensor(
                    out=gated[:, u, :], in0=outputs[:, u, :], scalar=c["gates"][:, 0:1], in1=recip[:],
                    op0=ALU.mult, op1=ALU.mult).then_inc(gated_done, 1)

            statistics(0)
            rstd_guess(0)
            for n in range(3):
                rstd_newton(0, n)
            norm(0, 0)
            norm(0, 1)
            dve.wait_ge(ones_ready, 1)
            v_copy(0, 0)
            for k in range(NT):
                maxes(0, 0, 0, k)

            def body(i):
                for u in range(2):
                    last_tile = is_last(i) and u == 1
                    norms = u == 0 and not is_last(i)
                    divides = not (isinstance(i, int) and i == 0 and u == 0)
                    before = (i, 0) if u else (i - 1, 1)
                    for g in range(HEADS):
                        for k in range(NT):
                            if g < 3:
                                maxes(i, u, g + 1, k)
                            elif not last_tile:
                                maxes(i + u, 1 - u, 0, k)
                        if g == 0 and norms:
                            statistics(i + 1)
                            rstd_guess(i + 1)
                        if g == 1:
                            if not last_tile:
                                v_copy(i + u, 1 - u)
                            if norms:
                                for n in range(3):
                                    rstd_newton(i + 1, n)
                        if g == 2:
                            if not is_last(i):
                                norm(i + 1, u)
                            if divides:
                                reciprocals(*before, 0)
                                reciprocals(*before, 1)
                        if g == 3 and divides:
                            reciprocals(*before, 2)
                            reciprocals(*before, 3)
                            gate(*before)

            batches(dve, body)
            for j in range(NT):
                reciprocals(BATCHES - 1, 1, j)
            gate(BATCHES - 1, 1)

        @block.tensor
        def _(pe):
            def v_transpose(i, u):
                t = 2 * i + u
                pe.wait_ge(ctx_loaded[u], 16 * i + 16)
                wait(pe, reduced, 16 * t - 4)
                for k in range(NT):
                    mm = nc.tensor.transpose(ps_v[:, k, :], ctx_nat[:, u, P * k:P * k + P], c["ident"][:])
                mm.then_inc(v_transposed, 1)

            def scores(i, u, g, k):
                h, n = ORDER[g], 4 * (2 * i + u) + g
                if k == 0:
                    pe.wait_ge(lo_ready, 2 * n + 2)
                wait(pe, reduced, 4 * n + k - 3)
                if k == NT - 1 and g == 3 and not (is_last(i) and u == 1):
                    pe.wait_ge(v_ready, 2 * (2 * i + u) + 4)
                if k == NT - 1 and isinstance(i, int) and i == 0 and u == 0 and g == 0:
                    pe.wait_ge(v_ready, 2)
                nc.tensor.matmul(ps_s[k][:, :], q_stack[:, u, h, P * k:P * k + P], k_stack[:, u, h, :],
                                 start=True, stop=True).then_inc(s_done, 1)

            def scores_t(i, u, g, k):
                h, n = ORDER[g], 4 * (2 * i + u) + g
                if k == 0:
                    pe.wait_ge(diag_ready, n + 1)
                wait(pe, exp_done, 4 * n + k - 1)
                nc.tensor.matmul(ps_st[k % 2][:, :], k_stack[:, u, h, P * k:P * k + P], q_stack[:, u, h, :],
                                 start=True, stop=False)
                nc.tensor.matmul(ps_st[k % 2][:, :], c["ones_r"][:], neg_max_diag[:, g % 2],
                                 start=False, stop=True).then_inc(st_done, 1)

            def values(i, u, g, k):
                h, n = ORDER[g], 4 * (2 * i + u) + g
                t = 2 * i + u
                if k == 0 and g == 0:
                    pe.wait_ge(v_ready, 2 * t + 2)
                    wait(pe, evacuated, 8 * t - 4)
                if k == 0 and g == 2:
                    wait(pe, evacuated, 8 * t)
                pe.wait_ge(exp_done, 4 * n + k + 1)
                col = 64 * (h // 2)
                nc.tensor.matmul(ps_od[h % 2][col:col + 64, :], v_ones[:, u, k, h, :], probs[:, g % 2, k, :],
                                 start=(k == 0), stop=(k == NT - 1)).then_inc(pv_done, 1)

            v_transpose(0, 0)
            for k in range(NT):
                scores(0, 0, 0, k)

            def body(i):
                for u in range(2):
                    last_tile = is_last(i) and u == 1
                    for g in range(HEADS):
                        for k in range(NT):
                            if k < 2:
                                for kk in (2 * k, 2 * k + 1):
                                    if g < 3:
                                        scores(i, u, g + 1, kk)
                                    elif not last_tile:
                                        scores(i + u, 1 - u, 0, kk)
                            if (g, k) == (1, 3) and not last_tile:
                                v_transpose(i + u, 1 - u)
                            scores_t(i, u, g, k)
                            if g > 0:
                                values(i, u, g - 1, k)
                            elif u == 1:
                                values(i, 0, 3, k)
                            elif not (isinstance(i, int) and i == 0):
                                values(i - 1, 1, 3, k)

            batches(pe, body)
            for k in range(NT):
                values(BATCHES - 1, 1, 3, k)


def split_weights(nc, c, t, w):
    D = t["L0_ffn_W_up"].shape[0]
    K = D // P
    E = t["L0_ffn_W_gate"].shape[0]
    with ExitStack() as ctx:
        raw = {n: ctx.enter_context(nc.sbuf_tensor(f"raw_{n}", [P, K, D], F32)) for n in ("up", "down", "expert")}
        raw_gate = ctx.enter_context(nc.sbuf_tensor("raw_gate", [E, D], F32))
        ps_w = ctx.enter_context(nc.psum_tensor("ps_w", [P, 8, D], F32))
        w_loaded = {n: ctx.enter_context(nc.semaphore(f"w_loaded_{n}"))
                    for n in ("up", "down", "expert", "gate", "route")}
        w_transposed = ctx.enter_context(nc.semaphore("w_transposed"))
        gate_transposed = ctx.enter_context(nc.semaphore("gate_transposed"))
        w_hi = ctx.enter_context(nc.semaphore("w_hi"))
        w_lo = ctx.enter_context(nc.semaphore("w_lo"))
        block = ctx.enter_context(nc.Block())

        @block.sync
        def _(sp):
            for n in ("up", "down", "expert"):
                sp.dma_start(raw[n][:], t[f"L0_ffn_W_{n}"].rearrange("(k p) n -> p k n", p=P)).then_inc(w_loaded[n], 16)
            sp.dma_start(raw_gate[:], t["L0_ffn_W_gate"]).then_inc(w_loaded["gate"], 16)
            sp.dma_start(w["route"][:], t["L1_ffn_Wg"].rearrange("(k p) n -> p k n", p=P)).then_inc(w_loaded["route"], 16)
            sp.dma_start(w["route_bias"][:], bass.AP(tensor=t["L1_ffn_bg"].tensor, offset=0,
                                                     ap=[[0, P], [1, 4]])).then_inc(w_loaded["route"], 16)
            sp.wait_ge(w_loaded["route"], 32)

        @block.tensor
        def _(pe):
            for m, n in enumerate(("up", "down")):
                pe.wait_ge(w_loaded[n], 16)
                for k in range(K):
                    for o in range(K):
                        mm = nc.tensor.transpose(ps_w[:, 4 * m + k, P * o:P * o + P], raw[n][:, o, P * k:P * k + P],
                                                 c["ident"][:])
                    mm.then_inc(w_transposed, 1)
            pe.wait_ge(w_loaded["gate"], 16)
            pe.wait_ge(w_lo, 2)
            for k in range(K):
                mm = nc.tensor.transpose(ps_w[:, 0, E * k:E * k + E], raw_gate[:, P * k:P * k + P],
                                         c["ident"][0:E, 0:E])
            mm.then_inc(gate_transposed, 1)

        def parts():
            out = []
            for m, n in enumerate(("up", "down")):
                for k in range(K):
                    out.append((w[n + "_hi"][:, k, :], w[n + "_lo"][:, k, :], ps_w[:, 4 * m + k, :],
                                w_transposed, 4 * m + k + 1))
            out.append((w["expert_hi"][:], w["expert_lo"][:], raw["expert"][:], w_loaded["expert"], 16))
            out.append((w["gate_hi"][:], w["gate_lo"][:],
                        ps_w[:, 0, 0:E * K].rearrange("p (k e) -> p k e", k=K), gate_transposed, 1))
            return out

        @block.scalar
        def _(act):
            for hi, lo, src, s, count in parts():
                act.wait_ge(s, count)
                nc.scalar.activation(hi, src, ACT.Copy).then_inc(w_hi, 1)

        @block.vector
        def _(dve):
            for n, (hi, lo, src, s, count) in enumerate(parts()):
                dve.wait_ge(w_hi, n + 1)
                nc.vector.tensor_tensor(lo, src, hi, ALU.subtract).then_inc(w_lo, 1)


def dense_and_memory(nc, c, w, t, x_res, xhat_d, out, logits):
    ctx_in, mask_in = t["ctx_2048"], t["mask_BxS2_bk0"]
    B, S, D = ctx_in.shape
    K = D // P
    U = S // P
    E = t["L0_ffn_W_gate"].shape[0]
    R = t["L1_ffn_Wg"].shape[1]
    SCALE = float(np.float32(1.0) / np.sqrt(np.float32(D)))
    NEG = 1e30
    RW = 8
    ctx_t = row_major(ctx_in).rearrange("(b u p) d -> b p u d", u=U, p=P)
    xhat_t = xhat_d.rearrange("(b u p) d -> b p u d", u=U, p=P)
    out_t = row_major(out).rearrange("(b u p) d -> b p u d", u=U, p=P)

    with ExitStack() as ctx:
        def sb(name, shape, dt=F32):
            return ctx.enter_context(nc.sbuf_tensor(name, shape, dt))

        def sem(name):
            return ctx.enter_context(nc.semaphore(name))

        def pair(name, shape):
            return sb(name + "_hi", shape, F32R), sb(name + "_lo", shape, F32R)

        xhat1 = sb("xhat1", [P, U, D])
        xhat2 = sb("xhat2", [P, U, D])
        xhat3 = sb("xhat3", [P, U, D])
        xt1 = pair("xt1", [P, K, S])
        xt2 = pair("xt2", [P, K, S])
        xt3 = sb("xt3", [P, K, S])
        hid = pair("hid", [P, K, S])
        mem_raw = sb("mem_raw", [P, U, D])
        mem = pair("mem", [P, U, D])
        mem_t = pair("mem_t", [P, K, S])
        masked = sb("masked", [P, U, S])
        probs = sb("mem_probs", [P, U, S])
        probs_t = pair("probs_t", [P, U, S])
        mask_u8 = sb("mask_u8", [P, B, S], U8)
        mask_f = sb("mask_f", [P, S])
        mask_add = sb("mask_add", [P, S])
        valid_gate = sb("valid_gate", [P, 2])
        row_max = sb("row_max", [P, U])
        neg_max = sb("neg_max", [P, U])
        row_sum = sb("row_sum", [P, U])
        row_scale = sb("row_scale", [P, 2, U])
        top_in = sb("top_in", [P, U, E])
        top = sb("top", [P, U, 8])
        rw = sb("rw", [P, 6, U])
        stats = sb("row_stats", [P, 3, U, 6])
        mean_var = sb("mean_vars", [P, 3, U, 2])
        rstd = sb("rstds", [P, 3, U])
        rsqrt_tmp = sb("rsqrt_tmp", [P, 3, 3 * U])
        fence = {n: sb(f"fence_{n}", [P, 1]) for n in ("top", "first", "mid", "last", "moments")}
        ps = ctx.enter_context(nc.psum_tensor("ps_b", [P, 8, 512], F32))
        halves = lambda bank: ps[:, bank, :].rearrange("p (k s) -> p k s", s=S)

        mem_loaded, mask_loaded = sem("mem_loaded"), sem("mask_loaded")
        xhat1_ready, xhat2_ready, xhat3_ready = sem("xhat1_ready"), sem("xhat2_ready"), sem("xhat3_ready")
        moments = {n: sem(f"moments{n}") for n in (1, 2, 3)}
        chain = sem("rstd_chain")
        xt1_ps, xt1_hi, xt1_lo = sem("xt1_ps"), sem("xt1_hi"), sem("xt1_lo")
        xt2_ps, xt2_hi, xt2_lo = sem("xt2_ps"), sem("xt2_hi"), sem("xt2_lo")
        memt_ps, memt_hi, memt_lo = sem("memt_ps"), sem("memt_hi"), sem("memt_lo")
        mem_hi, mem_lo = sem("mem_hi"), sem("mem_lo")
        gate_ps, gate_copied = sem("gate_ps"), sem("gate_copied")
        rw_step, rw_exp = sem("rw_step"), sem("rw_exp")
        up_ps, hid_hi, hid_lo = sem("up_ps"), sem("hid_hi"), sem("hid_lo")
        down_ps, x1_step = sem("down_ps"), sem("x1_step")
        scores_ps = sem("scores_ps")
        mask_ready, valid_ready = sem("mask_ready"), sem("valid_ready")
        sm_step, exp_done = sem("sm_step"), sem("mem_exp_done")
        pt_ps, pt_hi, pt_lo = sem("pt_ps"), sem("pt_hi"), sem("pt_lo")
        read_ps, scale_step, x2_ready = sem("read_ps"), sem("scale_step"), sem("x2_ready")
        xt3_ps, xt3_ready = sem("xt3_ps"), sem("xt3_ready")
        route_ps, logits_ready = sem("route_ps"), sem("logits_ready")
        xhat_stored, x_stored = sem("xhat3_stored"), sem("x_stored")

        block = ctx.enter_context(nc.Block())

        def iterations(eng, body):
            for s in range(3):
                body(s, s < B, s >= 1, s >= 2, True)
            with eng.Fori(3, B - 2) as s:
                body(s, True, True, True, True)
            body(B - 2, True, True, True, True)
            body(B - 1, True, True, True, False)
            body(B, False, True, True, False)
            body(B + 1, False, False, True, False)

        def x_tile(b, u):
            return x_res[:, bass.ds(U * b + u, 1), :].rearrange("p o d -> p (o d)")

        @block.sync
        def _(sp):
            sp.dma_start(mask_u8[:], bass.AP(tensor=mask_in.tensor, offset=0, ap=[[0, P], [S, B], [1, S]])
                         ).then_inc(mask_loaded, 16)

            def body(s, f, a, r, more):
                if f:
                    wait(sp, memt_ps, 2 * s)
                    wait(sp, mem_lo, s)
                    sp.dma_start(mem_raw[:], ctx_t[bass.ds(s, 1)].rearrange("o p u d -> (o p) u d")
                                 ).then_inc(mem_loaded, 16)

            iterations(sp, body)

        @block.gpsimd
        def _(pool):
            def body(s, f, a, r, more):
                if not a:
                    return
                b = s - 1
                pool.wait_ge(mem_hi, b + 1)
                wait(pool, read_ps, U * b)
                nc.gpsimd.tensor_tensor(mem[1][:], mem_raw[:], mem[0][:], ALU.subtract).then_inc(mem_lo, 1)

            iterations(pool, body)

        @block.scalar
        def _(act):
            def xt1_part(b):
                wait(act, down_ps, U * b)
                for n in range(2):
                    act.wait_ge(xt1_ps, 2 * b + n + 1)
                    nc.scalar.activation(xt1[0][:, 2 * n:2 * n + 2, :], halves(n), ACT.Copy).then_inc(xt1_hi, 1)

            xt1_part(0)

            def body(s, f, a, r, more):
                b = s - 1
                if f:
                    act.wait_ge(rw_step, RW * s + 3)
                    nc.scalar.activation(rw[:, 1, :], rw[:, 0, :], ACT.Exp).then_inc(rw_exp, 1)
                    for n in range(2):
                        act.wait_ge(up_ps, 2 * s + n + 1)
                        nc.scalar.activation(hid[0][:, 2 * n:2 * n + 2, :], halves(2 + n), ACT.Relu
                                             ).then_inc(hid_hi, 1)
                if a:
                    wait(act, scores_ps, b)
                    for n in range(2):
                        act.wait_ge(memt_ps, 2 * b + n + 1)
                        nc.scalar.activation(mem_t[0][:, 2 * n:2 * n + 2, :], halves(6 + n), ACT.Copy
                                             ).then_inc(memt_hi, 1)
                    for n in range(2):
                        act.wait_ge(xt2_ps, 2 * b + n + 1)
                        nc.scalar.activation(xt2[0][:, 2 * n:2 * n + 2, :], halves(4 + n), ACT.Copy
                                             ).then_inc(xt2_hi, 1)
                    act.wait_ge(mem_loaded, 16 * b + 16)
                    wait(act, read_ps, U * b)
                    wait(act, mem_lo, b)
                    nc.scalar.activation(mem[0][:], mem_raw[:], ACT.Copy).then_inc(mem_hi, 1)
                if r:
                    q = s - 2
                    act.wait_ge(xhat3_ready, U * q + U)
                    act.dma_start(xhat_t[bass.ds(q, 1)].rearrange("o p u d -> (o p) u d"),
                                  xhat3[:]).then_inc(xhat_stored, 16)
                    act.dma_start(out_t[bass.ds(q, 1)].rearrange("o p u d -> (o p) u d"),
                                  x_res[:, bass.ds(U * q, U), :]).then_inc(x_stored, 16)
                    wait(act, route_ps, q)
                    for n in range(2):
                        act.wait_ge(xt3_ps, 2 * q + n + 1)
                        nc.scalar.activation(xt3[:, 2 * n:2 * n + 2, :], halves(4 + n), ACT.Copy
                                             ).then_inc(xt3_ready, 1)
                if a:
                    act.wait_ge(sm_step, 4 * b + 4)
                    wait(act, pt_ps, b)
                    wait(act, scale_step, 2 * b)
                    for u in range(U):
                        nc.scalar.activation(probs[:, u, :], masked[:, u, :], ACT.Exp, bias=neg_max[:, u:u + 1],
                                             accum_out=row_sum[:, u:u + 1]).then_inc(exp_done, 1)
                    act.wait_ge(pt_ps, b + 1)
                    nc.scalar.activation(probs_t[0][:], halves(7), ACT.Copy).then_inc(pt_hi, 1)
                if f and more:
                    xt1_part(s + 1)

            iterations(act, body)
            act.wait_ge(xhat_stored, 16 * B)
            act.wait_ge(x_stored, 16 * B)

        @block.vector
        def _(dve):
            ready = {1: xhat1_ready, 2: xhat2_ready, 3: xhat3_ready}

            def statistics(n, b, u):
                nc.vector.bn_stats(stats[:, n - 1, u, :], x_tile(b, u)).then_inc(moments[n], 1)

            def rstd_chain(number, which):
                for n, b in which:
                    dve.wait_ge(moments[n], 2 * U * b + U)
                    wait(dve, ready[n], U * b)
                nc.vector.memset(fence["moments"][:], 0.0)
                for n, b in which:
                    for u in range(U):
                        nc.vector.bn_aggr(mean_var[:, n - 1, u, :], stats[:, n - 1, u, :]).then_inc(moments[n], 1)
                for n, b in which:
                    dve.wait_ge(moments[n], 2 * U * b + 2 * U)
                inverse_sqrt(nc, dve, rstd[:].rearrange("p n u -> p (n u)"),
                             mean_var[:].rearrange("p n u t -> p (n u) t")[:, :, 1],
                             [rsqrt_tmp[:, m, :] for m in range(3)], chain, RSQRT_STEPS * number)

            def norm(n, b, dst, number, free_sem, free_count):
                dve.wait_ge(chain, RSQRT_STEPS * (number + 1))
                wait(dve, free_sem, free_count)
                for u in range(U):
                    nc.vector.tensor_scalar(dst[:, u, :], x_tile(b, u), mean_var[:, n - 1, u, 0:1],
                                            rstd[:, n - 1, u:u + 1], ALU.subtract, ALU.mult).then_inc(ready[n], 1)

            def lo_part(dst, bank, n, hi, hi_sem, count, lo_sem):
                dve.wait_ge(hi_sem, count)
                nc.vector.tensor_tensor(dst[1][:, 2 * n:2 * n + 2, :], halves(bank), hi[:, 2 * n:2 * n + 2, :],
                                        ALU.subtract).then_inc(lo_sem, 1)

            def xt1_part(b):
                for n in range(2):
                    lo_part(xt1, n, n, xt1[0], xt1_hi, 2 * b + n + 1, xt1_lo)

            nc.vector.memset(mean_var[:], 0.0).then_inc(mask_ready, 1)
            dve.wait_ge(mask_ready, 1)
            for b in range(2):
                for u in range(U):
                    statistics(1, b, u)
                rstd_chain(b, [(1, b)])
                if b == 0:
                    norm(1, 0, xhat1, 0, xt1_ps, 0)
                    xt1_part(0)

            def body(s, f, a, r, more):
                b = s - 1
                number = s + 2
                if f and more:
                    norm(1, s + 1, xhat1, number - 1, xt1_ps, 2 * s + 2)
                if a:
                    dve.wait_ge(mask_loaded, 16)
                    nc.vector.tensor_copy(mask_f[:].unsqueeze(1), mask_u8[:, bass.ds(b, 1), :]).then_inc(mask_ready, 1)
                    dve.wait_ge(mask_ready, 2 * b + 2)
                    nc.vector.tensor_scalar(mask_add[:], mask_f[:], 1.0, NEG, ALU.subtract, ALU.mult
                                            ).then_inc(mask_ready, 1)
                    wait(dve, scale_step, 2 * b)
                    nc.vector.tensor_reduce(valid_gate[:, 0:1], mask_f[:], AX, ALU.max).then_inc(valid_ready, 1)
                    dve.wait_ge(valid_ready, 2 * b + 1)
                    nc.vector.tensor_scalar(valid_gate[:, 1:2], valid_gate[:, 0:1], c["gates"][:, 1:2], None,
                                            ALU.mult).then_inc(valid_ready, 1)
                if f:
                    base = RW * s
                    dve.wait_ge(gate_ps, s + 1)
                    nc.vector.tensor_copy(top_in[:], ps[:, 3, 0:U * E].rearrange("p (u e) -> p u e", u=U)
                                          ).then_inc(gate_copied, 1)
                    dve.wait_ge(gate_copied, s + 1)
                    nc.vector.memset(fence["top"][:], 0.0)
                    for u in range(U):
                        nc.vector.max(top[:, u, :], top_in[:, u, :]).then_inc(rw_step, 1)
                    dve.wait_ge(rw_step, base + 2)
                    nc.vector.tensor_tensor(rw[:, 0, :], top[:, :, 1], top[:, :, 0], ALU.subtract).then_inc(rw_step, 1)
                    dve.wait_ge(rw_exp, s + 1)
                    nc.vector.tensor_scalar(rw[:, 2, :], rw[:, 1, :], 1.0, None, ALU.add).then_inc(rw_step, 1)
                    dve.wait_ge(rw_step, base + 4)
                    nc.vector.reciprocal(rw[:, 3, :], rw[:, 2, :]).then_inc(rw_step, 1)
                    dve.wait_ge(rw_step, base + 5)
                    nc.vector.tensor_tensor(rw[:, 4, :], rw[:, 1, :], rw[:, 3, :], ALU.mult).then_inc(rw_step, 1)
                    dve.wait_ge(rw_step, base + 6)
                    nc.vector.tensor_tensor(rw[:, 2, :], rw[:, 3, :], rw[:, 4, :], ALU.add).then_inc(rw_step, 1)
                    dve.wait_ge(rw_step, base + 7)
                    nc.vector.tensor_scalar(rw[:, 5, :], rw[:, 2, :], c["gates"][:, 2:3], None, ALU.mult
                                            ).then_inc(rw_step, 1)
                    for n in range(2):
                        dve.wait_ge(hid_hi, 2 * s + n + 1)
                        nc.vector.scalar_tensor_tensor(
                            out=hid[1][:, 2 * n:2 * n + 2, :], in0=halves(2 + n), scalar=0.0,
                            in1=hid[0][:, 2 * n:2 * n + 2, :], op0=ALU.max, op1=ALU.subtract).then_inc(hid_lo, 1)
                if a:
                    for n in range(2):
                        lo_part(mem_t, 6 + n, n, mem_t[0], memt_hi, 2 * b + n + 1, memt_lo)
                    for n in range(2):
                        lo_part(xt2, 4 + n, n, xt2[0], xt2_hi, 2 * b + n + 1, xt2_lo)
                ahead = f and not (isinstance(s, int) and s + 2 >= B)
                if ahead:
                    for u in range(U):
                        statistics(1, s + 2, u)

                def first_ffn(u):
                    n = 2 * (U * s + u)
                    dve.wait_ge(down_ps, U * s + u + 1)
                    xt = x_tile(s, u)
                    nc.vector.scalar_tensor_tensor(out=xt, in0=ps[:, 2 * u, :], scalar=c["gates"][:, 2:3], in1=xt,
                                                   op0=ALU.mult, op1=ALU.add).then_inc(x1_step, 1)
                    dve.wait_ge(x1_step, n + 1)
                    dve.wait_ge(rw_step, RW * s + RW)
                    nc.vector.scalar_tensor_tensor(out=xt, in0=ps[:, 2 * u + 1, :], scalar=rw[:, 5, u:u + 1], in1=xt,
                                                   op0=ALU.mult, op1=ALU.add).then_inc(x1_step, 1)
                    dve.wait_ge(x1_step, n + 2)
                    nc.vector.memset(fence["mid" if u else "first"][:], 0.0)
                    statistics(2, s, u)

                if f:
                    first_ffn(0)
                if a:
                    dve.wait_ge(mask_ready, 2 * b + 3)
                    dve.wait_ge(scores_ps, b + 1)
                    wait(dve, exp_done, U * b)
                    nc.vector.scalar_tensor_tensor(
                        out=masked[:], in0=halves(6), scalar=SCALE,
                        in1=mask_f[:].unsqueeze(1).broadcast_to([P, U, S]), op0=ALU.mult, op1=ALU.mult
                    ).then_inc(sm_step, 1)
                    dve.wait_ge(sm_step, 4 * b + 1)
                    nc.vector.tensor_tensor(masked[:], masked[:], mask_add[:].unsqueeze(1).broadcast_to([P, U, S]),
                                            ALU.add).then_inc(sm_step, 1)
                    dve.wait_ge(sm_step, 4 * b + 2)
                    nc.vector.tensor_reduce(row_max[:], masked[:], AX, ALU.max).then_inc(sm_step, 1)
                    dve.wait_ge(sm_step, 4 * b + 3)
                    nc.vector.tensor_scalar(neg_max[:], row_max[:], -1.0, None, ALU.mult).then_inc(sm_step, 1)
                if f:
                    first_ffn(1)
                if r:
                    q = s - 2
                    dve.wait_ge(route_ps, q + 1)
                    nc.vector.tensor_tensor(
                        logits[:, bass.ds(U * q, U), :], ps[:, 5, 0:U * R].rearrange("p (u e) -> p u e", u=U),
                        w["route_bias"][:].unsqueeze(1).broadcast_to([P, U, R]), ALU.add).then_inc(logits_ready, 1)
                if a:
                    dve.wait_ge(pt_hi, b + 1)
                    nc.vector.tensor_tensor(probs_t[1][:], halves(7), probs_t[0][:], ALU.subtract).then_inc(pt_lo, 1)
                if f and more:
                    xt1_part(s + 1)
                if a:
                    dve.wait_ge(exp_done, U * b + U)
                    nc.vector.reciprocal(row_scale[:, 0, :], row_sum[:]).then_inc(scale_step, 1)
                    dve.wait_ge(scale_step, 2 * b + 1)
                    dve.wait_ge(valid_ready, 2 * b + 2)
                    wait(dve, x2_ready, U * b)
                    nc.vector.tensor_scalar(row_scale[:, 1, :], row_scale[:, 0, :], valid_gate[:, 1:2], None,
                                            ALU.mult).then_inc(scale_step, 1)
                    dve.wait_ge(scale_step, 2 * b + 2)
                    for u in range(U):
                        dve.wait_ge(read_ps, U * b + u + 1)
                        xt = x_tile(b, u)
                        nc.vector.scalar_tensor_tensor(out=xt, in0=ps[:, 4 + u, :], scalar=row_scale[:, 1, u:u + 1],
                                                       in1=xt, op0=ALU.mult, op1=ALU.add).then_inc(x2_ready, 1)
                    dve.wait_ge(x2_ready, U * b + U)
                    nc.vector.memset(fence["last"][:], 0.0)
                    for u in range(U):
                        statistics(3, b, u)
                if f or a:
                    rstd_chain(number, [(1, s + 2)] * bool(ahead) + [(2, s)] * bool(f) + [(3, b)] * bool(a))
                if f:
                    norm(2, s, xhat2, number, xt2_ps, 2 * s)
                if a:
                    wait(dve, xhat_stored, 16 * b)
                    norm(3, b, xhat3, number, xt3_ps, 2 * b)

            iterations(dve, body)

        @block.tensor
        def _(pe):
            def transposes(src, bank, done):
                for n in range(2):
                    for k in (2 * n, 2 * n + 1):
                        for u in range(U):
                            mm = nc.tensor.transpose(halves(bank + n)[:, k % 2, P * u:P * u + P],
                                                     src[:, u, P * k:P * k + P], c["ident"][:])
                    mm.then_inc(done, 1)

            def product(dst, lhs, rhs):
                n = len(lhs)
                for k in range(n):
                    for a_, b_ in ((0, 0), (0, 1), (1, 0)):
                        mm = nc.tensor.matmul(dst, lhs[k][a_], rhs[k][b_], start=(k == 0 and a_ == b_),
                                              stop=(k == n - 1 and a_ == 1))
                return mm

            def chunks(pair_, cols):
                return [[x[:, k, cols] for x in pair_] for k in range(K)]

            everything = slice(None)

            def down(s, u):
                tok = slice(P * u, P * u + P)
                product(ps[:, 2 * u, :], chunks(hid, tok), chunks((w["down_hi"], w["down_lo"]), everything))
                product(ps[:, 2 * u + 1, :], chunks(xt1, tok), chunks((w["expert_hi"], w["expert_lo"]), everything)
                        ).then_inc(down_ps, 1)

            def xt1_transposes(b):
                pe.wait_ge(xhat1_ready, U * b + U)
                wait(pe, x1_step, 2 * U * b - 2)
                transposes(xhat1, 0, xt1_ps)

            xt1_transposes(0)

            def body(s, f, a, r, more):
                b = s - 1
                if f:
                    pe.wait_ge(xt1_lo, 2 * s + 2)
                    wait(pe, x1_step, 2 * U * s)
                    for u in range(U):
                        mm = product(ps[:, 3, E * u:E * u + E], chunks(xt1, slice(P * u, P * u + P)),
                                     chunks((w["gate_hi"], w["gate_lo"]), everything))
                    mm.then_inc(gate_ps, 1)
                    for n in range(2):
                        if n == 1:
                            pe.wait_ge(gate_copied, s + 1)
                        for o in (2 * n, 2 * n + 1):
                            mm = product(halves(2 + n)[:, o % 2, :],
                                         chunks((w["up_hi"], w["up_lo"]), slice(P * o, P * o + P)),
                                         chunks(xt1, everything))
                        mm.then_inc(up_ps, 1)
                if a:
                    pe.wait_ge(mem_loaded, 16 * b + 16)
                    wait(pe, pt_lo, b)
                    wait(pe, sm_step, 4 * b)
                    transposes(mem_raw, 6, memt_ps)
                    pe.wait_ge(xhat2_ready, U * b + U)
                    wait(pe, x2_ready, U * b)
                    transposes(xhat2, 4, xt2_ps)
                if f:
                    pe.wait_ge(hid_lo, 2 * s + 2)
                    down(s, 0)
                if a:
                    pe.wait_ge(xt2_lo, 2 * b + 2)
                    pe.wait_ge(memt_lo, 2 * b + 2)
                    for u in range(U):
                        mm = product(halves(6)[:, u, :], chunks(xt2, slice(P * u, P * u + P)),
                                     chunks(mem_t, everything))
                    mm.then_inc(scores_ps, 1)
                if r:
                    q = s - 2
                    pe.wait_ge(xhat3_ready, U * q + U)
                    if a:
                        pe.wait_ge(xt2_lo, 2 * b + 2)
                    else:
                        pe.wait_ge(x2_ready, U * q + U)
                    transposes(xhat3, 4, xt3_ps)
                if f:
                    down(s, 1)
                if r:
                    q = s - 2
                    pe.wait_ge(xt3_ready, 2 * q + 2)
                    for u in range(U):
                        for k in range(K):
                            mm = nc.tensor.matmul(ps[:, 5, R * u:R * u + R], xt3[:, k, P * u:P * u + P],
                                                  w["route"][:, k, :], start=(k == 0), stop=(k == K - 1))
                    mm.then_inc(route_ps, 1)
                if a:
                    pe.wait_ge(exp_done, U * b + U)
                    for m in range(U):
                        for u in range(U):
                            mm = nc.tensor.transpose(halves(7)[:, m, P * u:P * u + P],
                                                     probs[:, u, P * m:P * m + P], c["ident"][:])
                    mm.then_inc(pt_ps, 1)
                if f and more:
                    xt1_transposes(s + 1)
                if a:
                    if r:
                        pe.wait_ge(logits_ready, s - 1)
                    pe.wait_ge(pt_lo, b + 1)
                    pe.wait_ge(mem_lo, b + 1)
                    for u in range(U):
                        product(ps[:, 4 + u, :], [[x[:, m, P * u:P * u + P] for x in probs_t] for m in range(U)],
                                [[x[:, m, :] for x in mem] for m in range(U)]).then_inc(read_ps, 1)

            iterations(pe, body)


def route(nc, c, logits, capacity, slot_token, slot_weight):
    T, E = logits.shape[1], logits.shape[2]
    B = capacity // P
    DIGIT = 3
    RADIX = 1 << DIGIT
    ROUNDS = 10
    BF16 = mybir.dt.bfloat16
    COLS = 5
    with ExitStack() as ctx:
        def sb(name, shape, dt=F32):
            return ctx.enter_context(nc.sbuf_tensor(name, shape, dt))

        def psum(name, shape):
            return ctx.enter_context(nc.psum_tensor(name, shape, F32))

        def sem(name):
            return ctx.enter_context(nc.semaphore(name))

        digit_i = sb("digit_i", [P, RADIX], I32)
        digits = sb("digits", [P, ROUNDS, RADIX], I32)
        before = sb("before", [P, P])
        token_i, token = sb("token_i", [P, T], I32), sb("token", [P, T])
        tile_i, row_i = sb("tile_i", [P, T], I32), sb("row_i", [P, T], I32)
        hi_iota_i, hi_iota = sb("hi_iota_i", [P, P], I32), sb("hi_iota", [P, P], BF16)
        lo_iota = sb("lo_iota", [P, B], BF16)
        restart = sb("restart", [P, 2 * E, T])
        beats = sb("beats", [P, T, E, E])
        rank = sb("rank", [P, T, E])
        assigned = sb("assigned", [P, T, E])
        best = sb("best", [P, T])
        shifted, expo = sb("shifted", [P, T, E]), sb("expo", [P, T, E])
        total, inv = sb("total", [P, T]), sb("inv", [P, T])
        prob = sb("prob", [P, T, E])
        unassigned = sb("unassigned", [P, T, E])
        score = sb("score", [P, E, T])
        kth = sb("kth", [P, E])
        cand = sb("cand", [P, E, RADIX])
        at_least = sb("at_least", [P, E, RADIX, T])
        part_count = sb("part_count", [P, E, RADIX])
        kept = sb("kept", [P, E, RADIX])
        flags = sb("flags", [P, 2, E, T])
        running = sb("running", [P, 2, E, T])
        earlier = sb("earlier", [P, 2, E, T])
        wanted = sb("wanted", [P, E])
        ties = sb("ties", [P, E])
        chosen_n = sb("chosen_n", [P, E])
        fits = sb("fits", [P, E, T])
        chosen = sb("chosen", [P, E, T])
        taken = sb("taken", [P, E, T])
        other = sb("other", [P, E, T])
        slot = sb("slot", [P, E, T])
        slot_i, slot_hi_i, slot_lo_i = (sb(n, [P, E, T], I32) for n in ("slot_i", "slot_hi_i", "slot_lo_i"))
        slot_hi, slot_lo = sb("slot_hi", [P, E, T], BF16), sb("slot_lo", [P, E, T], BF16)
        hot_hi = sb("hot_hi", [P, E, T, P], BF16)
        hot_lo = sb("hot_lo", [P, E, T, B], BF16)
        value = sb("value", [P, E, T, COLS], BF16)
        weight = sb("weight", [P, 3, E, T])
        placed = sb("placed", [P, E, T, COLS, B], BF16)
        w_sum = sb("w_sum", [P, E, B])
        slot_parts = sb("slot_parts", [P, E, COLS, B])
        ps_count = psum("ps_count", [P, 512])
        ps_before = psum("ps_before", [P, 512])
        ps_slot = psum("ps_slot", [P, E, 512])
        tables = sem("tables")
        cs = sem("cs")
        logits_shifted, exped = sem("logits_shifted"), sem("exped")
        counted, count_ps = sem("counted"), sem("count_ps")
        flags_ready, prefix_ps = sem("flags_ready"), sem("prefix_ps")
        placed_ready, slot_ps = sem("placed_ready"), sem("slot_ps")
        block = ctx.enter_context(nc.Block())

        @block.gpsimd
        def _(pool):
            nc.gpsimd.iota(digit_i[:], pattern=[[1, RADIX]], base=0, channel_multiplier=0).then_inc(tables, 1)
            nc.gpsimd.iota(token_i[:], pattern=[[P, T]], base=0, channel_multiplier=1).then_inc(tables, 1)
            nc.gpsimd.iota(tile_i[:], pattern=[[1, T]], base=0, channel_multiplier=0).then_inc(tables, 1)
            nc.gpsimd.iota(row_i[:], pattern=[[0, T]], base=0, channel_multiplier=1).then_inc(tables, 1)
            nc.gpsimd.iota(hi_iota_i[:], pattern=[[1, P]], base=0, channel_multiplier=0).then_inc(tables, 1)
            nc.gpsimd.memset(restart[:], 1.0).then_inc(tables, 1)
            pool.wait_ge(tables, 6)
            nc.gpsimd.memset(restart[:, :, 0:1], 0.0).then_inc(tables, 1)
            nc.gpsimd.affine_select(out=before[:], in_=c["ones"][:], compare_op=ALU.is_gt, fill=0.0, base=0,
                                    pattern=[[1, P]], channel_multiplier=-1).then_inc(tables, 1)

        @block.scalar
        def _(act):
            act.wait_ge(logits_shifted, 1)
            nc.scalar.activation(expo[:], shifted[:], ACT.Exp).then_inc(exped, 1)

        @block.tensor
        def _(pe):
            with pe.Fori(0, ROUNDS) as r:
                pe.wait_ge(counted, r + 1)
                nc.tensor.matmul(ps_count[:, 0:E * RADIX], c["ones"][:], part_count[:].rearrange("p e j -> p (e j)"),
                                 start=True, stop=True).then_inc(count_ps, 1)
            pe.wait_ge(tables, 8)
            pe.wait_ge(flags_ready, 2)
            f = flags[:].rearrange("p f e t -> p (f e t)")
            nc.tensor.matmul(ps_before[:, 0:2 * E * T], before[:], f, start=True, stop=True)
            nc.tensor.matmul(ps_count[:, 0:2 * E * T], c["ones"][:], f, start=True, stop=True).then_inc(prefix_ps, 1)
            for e in range(E):
                pe.wait_ge(placed_ready, e + 1)
                for t_ in range(T):
                    mm = nc.tensor.matmul(ps_slot[:, e, 0:COLS * B], hot_hi[:, e, t_, :],
                                          placed[:, e, t_].rearrange("p c b -> p (c b)"),
                                          start=(t_ == 0), stop=(t_ == T - 1))
                mm.then_inc(slot_ps, 1)

        @block.vector
        def _(dve):
            steps = [0]

            def link(ins):
                steps[0] += 1
                ins.then_inc(cs, 1)
                dve.wait_ge(cs, steps[0])

            V = nc.vector

            def per_expert(ap):
                return ap.unsqueeze(2).broadcast_to([P, E, T])

            dve.wait_ge(tables, 8)
            for r in range(ROUNDS):
                link(V.tensor_scalar(digits[:, r, :], digit_i[:], DIGIT * (ROUNDS - 1 - r), None,
                                     ALU.logical_shift_left))
            link(V.tensor_copy(token[:], token_i[:]))
            link(V.tensor_copy(hi_iota[:], hi_iota_i[:]))
            link(V.tensor_copy(lo_iota[:], digit_i[:, 0:B]))
            for e in range(E):
                link(V.tensor_copy(value[:, e, :, 0], tile_i[:]))
                link(V.tensor_copy(value[:, e, :, 1], row_i[:]))

            link(V.memset(beats[:], 0.0))
            for e in range(E):
                for js, op in ((slice(0, e), ALU.is_ge), (slice(e + 1, E), ALU.is_gt)):
                    n = js.stop - js.start
                    if n:
                        link(V.tensor_tensor(beats[:, :, e, js], logits[:, :, js],
                                             logits[:, :, e:e + 1].broadcast_to([P, T, n]), op))
            link(V.tensor_reduce(rank[:], beats[:], AX, ALU.add))
            link(V.tensor_scalar(assigned[:], rank[:], 2.0, None, ALU.is_lt))
            link(V.tensor_reduce(best[:], logits[:], AX, ALU.max))
            V.tensor_tensor(shifted[:], logits[:], best[:].unsqueeze(2).broadcast_to([P, T, E]),
                            ALU.subtract).then_inc(logits_shifted, 1)
            dve.wait_ge(exped, 1)
            link(V.tensor_tensor(expo[:], expo[:], assigned[:], ALU.mult))
            link(V.tensor_reduce(total[:], expo[:], AX, ALU.add))
            link(V.reciprocal(inv[:], total[:]))
            link(V.tensor_tensor(prob[:], expo[:], inv[:].unsqueeze(2).broadcast_to([P, T, E]), ALU.mult))
            link(V.tensor_scalar(unassigned[:], assigned[:], 1.0, None, ALU.subtract))
            link(V.tensor_tensor(score[:].rearrange("p e t -> p t e"), prob[:], unassigned[:], ALU.add))
            link(V.memset(kth[:], 0.0))

            base = steps[0]
            with dve.Fori(0, ROUNDS) as r:
                V.tensor_tensor(cand[:].bitcast(I32), kth[:].bitcast(I32).unsqueeze(2).broadcast_to([P, E, RADIX]),
                                digits[:, bass.ds(r, 1), :].broadcast_to([P, E, RADIX]),
                                ALU.bitwise_or).then_inc(cs, 1)
                dve.wait_ge(cs, 4 * r + base + 1)
                V.tensor_tensor(at_least[:], score[:].unsqueeze(2).broadcast_to([P, E, RADIX, T]),
                                cand[:].unsqueeze(3).broadcast_to([P, E, RADIX, T]), ALU.is_ge).then_inc(cs, 1)
                dve.wait_ge(cs, 4 * r + base + 2)
                V.tensor_reduce(part_count[:], at_least[:], AX, ALU.add).then_inc(counted, 1)
                dve.wait_ge(count_ps, r + 1)
                V.scalar_tensor_tensor(out=kept[:], in0=ps_count[:, 0:E * RADIX].rearrange("p (e j) -> p e j", e=E),
                                       scalar=float(capacity), in1=cand[:], op0=ALU.is_ge,
                                       op1=ALU.mult).then_inc(cs, 1)
                dve.wait_ge(cs, 4 * r + base + 3)
                V.tensor_reduce(kth[:], kept[:], AX, ALU.max).then_inc(cs, 1)
                dve.wait_ge(cs, 4 * r + base + 4)
            steps[0] += 4 * ROUNDS

            for n, op in enumerate((ALU.is_gt, ALU.is_equal)):
                V.tensor_tensor(flags[:, n], score[:], per_expert(kth[:]), op).then_inc(flags_ready, 1)
            dve.wait_ge(prefix_ps, 1)
            flat = lambda ap: ap[:].rearrange("p f e t -> p (f e t)")
            link(V.tensor_tensor_scan(flat(running), restart[:].rearrange("p f t -> p (f t)"),
                                      ps_count[:, 0:2 * E * T], 0.0, ALU.mult, ALU.add))
            link(V.tensor_tensor(flat(earlier), flat(running), ps_count[:, 0:2 * E * T], ALU.subtract))
            link(V.tensor_tensor(flat(earlier), flat(earlier), ps_before[:, 0:2 * E * T], ALU.add))
            link(V.tensor_scalar(wanted[:], running[:, 0, :, T - 1], -1.0, float(capacity), ALU.mult, ALU.add))
            link(V.tensor_tensor(ties[:], wanted[:], running[:, 1, :, T - 1], ALU.min))
            link(V.tensor_tensor(chosen_n[:], ties[:], running[:, 0, :, T - 1], ALU.add))
            link(V.tensor_tensor(fits[:], earlier[:, 1], per_expert(wanted[:]), ALU.is_lt))
            link(V.tensor_tensor(fits[:], fits[:], flags[:, 1], ALU.mult))
            link(V.tensor_tensor(chosen[:], flags[:, 0], fits[:], ALU.add))
            link(V.tensor_tensor(taken[:], earlier[:, 1], per_expert(wanted[:]), ALU.min))
            link(V.tensor_tensor(taken[:], taken[:], earlier[:, 0], ALU.add))
            link(V.tensor_tensor(other[:], token[:].unsqueeze(1).broadcast_to([P, E, T]), taken[:], ALU.subtract))
            link(V.tensor_tensor(other[:], other[:], per_expert(chosen_n[:]), ALU.add))
            link(V.tensor_tensor(slot[:], taken[:], other[:], ALU.subtract))
            link(V.tensor_tensor(slot[:], slot[:], chosen[:], ALU.mult))
            link(V.tensor_tensor(slot_i[:], slot[:], other[:], ALU.add))
            link(V.tensor_scalar(slot_hi_i[:], slot_i[:], DIGIT, None, ALU.logical_shift_right))
            link(V.tensor_scalar(slot_lo_i[:], slot_i[:], RADIX - 1, None, ALU.bitwise_and))
            link(V.tensor_copy(slot_hi[:], slot_hi_i[:]))
            link(V.tensor_copy(slot_lo[:], slot_lo_i[:]))
            link(V.tensor_tensor(weight[:, 0], chosen[:], prob[:].rearrange("p t e -> p e t"), ALU.mult))
            for n in range(3):
                link(V.tensor_copy(value[:, :, :, 2 + n], weight[:, n]))
                if n < 2:
                    link(V.tensor_tensor(weight[:, n + 1], weight[:, n], value[:, :, :, 2 + n], ALU.subtract))
            link(V.tensor_tensor(hot_lo[:], slot_lo[:].unsqueeze(3).broadcast_to([P, E, T, B]),
                                 lo_iota[:].unsqueeze(1).unsqueeze(1).broadcast_to([P, E, T, B]), ALU.is_equal))
            for e in range(E):
                link(V.tensor_tensor(placed[:, e], hot_lo[:, e].unsqueeze(2).broadcast_to([P, T, COLS, B]),
                                     value[:, e].unsqueeze(3).broadcast_to([P, T, COLS, B]), ALU.mult))
                V.tensor_tensor(hot_hi[:, e], slot_hi[:, e].unsqueeze(2).broadcast_to([P, T, P]),
                                hi_iota[:].unsqueeze(1).broadcast_to([P, T, P]), ALU.is_equal).then_inc(placed_ready, 1)
            for e in range(E):
                dve.wait_ge(slot_ps, e + 1)
                link(V.tensor_copy(slot_parts[:, e].rearrange("p c b -> p (c b)"), ps_slot[:, e, 0:COLS * B]))
            link(V.scalar_tensor_tensor(out=slot_token[:], in0=slot_parts[:, :, 0, :], scalar=float(P),
                                        in1=slot_parts[:, :, 1, :], op0=ALU.mult, op1=ALU.add))
            link(V.tensor_tensor(w_sum[:], slot_parts[:, :, 2, :], slot_parts[:, :, 3, :], ALU.add))
            link(V.tensor_tensor(w_sum[:], w_sum[:], slot_parts[:, :, 4, :], ALU.add))
            link(V.tensor_scalar(slot_weight[:], w_sum[:], c["gates"][:, 3:4], None, ALU.mult))


def experts(nc, c, w1, w2, slot_token, slot_weight, xhat_d, out):
    E, D, H = w1.shape
    K = D // P
    HT = H // P
    SLOTS = slot_token.shape[2]
    I = SLOTS // 2
    GROUP = 4
    RING = 4
    AHEAD = 2
    rows_out = row_major(out)
    w1_t = w1.rearrange("e (k p) h -> e p k h", p=P)
    w2_t = w2.rearrange("e (t p) d -> e p t d", p=P)
    with ExitStack() as ctx:
        def sb(name, shape, dt=F32):
            return ctx.enter_context(nc.sbuf_tensor(name, shape, dt))

        def sem(name):
            return ctx.enter_context(nc.semaphore(name))

        w1_raw = sb("w1_raw", [P, 2, K, GROUP * P])
        w2_raw = sb("w2_raw", [P, 2, GROUP, D])
        w1_s = [sb("w1_hi", [P, RING, K, P], F32R), sb("w1_lo", [P, RING, K, P], F32R)]
        w2_s = [sb("w2_hi", [P, RING, D], F32R), sb("w2_lo", [P, RING, D], F32R)]
        rows = sb("rows", [P, I, D])
        rows_t = [sb("rows_t_hi", [P, 2, K, D], F32R), sb("rows_t_lo", [P, 2, K, D], F32R)]
        hidden = sb("hidden", [P, 2, D])
        hid = [sb("hidden_hi", [P, 2, D], F32R), sb("hidden_lo", [P, 2, D], F32R)]
        scaled = sb("scaled", [P, I, D])
        gather_index = sb("gather_index", [P, I], U32)
        scatter_index = sb("scatter_index", [P, I], U32)
        factor = sb("factor", [P, I])
        ps_y = ctx.enter_context(nc.psum_tensor("ps_y", [P, I, 512], F32))
        ps_h = ctx.enter_context(nc.psum_tensor("ps_h", [P, 2, 512], F32))
        ps_t = ctx.enter_context(nc.psum_tensor("ps_t", [P, 2, I, P], F32))

        w_loaded = [sem(f"w_loaded{n}") for n in range(2)]
        w_hi, w_lo = sem("w_hi"), sem("w_lo")
        index_ready = sem("index_ready")
        factor_ready = sem("factor_ready")
        gathered = [sem(f"gathered{i}") for i in range(I)]
        rows_ps = sem("rows_ps")
        rows_hi, rows_lo = sem("rows_hi"), sem("rows_lo")
        h_ps, gelu_done = sem("h_ps"), sem("gelu_done")
        h_hi, h_lo = sem("h_hi"), sem("h_lo")
        y_done = sem("y_done")
        y_out = sem("y_out")
        scattered = sem("scattered")
        block = ctx.enter_context(nc.Block())
        STEPS = 2 * HT

        def all_experts(eng, body):
            body(0, True)
            with eng.Fori(1, E - 1) as e:
                body(e, True)
            body(E - 1, False)

        def first(e, half):
            return isinstance(e, int) and e == 0 and half == 0

        @block.sync
        def _(sp):
            def body(e, more):
                for half in range(2):
                    for q in range(HT // GROUP):
                        n, par = 8 * e + 4 * half + q, q % 2
                        wait(sp, w_lo, 2 * GROUP * (n - 1))
                        cols = slice(GROUP * P * q, GROUP * P * (q + 1))
                        sp.dma_start(w1_raw[:, par], w1_t[bass.ds(e, 1), :, :, cols].rearrange("o p k h -> (o p) k h")
                                     ).then_inc(w_loaded[par], 16)
                        sp.dma_start(w2_raw[:, par], w2_t[bass.ds(e, 1), :, GROUP * q:GROUP * q + GROUP, :]
                                     .rearrange("o p t d -> (o p) t d")).then_inc(w_loaded[par], 16)

            all_experts(sp, body)

        def gather_wait(e, half):
            n = 2 * e + half
            nc.gpsimd.wait_ge(index_ready, n + 1)
            wait(nc.gpsimd, rows_ps, K * n)

        def gather():
            for i in range(I):
                nc.gpsimd.indirect_dma_start(
                    out=rows[:, i, :], out_offset=None, in_=xhat_d,
                    in_offset=bass.IndirectOffsetOnAxis(ap=gather_index[:, i:i + 1], axis=0)
                ).then_inc(gathered[i], 16)

        @block.gpsimd
        def _(pool):
            def split(e, half, t):
                g, par, r = STEPS * e + HT * half + t, (t // GROUP) % 2, t % RING
                j = t % GROUP
                pool.wait_ge(w_hi, 2 * g + 1)
                nc.gpsimd.tensor_tensor(w1_s[1][:, r], w1_raw[:, par, :, P * j:P * j + P], w1_s[0][:, r],
                                        ALU.subtract).then_inc(w_lo, 1)
                pool.wait_ge(w_hi, 2 * g + 2)
                nc.gpsimd.tensor_tensor(w2_s[1][:, r], w2_raw[:, par, j, :], w2_s[0][:, r],
                                        ALU.subtract).then_inc(w_lo, 1)

            def scatter_wait(e, half, i):
                n = I * (2 * e + half) + i
                pool.wait_ge(y_out, n + 1)
                wait(pool, scattered, 16 * n)

            def scatter(i):
                nc.gpsimd.indirect_dma_start(
                    out=rows_out, out_offset=bass.IndirectOffsetOnAxis(
                        ap=scatter_index[:, i:i + 1], axis=0),
                    in_=scaled[:, i, :], in_offset=None, compute_op=ALU.add).then_inc(scattered, 16)

            gather_wait(0, 0)
            gather()
            for t in range(AHEAD):
                split(0, 0, t)

            def body(e, more):
                for half in range(2):
                    for t in range(HT):
                        i = (t - 3) // 2 if t in range(3, 3 + 2 * I, 2) and not first(e, half) else None
                        gathers = t == 1 and (half == 0 or more)
                        if i is not None:
                            scatter_wait(e if half else e - 1, 1 - half, i)
                        if gathers:
                            gather_wait(e + half, 1 - half)
                        if t + AHEAD < HT:
                            split(e, half, t + AHEAD)
                        elif half == 0:
                            split(e, 1, t + AHEAD - HT)
                        elif more:
                            split(e + 1, 0, t + AHEAD - HT)
                        if i is not None:
                            scatter(i)
                        if gathers:
                            gather()

            all_experts(pool, body)
            for i in range(I):
                scatter_wait(E - 1, 1, i)
                scatter(i)
            pool.wait_ge(scattered, 16 * 2 * E * I)

        @block.scalar
        def _(act):
            def split(e, half, t):
                g, par, r = STEPS * e + HT * half + t, (t // GROUP) % 2, t % RING
                j = t % GROUP
                act.wait_ge(w_loaded[par], 32 * (4 * e + 2 * half + t // (2 * GROUP) + 1))
                wait(act, y_done, I * (g - RING + 1))
                nc.scalar.activation(w1_s[0][:, r], w1_raw[:, par, :, P * j:P * j + P], ACT.Copy).then_inc(w_hi, 1)
                nc.scalar.activation(w2_s[0][:, r], w2_raw[:, par, j, :], ACT.Copy).then_inc(w_hi, 1)

            def rows_part(e, half, k):
                n = K * (2 * e + half) + k
                act.wait_ge(rows_ps, n + 1)
                nc.scalar.activation(rows_t[0][:, half, k, :], ps_t[:, k % 2].rearrange("p i s -> p (i s)"),
                                     ACT.Copy).then_inc(rows_hi, 1)

            def gelu(e, half, t):
                g = STEPS * e + HT * half + t
                act.wait_ge(h_ps, g + 1)
                wait(act, h_lo, g - 1)
                nc.scalar.activation(hidden[:, t % 2, :], ps_h[:, t % 2, :], ACT.Gelu).then_inc(gelu_done, 1)

            for t in range(AHEAD):
                split(0, 0, t)
            for k in range(K):
                rows_part(0, 0, k)

            def body(e, more):
                for half in range(2):
                    for t in range(HT):
                        gelu(e, half, t)
                        if t + AHEAD < HT:
                            split(e, half, t + AHEAD)
                        elif half == 0:
                            split(e, 1, t + AHEAD - HT)
                        elif more:
                            split(e + 1, 0, t + AHEAD - HT)
                        if 8 <= t < 8 + K:
                            if half == 0:
                                rows_part(e, 1, t - 8)
                            elif more:
                                rows_part(e + 1, 0, t - 8)

            all_experts(act, body)

        @block.vector
        def _(dve):
            def rows_part(e, half, k):
                n = K * (2 * e + half) + k
                dve.wait_ge(rows_hi, n + 1)
                nc.vector.tensor_tensor(rows_t[1][:, half, k, :], ps_t[:, k % 2].rearrange("p i s -> p (i s)"),
                                        rows_t[0][:, half, k, :], ALU.subtract).then_inc(rows_lo, 1)

            def outputs(e, half):
                blk = 2 * e + half
                wait(dve, scattered, 16 * I * blk)
                cols = slice(I * half, I * half + I)
                nc.vector.tensor_copy(scatter_index[:].unsqueeze(1), slot_token[:, bass.ds(e, 1), cols]
                                      ).then_inc(factor_ready, 1)
                nc.vector.tensor_copy(factor[:].unsqueeze(1), slot_weight[:, bass.ds(e, 1), cols]
                                      ).then_inc(factor_ready, 1)
                dve.wait_ge(factor_ready, 2 * blk + 2)
                for i in range(I):
                    dve.wait_ge(y_done, I * (HT * (blk + 1) - 1) + i + 1)
                    nc.vector.tensor_scalar(scaled[:, i, :], ps_y[:, i, :], factor[:, i:i + 1], None,
                                            ALU.mult).then_inc(y_out, 1)

            def hidden_parts(e, half, t):
                g = STEPS * e + HT * half + t
                dve.wait_ge(gelu_done, g + 1)
                wait(dve, y_done, I * (g - 1))
                nc.vector.tensor_copy(hid[0][:, t % 2, :], hidden[:, t % 2, :]).then_inc(h_hi, 1)
                dve.wait_ge(h_hi, g + 1)
                nc.vector.tensor_tensor(hid[1][:, t % 2, :], hidden[:, t % 2, :], hid[0][:, t % 2, :],
                                        ALU.subtract).then_inc(h_lo, 1)

            def pick(e, half):
                n = 2 * e + half
                wait(dve, rows_ps, K * n)
                nc.vector.tensor_copy(gather_index[:].unsqueeze(1),
                                      slot_token[:, bass.ds(e, 1), I * half:I * half + I]).then_inc(index_ready, 1)

            pick(0, 0)
            for k in range(K):
                rows_part(0, 0, k)

            def body(e, more):
                for half in range(2):
                    if half == 1:
                        outputs(e, 0)
                    elif not first(e, half):
                        outputs(e - 1, 1)
                    for t in range(HT):
                        if t == 0:
                            if half == 0:
                                pick(e, 1)
                            elif more:
                                pick(e + 1, 0)
                        hidden_parts(e, half, t)
                        if 8 <= t < 8 + K:
                            if half == 0:
                                rows_part(e, 1, t - 8)
                            elif more:
                                rows_part(e + 1, 0, t - 8)

            all_experts(dve, body)
            outputs(E - 1, 1)

        @block.tensor
        def _(pe):
            def transposes(e, half, k):
                n = K * (2 * e + half) + k
                if k == 0:
                    for i in range(I):
                        pe.wait_ge(gathered[i], 16 * (2 * e + half + 1))
                wait(pe, rows_lo, n - 1)
                for i in range(I):
                    mm = nc.tensor.transpose(ps_t[:, k % 2, i, :], rows[:, i, P * k:P * k + P], c["ident"][:])
                mm.then_inc(rows_ps, 1)

            def hidden_product(e, half, t):
                g, r = STEPS * e + HT * half + t, t % RING
                if t == 0:
                    pe.wait_ge(rows_lo, K * (2 * e + half) + K)
                pe.wait_ge(w_lo, 2 * g + 2)
                wait(pe, gelu_done, g - 1)
                for k in range(K):
                    for a, b in ((0, 0), (0, 1), (1, 0)):
                        mm = nc.tensor.matmul(ps_h[:, t % 2, :], w1_s[a][:, r, k, :], rows_t[b][:, half, k, :],
                                              start=(k == 0 and a == b), stop=(k == K - 1 and a == 1))
                mm.then_inc(h_ps, 1)

            def output_product(e, half, t):
                g, r = STEPS * e + HT * half + t, t % RING
                pe.wait_ge(h_lo, g + 1)
                for i in range(I):
                    n = I * (2 * e + half) + i
                    if t == 0:
                        wait(pe, y_out, n - I + 1)
                    tok = slice(P * i, P * i + P)
                    for a, b in ((0, 0), (0, 1), (1, 0)):
                        mm = nc.tensor.matmul(ps_y[:, i, :], hid[a][:, t % 2, tok], w2_s[b][:, r],
                                              start=(t == 0 and a == b), stop=(t == HT - 1 and a == 1))
                    mm.then_inc(y_done, 1)

            for k in range(K):
                transposes(0, 0, k)

            def body(e, more):
                for half in range(2):
                    for t in range(HT):
                        hidden_product(e, half, t)
                        if t > 0:
                            output_product(e, half, t - 1)
                        if 8 <= t < 8 + K:
                            if half == 0:
                                transposes(e, 1, t - 8)
                            elif more:
                                transposes(e + 1, 0, t - 8)
                    output_product(e, half, HT - 1)

            all_experts(pe, body)


def program(nc, t, out):
    with ExitStack() as ctx:
        def sb(name, shape, dt=F32):
            return ctx.enter_context(nc.sbuf_tensor(name, shape, dt))

        B, S, D = t["x"].shape
        TOK, K = B * S, D // P
        E = t["L1_ffn_W1"].shape[0]
        CAPACITY = TOK // E
        logits = sb("logits", [P, TOK // P, E])
        slot_token = sb("slot_token", [P, E, CAPACITY // P], U32)
        slot_weight = sb("slot_weight", [P, E, CAPACITY // P])
        xhat_d = nc.dram_tensor("xhat_d", (TOK, D), F32).ap()
        c = build_constants(nc, ctx, t["g_xattn"], t["g_ffn"])
        with ExitStack() as xctx:
            x_res = xctx.enter_context(nc.sbuf_tensor("x_res", [P, TOK // P, D], F32))
            column_attention(nc, c, t["x"], t["ctx_2048"], xhat_d, x_res)
            w = {n + part: xctx.enter_context(nc.sbuf_tensor("w_" + n + part, [P, K, cols], F32R))
                 for n, cols in (("up", D), ("down", D), ("expert", D), ("gate", 8)) for part in ("_hi", "_lo")}
            w["route"] = xctx.enter_context(nc.sbuf_tensor("w_route", [P, K, E], F32))
            w["route_bias"] = xctx.enter_context(nc.sbuf_tensor("w_route_bias", [P, E], F32))
            split_weights(nc, c, t, w)
            dense_and_memory(nc, c, w, t, x_res, xhat_d, out, logits)
        route(nc, c, logits, CAPACITY, slot_token, slot_weight)
        experts(nc, c, t["L1_ffn_W1"], t["L1_ffn_W2"], slot_token, slot_weight, xhat_d, out)


_INS = ["x", "ctx_2048", "mask_BxS2_bk0", "g_xattn", "g_ffn", "L0_ffn_W_up", "L0_ffn_W_down", "L0_ffn_W_gate",
        "L0_ffn_W_expert", "L1_ffn_Wg", "L1_ffn_bg", "L1_ffn_W1", "L1_ffn_W2"]


def kernel(**inputs):
    import numpy as _np
    import concourse.bacc as _bacc
    from concourse import mybir as _mybir
    from concourse.bass_utils import run_bass_kernel_spmd as _run

    nc = _bacc.Bacc("TRN2", target_bir_lowering=False, num_devices=1)
    arrays, tensors = {}, {}
    for name in _INS:
        a = _np.ascontiguousarray(inputs[name])
        arrays[f"in_{name}"] = a
        tensors[name] = nc.dram_tensor(f"in_{name}", a.shape, _mybir.dt.from_np(a.dtype), kind="ExternalInput").ap()
    out = nc.dram_tensor("out_x", (16, 256, 512), _mybir.dt.float32, kind="ExternalOutput").ap()
    program(nc, tensors, out)
    r = _run(nc, [arrays], core_ids=[0])
    return r.results[0]["out_x"]
```

```python
from contextlib import ExitStack

import numpy as np

import concourse.bass as bass
from concourse import mybir

P = 128
F32 = mybir.dt.float32
F32R = mybir.dt.float32r
I32 = mybir.dt.int32
U32 = mybir.dt.uint32
U8 = mybir.dt.uint8
ALU = mybir.AluOpType
ACT = mybir.ActivationFunctionType
AX = mybir.AxisListType.X
BF16 = mybir.dt.bfloat16
EPS = 1e-5


def wait(eng, sem, value):
    if isinstance(value, int) and value <= 0:
        return
    eng.wait_ge(sem, value)


RSQRT_STEPS = 12


def inverse_sqrt(nc, dve, y, var, tmp, step, base):
    rsqrt_guess(nc, dve, y, var, tmp, step, base)
    for n in range(3):
        rsqrt_newton(nc, dve, y, tmp, step, base, n)


def rsqrt_guess(nc, dve, y, var, tmp, step, base):
    nc.vector.tensor_scalar(tmp[0], var, EPS, None, ALU.add).then_inc(step, 1)
    dve.wait_ge(step, base + 1)
    nc.vector.tensor_scalar(tmp[1].bitcast(I32), tmp[0].bitcast(I32), 1, None,
                            ALU.logical_shift_right).then_inc(step, 1)
    dve.wait_ge(step, base + 2)
    nc.vector.tensor_scalar(y.bitcast(I32), tmp[1].bitcast(I32), -1.0, float(0x5F3759DF),
                            ALU.mult, ALU.add).then_inc(step, 1)


def rsqrt_newton(nc, dve, y, tmp, step, base, n):
    done = base + 3 + 3 * n
    dve.wait_ge(step, done)
    nc.vector.tensor_tensor(tmp[1], y, y, ALU.mult).then_inc(step, 1)
    dve.wait_ge(step, done + 1)
    nc.vector.scalar_tensor_tensor(out=tmp[2], in0=tmp[1], scalar=-0.5, in1=tmp[0],
                                   op0=ALU.mult, op1=ALU.mult).then_inc(step, 1)
    dve.wait_ge(step, done + 2)
    nc.vector.scalar_tensor_tensor(out=y, in0=tmp[2], scalar=1.5, in1=y,
                                   op0=ALU.add, op1=ALU.mult).then_inc(step, 1)


def row_major(t):
    return t.rearrange("b s d -> (b s) d")


DIGIT = 3
RADIX = 1 << DIGIT
ROUNDS = 10


def build_constants(nc, ctx, g_xattn, g_ffn, T, E):
    def sb(name, shape, dt):
        return ctx.enter_context(nc.sbuf_tensor(name, shape, dt))

    c = {
        "ident": sb("ident", [P, P], F32),
        "ones": sb("ones", [P, P], F32),
        "minus_ones": sb("minus_ones", [P, P], F32R),
        "gates": sb("gates", [P, 4], F32),
        "gates_raw": sb("gates_raw", [P, 4], F32),
        "digits": sb("digits", [P, ROUNDS, RADIX], I32),
        "token": sb("token", [P, T], F32),
        "column": sb("column", [P, P], BF16),
        "value": sb("value", [P, E, T, 5], BF16),
    }
    with nc.sbuf_tensor("token_i", [P, T], I32) as token_i, nc.sbuf_tensor("column_i", [P, P], I32) as column_i, \
            nc.sbuf_tensor("tile_i", [P, T], I32) as tile_i, nc.sbuf_tensor("row_i", [P, T], I32) as row_i, \
            nc.semaphore("gates_loaded") as gates_loaded, nc.semaphore("cleared") as cleared, \
            nc.semaphore("const_step") as const_step, nc.semaphore("iotas") as iotas, \
            nc.semaphore("tables") as tables, nc.Block() as block:
        @block.sync
        def _(sp):
            for n, g in enumerate((g_xattn, g_ffn)):
                sp.dma_start(c["gates_raw"][:, 2 * n:2 * n + 2],
                             bass.AP(tensor=g.tensor, offset=0, ap=[[0, P], [1, 2]])).then_inc(gates_loaded, 16)
            sp.wait_ge(gates_loaded, 32)

        @block.scalar
        def _(act):
            act.wait_ge(gates_loaded, 32)
            nc.scalar.activation(c["gates"][:], c["gates_raw"][:], ACT.Tanh).then_inc(const_step, 1)
            act.wait_ge(const_step, 1)

        @block.gpsimd
        def _(pool):
            nc.gpsimd.memset(c["ident"][:], 0.0).then_inc(cleared, 1)
            nc.gpsimd.memset(c["ones"][:], 1.0).then_inc(cleared, 1)
            pool.wait_ge(cleared, 2)
            nc.gpsimd.affine_select(out=c["ident"][:], in_=c["ident"][:], compare_op=ALU.not_equal, fill=1.0,
                                    base=0, pattern=[[-1, P]], channel_multiplier=1).then_inc(cleared, 1)
            nc.gpsimd.iota(column_i[:], pattern=[[1, P]], base=0, channel_multiplier=0).then_inc(iotas, 1)
            nc.gpsimd.iota(token_i[:], pattern=[[P, T]], base=0, channel_multiplier=1).then_inc(iotas, 1)
            nc.gpsimd.iota(tile_i[:], pattern=[[1, T]], base=0, channel_multiplier=0).then_inc(iotas, 1)
            nc.gpsimd.iota(row_i[:], pattern=[[0, T]], base=0, channel_multiplier=1).then_inc(iotas, 1)
            pool.wait_ge(cleared, 3)
            pool.wait_ge(iotas, 4)

        @block.vector
        def _(dve):
            dve.wait_ge(cleared, 2)
            nc.vector.tensor_scalar(c["minus_ones"][:], c["ones"][:], -1.0, None, ALU.mult).then_inc(tables, 1)
            dve.wait_ge(iotas, 4)
            for n in range(ROUNDS):
                nc.vector.tensor_scalar(c["digits"][:, n, :], column_i[:, 0:RADIX], DIGIT * (ROUNDS - 1 - n), None,
                                        ALU.logical_shift_left).then_inc(tables, 1)
            nc.vector.tensor_copy(c["token"][:], token_i[:]).then_inc(tables, 1)
            nc.vector.tensor_copy(c["column"][:], column_i[:]).then_inc(tables, 1)
            for e in range(E):
                nc.vector.tensor_copy(c["value"][:, e, :, 0], tile_i[:]).then_inc(tables, 1)
                nc.vector.tensor_copy(c["value"][:, e, :, 1], row_i[:]).then_inc(tables, 1)
            dve.wait_ge(tables, ROUNDS + 3 + 2 * E)
    return c


def column_attention(nc, c, x_in, ctx_in, xhat_d, x_res, weights, raw, raw_loaded):
    D = x_in.shape[2]
    TOK = x_in.shape[0] * x_in.shape[1]
    TILES = TOK // P
    BATCHES = TILES // 2
    HEADS = 4
    ROWS = P // HEADS
    STACK = 3 * ROWS
    NT = D // P
    SCALE = float(np.float32(1.0) / np.sqrt(np.float32(ROWS)))
    NORM_STEPS = 4 + RSQRT_STEPS
    ORDER = (0, 2, 1, 3)
    x_t = row_major(x_in).rearrange("(t p) d -> p t d", p=P)
    ctx_t = row_major(ctx_in).rearrange("(t p) d -> t p d", p=P)
    ctx_h = row_major(ctx_in).rearrange("(t h r) d -> t r h d", h=HEADS, r=ROWS)
    xhat_t = xhat_d.rearrange("(t p) d -> t p d", p=P)
    xhat_h = xhat_d.rearrange("(t h r) d -> t r h d", h=HEADS, r=ROWS)
    IDENT4 = c["ident"][:].unsqueeze(1).broadcast_to([P, NT, P])

    with ExitStack() as ctx:
        def sb(name, shape, dt=F32):
            return ctx.enter_context(nc.sbuf_tensor(name, shape, dt))

        def sem(name):
            return ctx.enter_context(nc.semaphore(name))

        ctx_nat = sb("ctx_nat", [P, 2, D])
        k_raw = sb("k_raw", [STACK, 2, HEADS, D])
        q_raw = sb("q_raw", [STACK, 2, HEADS, D])
        k_stack = sb("k_stack", [STACK, 2, HEADS, D], F32R)
        q_stack = sb("q_stack", [STACK, 2, HEADS, D], F32R)
        v_ones = sb("v_ones", [P, 2, NT, HEADS, 2 * ROWS])
        probs = sb("probs", [P, 2, NT, D])
        maxima = sb("maxima", [P, 2, NT])
        max_diag = sb("max_diag", [P, 2, NT, P], F32R)
        xhat = sb("xhat", [P, 2, D])
        stats = sb("stats", [P, 2, 6])
        mean_var = sb("mean_var", [P, 2, 2])
        rstd = sb("rstd", [P, 2])
        fence = sb("fence", [P, 1])
        tmp3 = sb("tmp3", [P, 3, 2])
        outputs = sb("outputs", [P, 2, D])
        denominators = sb("denominators", [P, 2, D])
        recip = sb("recip", [P, D])
        gated = sb("gated", [P, 2, D])
        ps_s = ctx.enter_context(nc.psum_tensor("ps_s", [P, NT, D], F32))
        ps_st = [ctx.enter_context(nc.psum_tensor(f"ps_st{n}", [P, D], F32)) for n in range(2)]
        ps_od = [ctx.enter_context(nc.psum_tensor(f"ps_od{n}", [P, D], F32)) for n in range(2)]
        ps_v = ps_s[:, NT - 1, :].rearrange("p (n r) -> p n r", n=NT)

        x_loaded = sem("x_loaded")
        ctx_loaded = [sem(f"ctx_loaded{u}") for u in range(2)]
        k_loaded = [sem(f"k_loaded{u}") for u in range(2)]
        q_loaded = [sem(f"q_loaded{u}") for u in range(2)]
        xhat_stored = sem("xhat_stored")
        ln_step = sem("ln_step")
        xhat_ready = sem("xhat_ready")
        hi_ready = sem("hi_ready")
        lo_ready = sem("lo_ready")
        ones_ready = sem("ones_ready")
        v_transposed = sem("v_transposed")
        v_ready = sem("v_ready")
        s_done = sem("s_done")
        reduced = sem("reduced")
        diag_ready = sem("diag_ready")
        st_done = sem("st_done")
        exp_done = sem("exp_done")
        pv_done = sem("pv_done")
        evacuated = sem("evacuated")
        recip_done = sem("recip_done")
        gated_done = sem("gated_done")
        x_added = sem("x_added")

        block = ctx.enter_context(nc.Block())

        def batches(eng, body):
            body(0)
            body(1)
            with eng.Fori(2, BATCHES - 1) as i:
                body(i)
            body(BATCHES - 1)

        def head_after_next(i, u, g):
            return (i, u, g + 2) if g < 2 else (i + u, 1 - u, g - 2)

        def is_last(i):
            return isinstance(i, int) and i == BATCHES - 1

        @block.sync
        def _(sp):
            sp.dma_start(x_res[:, 0:2, :], x_t[:, 0:2, :]).then_inc(x_loaded, 16)

            def body(i):
                sp.wait_ge(x_loaded, 16 * i + 16)
                if not is_last(i):
                    sp.dma_start(x_res[:, bass.ds(2 * i + 2, 2), :],
                                 x_t[:, bass.ds(2 * i + 2, 2), :]).then_inc(x_loaded, 16)
                for u in range(2):
                    t = 2 * i + u
                    wait(sp, lo_ready, 8 * t - 8)
                    for r in range(3):
                        sp.dma_start(k_raw[ROWS * r:ROWS * r + ROWS, u, :, :],
                                     ctx_h[bass.ds(t, 1)].rearrange("o r h d -> (o r) h d")).then_inc(k_loaded[u], 16)
                    wait(sp, v_transposed, t - 1)
                    sp.dma_start(ctx_nat[:, u, :],
                                 ctx_t[bass.ds(t, 1)].rearrange("o p d -> (o p) d")).then_inc(ctx_loaded[u], 16)
                    sp.wait_ge(xhat_ready, t + 1)
                    sp.dma_start(xhat_t[bass.ds(t, 1)].rearrange("o p d -> (o p) d"),
                                 xhat[:, u, :]).then_inc(xhat_stored, 16)
                    sp.wait_ge(xhat_stored, 16 * t + 16)
                    for r in range(3):
                        sp.dma_start(q_raw[ROWS * r:ROWS * r + ROWS, u, :, :],
                                     xhat_h[bass.ds(t, 1)].rearrange("o r h d -> (o r) h d")).then_inc(q_loaded[u], 16)

            batches(sp, body)
            for n in raw:
                sp.dma_start(raw[n][:], weights[n].rearrange("(k p) n -> p k n", p=P)).then_inc(raw_loaded[n], 16)

        @block.gpsimd
        def _(pool):
            nc.gpsimd.memset(v_ones[:], 1.0).then_inc(ones_ready, 1)

            def split(i, u, g, prologue=False):
                t = 2 * i + u
                h, n = ORDER[g], 4 * t + g
                mid, low = slice(ROWS, 2 * ROWS), slice(2 * ROWS, STACK)
                if prologue:
                    pool.wait_ge(ones_ready, 1)
                    wait(pool, lo_ready, 2 * n)
                    if g == 2:
                        pool.wait_ge(diag_ready, 1)
                else:
                    pool.wait_ge(diag_ready, n - 2)
                    if g == 0:
                        wait(pool, x_added, t - 2)
                pool.wait_ge(hi_ready, 2 * n + 1)
                nc.gpsimd.tensor_tensor(k_stack[mid, u, h, :], k_raw[mid, u, h, :], k_stack[mid, u, h, :],
                                        ALU.subtract).then_inc(lo_ready, 1)
                pool.wait_ge(hi_ready, 2 * n + 2)
                pool.wait_ge(lo_ready, 2 * n + 1)
                nc.gpsimd.tensor_tensor(q_stack[low, u, h, :], q_raw[low, u, h, :], q_stack[low, u, h, :],
                                        ALU.subtract).then_inc(lo_ready, 1)

            def diag(i, u, g, splits):
                n = 4 * (2 * i + u) + g
                pool.wait_ge(reduced, 2 * n + 2)
                pool.wait_ge(lo_ready, 2 * splits)
                wait(pool, st_done, 4 * n - 4)
                nc.gpsimd.tensor_tensor(
                    max_diag[:, g % 2], IDENT4,
                    maxima[:, g % 2, :].unsqueeze(2).broadcast_to([P, NT, P]), ALU.mult).then_inc(diag_ready, 1)

            def add(i, u, splits):
                t = 2 * i + u
                pool.wait_ge(lo_ready, 2 * splits)
                pool.wait_ge(gated_done, t + 1)
                xt = x_res[:, bass.ds(t, 1), :].rearrange("p o d -> p (o d)")
                nc.gpsimd.tensor_tensor(xt, gated[:, u, :], xt, ALU.add).then_inc(x_added, 1)

            for g in range(HEADS):
                split(0, 0, g, prologue=True)
                if g == 1:
                    diag(0, 0, 0, 2)

            def body(i):
                for u in range(2):
                    for g in range(HEADS):
                        last_tile = is_last(i) and u == 1
                        n_next = 4 * (2 * i + u + 1) + g
                        splits = 4 * TILES if last_tile else n_next
                        if g < 3:
                            diag(i, u, g + 1, splits)
                        elif not last_tile:
                            diag(i + u, 1 - u, 0, splits)
                        if not last_tile:
                            split(i + u, 1 - u, g)
                        if g == 3:
                            splits = 4 * TILES if last_tile else n_next + 1
                            if u == 1:
                                add(i, 0, splits)
                            elif not (isinstance(i, int) and i == 0):
                                add(i - 1, 1, splits)

            batches(pool, body)
            add(BATCHES - 1, 1, 4 * TILES)

        @block.scalar
        def _(act):
            def k_hi(i, u, g):
                h, t = ORDER[g], 2 * i + u
                act.wait_ge(k_loaded[u], 48 * i + 48)
                wait(act, st_done, 16 * t + 4 * g - 28)
                nc.scalar.activation(k_stack[:, u, h, :], k_raw[:, u, h, :], ACT.Copy).then_inc(hi_ready, 1)

            def q_hi(i, u, g):
                h = ORDER[g]
                act.wait_ge(q_loaded[u], 48 * i + 48)
                nc.scalar.activation(q_stack[:, u, h, :], q_raw[:, u, h, :], ACT.Copy).then_inc(hi_ready, 1)

            def exps(i, u, g, k):
                n = 4 * (2 * i + u) + g
                act.wait_ge(st_done, 4 * n + k + 1)
                wait(act, pv_done, 4 * n + k - 7)
                nc.scalar.activation(probs[:, g % 2, k, :], ps_st[k % 2][:, :], ACT.Exp,
                                     scale=SCALE).then_inc(exp_done, 1)

            def evacuate(i, u, h):
                t, bank = 2 * i + u, h % 2
                act.wait_ge(pv_done, 8 * (2 * t + bank) + 8)
                wait(act, gated_done, t - 1)
                own, other = 32 * h, 32 * (h ^ 1)
                nc.scalar.activation(outputs[own:own + 32, u, :], ps_od[bank][own:own + 32, :],
                                     ACT.Copy).then_inc(evacuated, 1)
                nc.scalar.activation(denominators[own:own + 32, u, :], ps_od[bank][other:other + 32, :],
                                     ACT.Copy).then_inc(evacuated, 1)

            def v_copy(i, u):
                t = 2 * i + u
                act.wait_ge(v_transposed, t + 1)
                wait(act, pv_done, 16 * t - 16)
                src = ps_v.rearrange("p n (h r) -> p n h r", h=HEADS)
                for odd in range(2):
                    nc.scalar.activation(v_ones[:, u, :, odd:HEADS:2, ROWS * odd:ROWS * odd + ROWS],
                                         src[:, :, odd:HEADS:2, :], ACT.Copy).then_inc(v_ready, 1)

            act.wait_ge(ones_ready, 1)
            for g in range(HEADS):
                k_hi(0, 0, g)
                if g == 0:
                    v_copy(0, 0)
                q_hi(0, 0, g)

            def body(i):
                for u in range(2):
                    more = not (is_last(i) and u == 1)
                    for g in range(HEADS):
                        before = (i, 0) if u else (i - 1, 1)
                        if g == 1 and not (isinstance(i, int) and i == 0 and u == 0):
                            leaving = [(*before, 1), (*before, 3)]
                        elif g == 3:
                            leaving = [(i, u, 0), (i, u, 2)]
                        else:
                            leaving = []
                        exps(i, u, g, 0)
                        if more:
                            k_hi(i + u, 1 - u, g)
                        exps(i, u, g, 1)
                        if g == 2 and more:
                            v_copy(i + u, 1 - u)
                        if more:
                            q_hi(i + u, 1 - u, g)
                        exps(i, u, g, 2)
                        if leaving:
                            evacuate(*leaving[0])
                        exps(i, u, g, 3)
                        if leaving:
                            evacuate(*leaving[1])

            batches(act, body)
            evacuate(BATCHES - 1, 1, 1)
            evacuate(BATCHES - 1, 1, 3)

        @block.vector
        def _(dve):
            def statistics(i):
                base = NORM_STEPS * i
                dve.wait_ge(x_loaded, 16 * i + 16)
                for u in range(2):
                    xt = x_res[:, bass.ds(2 * i + u, 1), :].rearrange("p o d -> p (o d)")
                    nc.vector.bn_stats(stats[:, u, :], xt).then_inc(ln_step, 1)
                wait(dve, xhat_ready, 2 * i)
                dve.wait_ge(ln_step, base + 2)
                nc.vector.memset(fence[:], 0.0)
                for u in range(2):
                    nc.vector.bn_aggr(mean_var[:, u, :], stats[:, u, :]).then_inc(ln_step, 1)

            def rstd_guess(i):
                dve.wait_ge(ln_step, NORM_STEPS * i + 4)
                rsqrt_guess(nc, dve, rstd[:], mean_var[:, :, 1], [tmp3[:, n, :] for n in range(3)],
                            ln_step, NORM_STEPS * i + 4)

            def rstd_newton(i, n):
                rsqrt_newton(nc, dve, rstd[:], [tmp3[:, n, :] for n in range(3)], ln_step,
                             NORM_STEPS * i + 4, n)

            def norm(i, u):
                t = 2 * i + u
                xt = x_res[:, bass.ds(t, 1), :].rearrange("p o d -> p (o d)")
                dve.wait_ge(ln_step, NORM_STEPS * i + NORM_STEPS)
                wait(dve, xhat_stored, 16 * t - 16)
                nc.vector.tensor_scalar(xhat[:, u, :], xt, mean_var[:, u, 0:1], rstd[:, u:u + 1],
                                        ALU.subtract, ALU.mult).then_inc(xhat_ready, 1)

            def maxes(i, u, g, j):
                n = 4 * (2 * i + u) + g
                if j == 0:
                    wait(dve, diag_ready, n - 1)
                dve.wait_ge(s_done, 4 * n + 2 * j + 2)
                nc.vector.tensor_reduce(maxima[:, g % 2, 2 * j:2 * j + 2], ps_s[:, 2 * j:2 * j + 2, :], AX,
                                        ALU.max).then_inc(reduced, 1)

            def reciprocals(i, u, j):
                t = 2 * i + u
                cols = slice(D // 2 * j, D // 2 * (j + 1))
                if j == 0:
                    dve.wait_ge(evacuated, 8 * t + 8)
                    wait(dve, gated_done, t)
                nc.vector.reciprocal(recip[:, cols], denominators[:, u, cols]).then_inc(recip_done, 1)

            def gate(i, u):
                t = 2 * i + u
                dve.wait_ge(recip_done, 2 * t + 2)
                wait(dve, x_added, t - 1)
                nc.vector.scalar_tensor_tensor(
                    out=gated[:, u, :], in0=outputs[:, u, :], scalar=c["gates"][:, 0:1], in1=recip[:],
                    op0=ALU.mult, op1=ALU.mult).then_inc(gated_done, 1)

            statistics(0)
            rstd_guess(0)
            for n in range(3):
                rstd_newton(0, n)
            norm(0, 0)
            norm(0, 1)
            for g in range(2):
                for j in range(2):
                    maxes(0, 0, g, j)

            def body(i):
                for u in range(2):
                    last_tile = is_last(i) and u == 1
                    norms = u == 0 and not is_last(i)
                    divides = not (isinstance(i, int) and i == 0 and u == 0)
                    before = (i, 0) if u else (i - 1, 1)
                    for g in range(HEADS):
                        if g == 0 and norms:
                            statistics(i + 1)
                            rstd_guess(i + 1)
                        if g == 1 and norms:
                            for n in range(3):
                                rstd_newton(i + 1, n)
                        if g == 2:
                            if not is_last(i):
                                norm(i + 1, u)
                            if divides:
                                reciprocals(*before, 0)
                        if g == 3 and divides:
                            reciprocals(*before, 1)
                            gate(*before)
                        if g < 2 or not last_tile:
                            for j in range(2):
                                maxes(*head_after_next(i, u, g), j)

            batches(dve, body)
            for j in range(2):
                reciprocals(BATCHES - 1, 1, j)
            gate(BATCHES - 1, 1)

        @block.tensor
        def _(pe):
            def v_transpose(i, u):
                t = 2 * i + u
                pe.wait_ge(ctx_loaded[u], 16 * i + 16)
                wait(pe, reduced, 8 * t)
                for k in range(NT):
                    mm = nc.tensor.transpose(ps_v[:, k, :], ctx_nat[:, u, P * k:P * k + P], c["ident"][:])
                mm.then_inc(v_transposed, 1)

            def scores(i, u, g, k):
                h, n = ORDER[g], 4 * (2 * i + u) + g
                if k == 0:
                    pe.wait_ge(lo_ready, 2 * n + 2)
                wait(pe, reduced, 2 * n + k // 2 - 1)
                if k == NT - 1 and g == 0:
                    pe.wait_ge(v_ready, 2 * (2 * i + u) + 2)
                nc.tensor.matmul(ps_s[:, k, :], q_stack[:, u, h, P * k:P * k + P], k_stack[:, u, h, :],
                                 start=True, stop=True).then_inc(s_done, 1)

            def scores_t(i, u, g, k):
                h, n = ORDER[g], 4 * (2 * i + u) + g
                if k == 0:
                    pe.wait_ge(diag_ready, n + 1)
                wait(pe, exp_done, 4 * n + k - 1)
                nc.tensor.matmul(ps_st[k % 2][:, :], k_stack[:, u, h, P * k:P * k + P], q_stack[:, u, h, :],
                                 start=True, stop=False)
                nc.tensor.matmul(ps_st[k % 2][:, :], c["minus_ones"][:], max_diag[:, g % 2],
                                 start=False, stop=True).then_inc(st_done, 1)

            def values(i, u, g, k):
                h, n = ORDER[g], 4 * (2 * i + u) + g
                t = 2 * i + u
                if k == 0 and g == 0:
                    pe.wait_ge(v_ready, 2 * t + 2)
                    wait(pe, evacuated, 8 * t - 4)
                if k == 0 and g == 2:
                    wait(pe, evacuated, 8 * t)
                pe.wait_ge(exp_done, 4 * n + k + 1)
                col = 64 * (h // 2)
                nc.tensor.matmul(ps_od[h % 2][col:col + 64, :], v_ones[:, u, k, h, :], probs[:, g % 2, k, :],
                                 start=(k == 0), stop=(k == NT - 1)).then_inc(pv_done, 1)

            v_transpose(0, 0)
            for g in range(2):
                for k in range(NT):
                    scores(0, 0, g, k)

            def body(i):
                for u in range(2):
                    last_tile = is_last(i) and u == 1
                    for g in range(HEADS):
                        for k in range(NT):
                            if k >= 2 and (g < 2 or not last_tile):
                                for kk in (2 * k - 4, 2 * k - 3):
                                    scores(*head_after_next(i, u, g), kk)
                            if (g, k) == (2, 1) and not last_tile:
                                v_transpose(i + u, 1 - u)
                            scores_t(i, u, g, k)
                            if g > 0:
                                values(i, u, g - 1, k)
                            elif u == 1:
                                values(i, 0, 3, k)
                            elif not (isinstance(i, int) and i == 0):
                                values(i - 1, 1, 3, k)

            batches(pe, body)
            for k in range(NT):
                values(BATCHES - 1, 1, 3, k)


def dense_and_memory(nc, c, w, t, raw, raw_loaded, x_res, xhat_d, out, logits):
    ctx_in, mask_in = t["ctx_2048"], t["mask_BxS2_bk0"]
    B, S, D = ctx_in.shape
    K = D // P
    U = S // P
    E = t["L0_ffn_W_gate"].shape[0]
    R = t["L1_ffn_Wg"].shape[1]
    SCALE = float(np.float32(1.0) / np.sqrt(np.float32(D)))
    NEG = 1e30
    RW = 8
    ctx_t = row_major(ctx_in).rearrange("(b u p) d -> b p u d", u=U, p=P)
    xhat_t = xhat_d.rearrange("(b u p) d -> b p u d", u=U, p=P)
    out_t = row_major(out).rearrange("(b u p) d -> b p u d", u=U, p=P)

    with ExitStack() as ctx:
        def sb(name, shape, dt=F32):
            return ctx.enter_context(nc.sbuf_tensor(name, shape, dt))

        def sem(name):
            return ctx.enter_context(nc.semaphore(name))

        def pair(name, shape):
            return sb(name + "_hi", shape, F32R), sb(name + "_lo", shape, F32R)

        xhat1 = sb("xhat1", [P, U, D])
        xhat23 = sb("xhat23", [P, 2, U, D])
        xhat2, xhat3 = xhat23[:, 0], xhat23[:, 1]
        xt1 = pair("xt1", [P, K, S])
        xt2 = pair("xt2", [P, K, S])
        xt3 = sb("xt3", [P, K, S])
        hid = pair("hid", [P, K, S])
        mem_raw = sb("mem_raw", [P, U, D])
        mem = pair("mem", [P, U, D])
        mem_t = pair("mem_t", [P, K, S])
        masked = sb("masked", [P, U, S])
        probs = sb("mem_probs", [P, U, S])
        probs_t = pair("probs_t", [P, U, S])
        mask_u8 = sb("mask_u8", [P, B, S], U8)
        mask_f = sb("mask_f", [P, S])
        mask_add = sb("mask_add", [P, S])
        valid_gate = sb("valid_gate", [P, 2])
        row_max = sb("row_max", [P, U])
        neg_max = sb("neg_max", [P, U])
        row_sum = sb("row_sum", [P, U])
        row_scale = sb("row_scale", [P, 2, U])
        top_in = sb("top_in", [P, U, E])
        top = sb("top", [P, U, 8])
        rw = sb("rw", [P, 6, U])
        stats = sb("row_stats", [P, 3, U, 6])
        mean_var = sb("mean_vars", [P, 3, U, 2])
        rstd = sb("rstds", [P, 3, U])
        rsqrt_tmp = sb("rsqrt_tmp", [P, 3, 3 * U])
        fence = {n: sb(f"fence_{n}", [P, 1]) for n in ("top", "first", "mid", "last", "moments")}
        ps = ctx.enter_context(nc.psum_tensor("ps_b", [P, 8, 512], F32))
        raw_expert = xhat23[:].rearrange("p n u d -> p (n u) d")
        raw_gate = masked[0:E].rearrange("p u s -> p (u s)")
        halves = lambda bank: ps[:, bank, :].rearrange("p (k s) -> p k s", s=S)

        w_transposed = sem("w_transposed")
        w_hi, w_lo = sem("w_hi"), sem("w_lo")
        expert_loaded, gate_loaded, route_loaded = sem("expert_loaded"), sem("gate_loaded"), sem("route_loaded")
        UP_SPLIT, ALL_SPLIT = K + 1, 2 * K + 2
        mem_loaded, mask_loaded = sem("mem_loaded"), sem("mask_loaded")
        xhat1_ready, xhat2_ready, xhat3_ready = sem("xhat1_ready"), sem("xhat2_ready"), sem("xhat3_ready")
        moments = {n: sem(f"moments{n}") for n in (1, 2, 3)}
        chain = sem("rstd_chain")
        xt1_ps, xt1_hi, xt1_lo = sem("xt1_ps"), sem("xt1_hi"), sem("xt1_lo")
        xt2_ps, xt2_hi, xt2_lo = sem("xt2_ps"), sem("xt2_hi"), sem("xt2_lo")
        memt_ps, memt_hi, memt_lo = sem("memt_ps"), sem("memt_hi"), sem("memt_lo")
        mem_hi, mem_lo = sem("mem_hi"), sem("mem_lo")
        gate_ps, gate_copied = sem("gate_ps"), sem("gate_copied")
        rw_step, rw_exp = sem("rw_step"), sem("rw_exp")
        up_ps, hid_hi, hid_lo = sem("up_ps"), sem("hid_hi"), sem("hid_lo")
        down_ps, x1_step = sem("down_ps"), sem("x1_step")
        scores_ps = sem("scores_ps")
        mask_ready, valid_ready = sem("mask_ready"), sem("valid_ready")
        sm_step, exp_done = sem("sm_step"), sem("mem_exp_done")
        pt_ps, pt_hi, pt_lo = sem("pt_ps"), sem("pt_hi"), sem("pt_lo")
        read_ps, scale_step, x2_ready = sem("read_ps"), sem("scale_step"), sem("x2_ready")
        xt3_ps, xt3_ready = sem("xt3_ps"), sem("xt3_ready")
        route_ps, logits_ready = sem("route_ps"), sem("logits_ready")
        xhat_stored, x_stored = sem("xhat3_stored"), sem("x_stored")

        block = ctx.enter_context(nc.Block())

        def iterations(eng, body):
            for s in range(3):
                body(s, s < B, s >= 1, s >= 2, True)
            with eng.Fori(3, B - 2) as s:
                body(s, True, True, True, True)
            body(B - 2, True, True, True, True)
            body(B - 1, True, True, True, False)
            body(B, False, True, True, False)
            body(B + 1, False, False, True, False)

        def weight_parts():
            gate = ps[:, 3, 0:E * K].rearrange("p (k e) -> p k e", k=K)
            return ([(w["up_hi"][:, k, :], w["up_lo"][:, k, :], ps[:, 4 + k, :], w_transposed, k + 1) for k in range(K)]
                    + [(w["gate"][:, :, 0], w["gate"][:, :, 1], gate, w_transposed, K + 1)]
                    + [(w["down_hi"][:, k, :], w["down_lo"][:, k, :], ps[:, 4 + k, :], w_transposed, K + 2 + k)
                       for k in range(K)]
                    + [(w["expert_hi"][:], w["expert_lo"][:], raw_expert, expert_loaded, 16)])

        def x_tile(b, u):
            return x_res[:, bass.ds(U * b + u, 1), :].rearrange("p o d -> p (o d)")

        @block.sync
        def _(sp):
            sp.dma_start(raw_gate, t["L0_ffn_W_gate"]).then_inc(gate_loaded, 16)
            sp.dma_start(raw_expert, t["L0_ffn_W_expert"].rearrange("(k p) n -> p k n", p=P)
                         ).then_inc(expert_loaded, 16)
            sp.dma_start(w["route"][:], t["L1_ffn_Wg"].rearrange("(k p) n -> p k n", p=P)).then_inc(route_loaded, 16)
            sp.dma_start(w["route_bias"][:], bass.AP(tensor=t["L1_ffn_bg"].tensor, offset=0, ap=[[0, P], [1, R]])
                         ).then_inc(route_loaded, 16)
            sp.dma_start(mask_u8[:], bass.AP(tensor=mask_in.tensor, offset=0, ap=[[0, P], [S, B], [1, S]])
                         ).then_inc(mask_loaded, 16)

            def body(s, f, a, r, more):
                if f:
                    wait(sp, memt_ps, 2 * s)
                    wait(sp, mem_lo, s)
                    sp.dma_start(mem_raw[:], ctx_t[bass.ds(s, 1)].rearrange("o p u d -> (o p) u d")
                                 ).then_inc(mem_loaded, 16)

            iterations(sp, body)

        @block.gpsimd
        def _(pool):
            def body(s, f, a, r, more):
                if not a:
                    return
                b = s - 1
                pool.wait_ge(mem_hi, b + 1)
                wait(pool, read_ps, U * b)
                nc.gpsimd.tensor_tensor(mem[1][:], mem_raw[:], mem[0][:], ALU.subtract).then_inc(mem_lo, 1)

            iterations(pool, body)

        @block.scalar
        def _(act):
            def xt1_part(b):
                wait(act, down_ps, U * b)
                for n in range(2):
                    act.wait_ge(xt1_ps, 2 * b + n + 1)
                    nc.scalar.activation(xt1[0][:, 2 * n:2 * n + 2, :], halves(n), ACT.Copy).then_inc(xt1_hi, 1)

            for n, (hi, _, src, loaded, count) in enumerate(weight_parts()):
                if n == UP_SPLIT:
                    xt1_part(0)
                act.wait_ge(loaded, count)
                nc.scalar.activation(hi, src, ACT.Copy).then_inc(w_hi, 1)

            def body(s, f, a, r, more):
                b = s - 1
                if f:
                    for n in range(2):
                        act.wait_ge(up_ps, 2 * s + n + 1)
                        nc.scalar.activation(hid[0][:, 2 * n:2 * n + 2, :], halves(2 + n), ACT.Relu
                                             ).then_inc(hid_hi, 1)
                    act.wait_ge(rw_step, RW * s + 3)
                    nc.scalar.activation(rw[:, 1, :], rw[:, 0, :], ACT.Exp).then_inc(rw_exp, 1)
                if a:
                    wait(act, scores_ps, b)
                    for n in range(2):
                        act.wait_ge(memt_ps, 2 * b + n + 1)
                        nc.scalar.activation(mem_t[0][:, 2 * n:2 * n + 2, :], halves(6 + n), ACT.Copy
                                             ).then_inc(memt_hi, 1)
                    for n in range(2):
                        act.wait_ge(xt2_ps, 2 * b + n + 1)
                        nc.scalar.activation(xt2[0][:, 2 * n:2 * n + 2, :], halves(4 + n), ACT.Copy
                                             ).then_inc(xt2_hi, 1)
                    act.wait_ge(mem_loaded, 16 * b + 16)
                    wait(act, read_ps, U * b)
                    wait(act, mem_lo, b)
                    nc.scalar.activation(mem[0][:], mem_raw[:], ACT.Copy).then_inc(mem_hi, 1)
                if r:
                    q = s - 2
                    act.wait_ge(xhat3_ready, U * q + U)
                    act.dma_start(xhat_t[bass.ds(q, 1)].rearrange("o p u d -> (o p) u d"),
                                  xhat3[:]).then_inc(xhat_stored, 16)
                    act.dma_start(out_t[bass.ds(q, 1)].rearrange("o p u d -> (o p) u d"),
                                  x_res[:, bass.ds(U * q, U), :]).then_inc(x_stored, 16)
                    wait(act, route_ps, q)
                    for n in range(2):
                        act.wait_ge(xt3_ps, 2 * q + n + 1)
                        nc.scalar.activation(xt3[:, 2 * n:2 * n + 2, :], halves(4 + n), ACT.Copy
                                             ).then_inc(xt3_ready, 1)
                if a:
                    act.wait_ge(sm_step, 4 * b + 4)
                    wait(act, pt_ps, b)
                    wait(act, scale_step, 2 * b)
                    for u in range(U):
                        nc.scalar.activation(probs[:, u, :], masked[:, u, :], ACT.Exp, bias=neg_max[:, u:u + 1],
                                             accum_out=row_sum[:, u:u + 1]).then_inc(exp_done, 1)
                    act.wait_ge(pt_ps, b + 1)
                    nc.scalar.activation(probs_t[0][:], halves(7), ACT.Copy).then_inc(pt_hi, 1)
                if f and more:
                    xt1_part(s + 1)

            iterations(act, body)
            act.wait_ge(xhat_stored, 16 * B)
            act.wait_ge(x_stored, 16 * B)

        @block.vector
        def _(dve):
            ready = {1: xhat1_ready, 2: xhat2_ready, 3: xhat3_ready}

            def statistics(n, b, u):
                nc.vector.bn_stats(stats[:, n - 1, u, :], x_tile(b, u)).then_inc(moments[n], 1)

            def rstd_chain(number, which):
                for n, b in which:
                    dve.wait_ge(moments[n], 2 * U * b + U)
                    wait(dve, ready[n], U * b)
                nc.vector.memset(fence["moments"][:], 0.0)
                for n, b in which:
                    for u in range(U):
                        nc.vector.bn_aggr(mean_var[:, n - 1, u, :], stats[:, n - 1, u, :]).then_inc(moments[n], 1)
                for n, b in which:
                    dve.wait_ge(moments[n], 2 * U * b + 2 * U)
                inverse_sqrt(nc, dve, rstd[:].rearrange("p n u -> p (n u)"),
                             mean_var[:].rearrange("p n u t -> p (n u) t")[:, :, 1],
                             [rsqrt_tmp[:, m, :] for m in range(3)], chain, RSQRT_STEPS * number)

            def norm(n, b, dst, number, free_sem, free_count):
                dve.wait_ge(chain, RSQRT_STEPS * (number + 1))
                wait(dve, free_sem, free_count)
                for u in range(U):
                    nc.vector.tensor_scalar(dst[:, u, :], x_tile(b, u), mean_var[:, n - 1, u, 0:1],
                                            rstd[:, n - 1, u:u + 1], ALU.subtract, ALU.mult).then_inc(ready[n], 1)

            def lo_part(dst, bank, n, hi, hi_sem, count, lo_sem):
                dve.wait_ge(hi_sem, count)
                nc.vector.tensor_tensor(dst[1][:, 2 * n:2 * n + 2, :], halves(bank), hi[:, 2 * n:2 * n + 2, :],
                                        ALU.subtract).then_inc(lo_sem, 1)

            def xt1_part(b):
                for n in range(2):
                    lo_part(xt1, n, n, xt1[0], xt1_hi, 2 * b + n + 1, xt1_lo)

            nc.vector.memset(mean_var[:], 0.0).then_inc(mask_ready, 1)
            dve.wait_ge(mask_ready, 1)
            def first_chain(b):
                for u in range(U):
                    statistics(1, b, u)
                rstd_chain(b, [(1, b)])

            first_chain(0)
            norm(1, 0, xhat1, 0, xt1_ps, 0)
            for n, (hi, lo, src, _, _) in enumerate(weight_parts()):
                if n == UP_SPLIT:
                    xt1_part(0)
                dve.wait_ge(w_hi, n + 1)
                nc.vector.tensor_tensor(lo, src, hi, ALU.subtract).then_inc(w_lo, 1)
            first_chain(1)
            dve.wait_ge(w_lo, ALL_SPLIT)

            def body(s, f, a, r, more):
                b = s - 1
                number = s + 2
                base = RW * s
                if f:
                    dve.wait_ge(gate_ps, s + 1)
                    parts = ps[:, 1, 0:2 * U * E].rearrange("p (u n e) -> p u n e", u=U, n=2)
                    nc.vector.tensor_reduce(top_in[:], parts.rearrange("p u n e -> p u e n"), AX, ALU.add
                                            ).then_inc(gate_copied, 1)
                    dve.wait_ge(gate_copied, s + 1)
                    nc.vector.memset(fence["top"][:], 0.0)
                    for u in range(U):
                        nc.vector.max(top[:, u, :], top_in[:, u, :]).then_inc(rw_step, 1)
                    dve.wait_ge(rw_step, RW * s + 2)
                    nc.vector.tensor_tensor(rw[:, 0, :], top[:, :, 1], top[:, :, 0], ALU.subtract).then_inc(rw_step, 1)
                    for n in range(2):
                        dve.wait_ge(hid_hi, 2 * s + n + 1)
                        nc.vector.scalar_tensor_tensor(
                            out=hid[1][:, 2 * n:2 * n + 2, :], in0=halves(2 + n), scalar=0.0,
                            in1=hid[0][:, 2 * n:2 * n + 2, :], op0=ALU.max, op1=ALU.subtract).then_inc(hid_lo, 1)
                if a:
                    for n in range(2):
                        lo_part(mem_t, 6 + n, n, mem_t[0], memt_hi, 2 * b + n + 1, memt_lo)
                    for n in range(2):
                        lo_part(xt2, 4 + n, n, xt2[0], xt2_hi, 2 * b + n + 1, xt2_lo)
                if f:
                    dve.wait_ge(rw_exp, s + 1)
                    nc.vector.tensor_scalar(rw[:, 2, :], rw[:, 1, :], 1.0, None, ALU.add).then_inc(rw_step, 1)
                    dve.wait_ge(rw_step, base + 4)
                    nc.vector.reciprocal(rw[:, 3, :], rw[:, 2, :]).then_inc(rw_step, 1)
                    dve.wait_ge(rw_step, base + 5)
                    nc.vector.tensor_tensor(rw[:, 4, :], rw[:, 1, :], rw[:, 3, :], ALU.mult).then_inc(rw_step, 1)
                    dve.wait_ge(rw_step, base + 6)
                    nc.vector.tensor_tensor(rw[:, 2, :], rw[:, 3, :], rw[:, 4, :], ALU.add).then_inc(rw_step, 1)
                    dve.wait_ge(rw_step, base + 7)
                    nc.vector.tensor_scalar(rw[:, 5, :], rw[:, 2, :], c["gates"][:, 2:3], None, ALU.mult
                                            ).then_inc(rw_step, 1)
                if r:
                    q = s - 2
                    wait(dve, xhat_stored, 16 * q)
                    norm(3, q, xhat3, number - 1, xt3_ps, 2 * q)
                if f and more:
                    norm(1, s + 1, xhat1, number - 1, xt1_ps, 2 * s + 2)
                if a:
                    dve.wait_ge(mask_loaded, 16)
                    nc.vector.tensor_copy(mask_f[:].unsqueeze(1), mask_u8[:, bass.ds(b, 1), :]).then_inc(mask_ready, 1)
                    dve.wait_ge(mask_ready, 2 * b + 2)
                    nc.vector.tensor_scalar(mask_add[:], mask_f[:], 1.0, NEG, ALU.subtract, ALU.mult
                                            ).then_inc(mask_ready, 1)
                    wait(dve, scale_step, 2 * b)
                    nc.vector.tensor_reduce(valid_gate[:, 0:1], mask_f[:], AX, ALU.max).then_inc(valid_ready, 1)
                    dve.wait_ge(valid_ready, 2 * b + 1)
                    nc.vector.tensor_scalar(valid_gate[:, 1:2], valid_gate[:, 0:1], c["gates"][:, 1:2], None,
                                            ALU.mult).then_inc(valid_ready, 1)
                ahead = f and not (isinstance(s, int) and s + 2 >= B)
                if ahead:
                    for u in range(U):
                        statistics(1, s + 2, u)

                def first_ffn(u):
                    n = 2 * (U * s + u)
                    dve.wait_ge(down_ps, U * s + u + 1)
                    xt = x_tile(s, u)
                    nc.vector.scalar_tensor_tensor(out=xt, in0=ps[:, 2 * u, :], scalar=c["gates"][:, 2:3], in1=xt,
                                                   op0=ALU.mult, op1=ALU.add).then_inc(x1_step, 1)
                    dve.wait_ge(x1_step, n + 1)
                    dve.wait_ge(rw_step, RW * s + RW)
                    nc.vector.scalar_tensor_tensor(out=xt, in0=ps[:, 2 * u + 1, :], scalar=rw[:, 5, u:u + 1], in1=xt,
                                                   op0=ALU.mult, op1=ALU.add).then_inc(x1_step, 1)
                    dve.wait_ge(x1_step, n + 2)
                    nc.vector.memset(fence["mid" if u else "first"][:], 0.0)
                    statistics(2, s, u)

                if f:
                    first_ffn(0)
                if a:
                    dve.wait_ge(mask_ready, 2 * b + 3)
                    dve.wait_ge(scores_ps, b + 1)
                    wait(dve, exp_done, U * b)
                    nc.vector.scalar_tensor_tensor(
                        out=masked[:], in0=halves(6), scalar=SCALE,
                        in1=mask_f[:].unsqueeze(1).broadcast_to([P, U, S]), op0=ALU.mult, op1=ALU.mult
                    ).then_inc(sm_step, 1)
                    dve.wait_ge(sm_step, 4 * b + 1)
                    nc.vector.tensor_tensor(masked[:], masked[:], mask_add[:].unsqueeze(1).broadcast_to([P, U, S]),
                                            ALU.add).then_inc(sm_step, 1)
                    dve.wait_ge(sm_step, 4 * b + 2)
                    nc.vector.tensor_reduce(row_max[:], masked[:], AX, ALU.max).then_inc(sm_step, 1)
                    dve.wait_ge(sm_step, 4 * b + 3)
                    nc.vector.tensor_scalar(neg_max[:], row_max[:], -1.0, None, ALU.mult).then_inc(sm_step, 1)
                if f:
                    first_ffn(1)
                if a:
                    dve.wait_ge(pt_hi, b + 1)
                    nc.vector.tensor_tensor(probs_t[1][:], halves(7), probs_t[0][:], ALU.subtract).then_inc(pt_lo, 1)
                if r:
                    q = s - 2
                    dve.wait_ge(route_ps, q + 1)
                    nc.vector.tensor_tensor(
                        logits[:, bass.ds(U * q, U), :], ps[:, 5, 0:U * R].rearrange("p (u e) -> p u e", u=U),
                        w["route_bias"][:].unsqueeze(1).broadcast_to([P, U, R]), ALU.add).then_inc(logits_ready, 1)
                if f and more:
                    xt1_part(s + 1)
                if a:
                    dve.wait_ge(exp_done, U * b + U)
                    nc.vector.reciprocal(row_scale[:, 0, :], row_sum[:]).then_inc(scale_step, 1)
                    dve.wait_ge(scale_step, 2 * b + 1)
                    dve.wait_ge(valid_ready, 2 * b + 2)
                    wait(dve, x2_ready, U * b)
                    nc.vector.tensor_scalar(row_scale[:, 1, :], row_scale[:, 0, :], valid_gate[:, 1:2], None,
                                            ALU.mult).then_inc(scale_step, 1)
                    dve.wait_ge(scale_step, 2 * b + 2)
                    for u in range(U):
                        dve.wait_ge(read_ps, U * b + u + 1)
                        xt = x_tile(b, u)
                        nc.vector.scalar_tensor_tensor(out=xt, in0=ps[:, 4 + u, :], scalar=row_scale[:, 1, u:u + 1],
                                                       in1=xt, op0=ALU.mult, op1=ALU.add).then_inc(x2_ready, 1)
                    dve.wait_ge(x2_ready, U * b + U)
                    nc.vector.memset(fence["last"][:], 0.0)
                    for u in range(U):
                        statistics(3, b, u)
                if f or a:
                    rstd_chain(number, [(1, s + 2)] * bool(ahead) + [(2, s)] * bool(f) + [(3, b)] * bool(a))
                if f:
                    norm(2, s, xhat2, number, xt2_ps, 2 * s)

            iterations(dve, body)

        @block.tensor
        def _(pe):
            def transposes(src, bank, done):
                for n in range(2):
                    for k in (2 * n, 2 * n + 1):
                        for u in range(U):
                            mm = nc.tensor.transpose(halves(bank + n)[:, k % 2, P * u:P * u + P],
                                                     src[:, u, P * k:P * k + P], c["ident"][:])
                    mm.then_inc(done, 1)

            def product(dst, lhs, rhs):
                n = len(lhs)
                for k in range(n):
                    for a_, b_ in ((0, 0), (0, 1), (1, 0)):
                        mm = nc.tensor.matmul(dst, lhs[k][a_], rhs[k][b_], start=(k == 0 and a_ == b_),
                                              stop=(k == n - 1 and a_ == 1))
                return mm

            def chunks(pair_, cols):
                return [[x[:, k, cols] for x in pair_] for k in range(K)]

            everything = slice(None)

            def down(s, u):
                tok = slice(P * u, P * u + P)
                product(ps[:, 2 * u, :], chunks(hid, tok), chunks((w["down_hi"], w["down_lo"]), everything))
                product(ps[:, 2 * u + 1, :], chunks(xt1, tok), chunks((w["expert_hi"], w["expert_lo"]), everything)
                        ).then_inc(down_ps, 1)

            def xt1_transposes(b):
                pe.wait_ge(xhat1_ready, U * b + U)
                wait(pe, x1_step, 2 * U * b - 2)
                transposes(xhat1, 0, xt1_ps)

            def weight_transposes(name, free):
                pe.wait_ge(raw_loaded[name], 16)
                for k in range(K):
                    wait(pe, w_lo, free and free + k)
                    for o in range(K):
                        mm = nc.tensor.transpose(ps[:, 4 + k, P * o:P * o + P], raw[name][:, o, P * k:P * k + P],
                                                 c["ident"][:])
                    mm.then_inc(w_transposed, 1)

            weight_transposes("up", 0)
            pe.wait_ge(gate_loaded, 16)
            for k in range(K):
                mm = nc.tensor.transpose(ps[:, 3, E * k:E * k + E], raw_gate[:, P * k:P * k + P],
                                         c["ident"][0:E, 0:E])
            mm.then_inc(w_transposed, 1)
            xt1_transposes(0)
            weight_transposes("down", 1)
            pe.wait_ge(route_loaded, 32)

            def body(s, f, a, r, more):
                b = s - 1
                if f:
                    if isinstance(s, int) and s == 0:
                        pe.wait_ge(w_lo, UP_SPLIT)
                    pe.wait_ge(xt1_lo, 2 * s + 2)
                    wait(pe, x1_step, 2 * U * s)
                    for u in range(U):
                        for k in range(K):
                            for a_ in ((0, 1) if k < K - 1 else (1, 0)):
                                cols = E if a_ else 2 * E
                                mm = nc.tensor.matmul(
                                    ps[:, 1, 2 * E * u:2 * E * u + cols], xt1[a_][:, k, P * u:P * u + P],
                                    w["gate"][:, k].rearrange("p n e -> p (n e)")[:, 0:cols],
                                    start=(k == 0 and a_ == 0), stop=(k == K - 1 and a_ == 0))
                    mm.then_inc(gate_ps, 1)
                    for n in range(2):
                        for o in (2 * n, 2 * n + 1):
                            mm = product(halves(2 + n)[:, o % 2, :],
                                         chunks((w["up_hi"], w["up_lo"]), slice(P * o, P * o + P)),
                                         chunks(xt1, everything))
                        mm.then_inc(up_ps, 1)
                if a:
                    pe.wait_ge(mem_loaded, 16 * b + 16)
                    wait(pe, pt_lo, b)
                    wait(pe, sm_step, 4 * b)
                    transposes(mem_raw, 6, memt_ps)
                    pe.wait_ge(xhat2_ready, U * b + U)
                    wait(pe, x2_ready, U * b)
                    transposes(xhat2, 4, xt2_ps)
                if f:
                    pe.wait_ge(hid_lo, 2 * s + 2)
                    pe.wait_ge(gate_copied, s + 1)
                    if isinstance(s, int) and s == 0:
                        pe.wait_ge(w_lo, ALL_SPLIT)
                    down(s, 0)
                if a:
                    pe.wait_ge(xt2_lo, 2 * b + 2)
                    pe.wait_ge(memt_lo, 2 * b + 2)
                    for u in range(U):
                        mm = product(halves(6)[:, u, :], chunks(xt2, slice(P * u, P * u + P)),
                                     chunks(mem_t, everything))
                    mm.then_inc(scores_ps, 1)
                if r:
                    q = s - 2
                    pe.wait_ge(xhat3_ready, U * q + U)
                    if a:
                        pe.wait_ge(xt2_lo, 2 * b + 2)
                    else:
                        pe.wait_ge(x2_ready, U * q + U)
                    transposes(xhat3, 4, xt3_ps)
                if f:
                    down(s, 1)
                if a:
                    pe.wait_ge(exp_done, U * b + U)
                    for m in range(U):
                        for u in range(U):
                            mm = nc.tensor.transpose(halves(7)[:, m, P * u:P * u + P],
                                                     probs[:, u, P * m:P * m + P], c["ident"][:])
                    mm.then_inc(pt_ps, 1)
                if r:
                    q = s - 2
                    pe.wait_ge(xt3_ready, 2 * q + 2)
                    for u in range(U):
                        for k in range(K):
                            mm = nc.tensor.matmul(ps[:, 5, R * u:R * u + R], xt3[:, k, P * u:P * u + P],
                                                  w["route"][:, k, :], start=(k == 0), stop=(k == K - 1))
                    mm.then_inc(route_ps, 1)
                if f and more:
                    xt1_transposes(s + 1)
                if a:
                    if r:
                        pe.wait_ge(logits_ready, s - 1)
                    pe.wait_ge(pt_lo, b + 1)
                    pe.wait_ge(mem_lo, b + 1)
                    for u in range(U):
                        product(ps[:, 4 + u, :], [[x[:, m, P * u:P * u + P] for x in probs_t] for m in range(U)],
                                [[x[:, m, :] for x in mem] for m in range(U)]).then_inc(read_ps, 1)

            iterations(pe, body)


class SlotTables:
    COLS = 5
    PIECES = 5

    def __init__(self, nc, ctx, c, T, E, capacity):
        self.nc, self.c, self.T = nc, c, T
        B = self.B = capacity // P

        def sb(name, shape, dt=F32):
            return ctx.enter_context(nc.sbuf_tensor(name, shape, dt))

        self.token, self.weight = sb("slot_token", [P, E, B], U32), sb("slot_weight", [P, E, B])
        self.hi, self.hot_lo = sb("slot_hi", [P, E, T], BF16), sb("hot_lo", [P, E, T, B], BF16)
        self.placed = sb("placed", [P, T, self.COLS, B], BF16)
        self.hot_hi = sb("hot_hi", [P, T, P], BF16)
        self.parts, self.sum = sb("slot_parts", [P, self.COLS, B]), sb("slot_sum", [P, B])
        self.hot_ready, self.summed, self.copied, self.step = (
            ctx.enter_context(nc.semaphore(n)) for n in ("hot_ready", "slots_summed", "slots_copied", "slot_step"))

    def piece(self, dve, e, n):
        T, B, V = self.T, self.B, self.nc.vector
        if n == 0:
            wait(dve, self.summed, e)
            V.tensor_tensor(self.placed[:], self.hot_lo[:, e].unsqueeze(2).broadcast_to([P, T, self.COLS, B]),
                            self.c["value"][:, e].unsqueeze(3).broadcast_to([P, T, self.COLS, B]),
                            ALU.mult).then_inc(self.hot_ready, 1)
        else:
            q = T // (self.PIECES - 1)
            tiles = slice(q * (n - 1), q * n)
            V.tensor_tensor(self.hot_hi[:, tiles], self.hi[:, e, tiles].unsqueeze(2).broadcast_to([P, q, P]),
                            self.c["column"][:].unsqueeze(1).broadcast_to([P, q, P]),
                            ALU.is_equal).then_inc(self.hot_ready, 1)

    def add_up(self, pe, e, ps):
        pe.wait_ge(self.hot_ready, self.PIECES * (e + 1))
        for n in range(self.T):
            mm = self.nc.tensor.matmul(ps[:, 0:self.COLS * self.B], self.hot_hi[:, n, :],
                                       self.placed[:, n].rearrange("p c b -> p (c b)"),
                                       start=(n == 0), stop=(n == self.T - 1))
        mm.then_inc(self.summed, 1)

    def finish(self, dve, e, ps):
        V, parts, step = self.nc.vector, self.parts, self.step
        dve.wait_ge(self.summed, e + 1)
        V.tensor_copy(parts[:].rearrange("p c b -> p (c b)"), ps[:, 0:self.COLS * self.B]).then_inc(self.copied, 1)
        dve.wait_ge(self.copied, e + 1)
        V.scalar_tensor_tensor(out=self.token[:, e], in0=parts[:, 0, :], scalar=float(P), in1=parts[:, 1, :],
                               op0=ALU.mult, op1=ALU.add).then_inc(step, 1)
        V.tensor_tensor(self.sum[:], parts[:, 2, :], parts[:, 3, :], ALU.add).then_inc(step, 1)
        dve.wait_ge(step, 4 * e + 2)
        V.tensor_tensor(self.sum[:], self.sum[:], parts[:, 4, :], ALU.add).then_inc(step, 1)
        dve.wait_ge(step, 4 * e + 3)
        V.tensor_scalar(self.weight[:, e], self.sum[:], self.c["gates"][:, 3:4], None, ALU.mult).then_inc(step, 1)
        dve.wait_ge(step, 4 * e + 4)


def route(nc, c, logits, capacity, slots, weights):
    T, E = logits.shape[1], logits.shape[2]
    B = capacity // P
    with ExitStack() as ctx:
        def sb(name, shape, dt=F32):
            return ctx.enter_context(nc.sbuf_tensor(name, shape, dt))

        def psum(name, shape):
            return ctx.enter_context(nc.psum_tensor(name, shape, F32))

        def sem(name):
            return ctx.enter_context(nc.semaphore(name))

        digits, token, value, column = (c[n] for n in ("digits", "token", "value", "column"))
        before = sb("before", [P, P])
        restart = sb("restart", [P, 2 * E, T])
        beats = sb("beats", [P, T, E, E])
        rank = sb("rank", [P, T, E])
        assigned = sb("assigned", [P, T, E])
        best = sb("best", [P, T])
        shifted, expo = sb("shifted", [P, T, E]), sb("expo", [P, T, E])
        total, inv = sb("total", [P, T]), sb("inv", [P, T])
        prob = sb("prob", [P, T, E])
        unassigned = sb("unassigned", [P, T, E])
        score = sb("score", [P, E, T])
        kth = sb("kth", [P, E])
        ones_bf = sb("ones_bf", [P, P], BF16)
        cand = sb("cand", [P, E, RADIX])
        at_least = sb("at_least", [P, T, E, RADIX], BF16)
        kept = sb("kept", [P, E, RADIX])
        flags = sb("flags", [P, 2, E, T])
        running = sb("running", [P, 2, E, T])
        earlier = sb("earlier", [P, 2, E, T])
        wanted = sb("wanted", [P, E])
        ties = sb("ties", [P, E])
        chosen_n = sb("chosen_n", [P, E])
        fits = sb("fits", [P, E, T])
        chosen = sb("chosen", [P, E, T])
        taken = sb("taken", [P, E, T])
        other = sb("other", [P, E, T])
        slot = sb("slot", [P, E, T])
        slot_i, slot_hi_i, slot_lo_i = (sb(n, [P, E, T], I32) for n in ("slot_i", "slot_hi_i", "slot_lo_i"))
        slot_lo = sb("slot_lo", [P, E, T], BF16)
        weight = sb("weight", [P, 3, E, T])
        ps_count = psum("ps_count", [P, 512])
        ps_before = psum("ps_before", [P, 512])
        ps_slot = psum("ps_slot", [P, 512])
        cs = sem("cs")
        tables = sem("tables")
        logits_shifted, exped = sem("logits_shifted"), sem("exped")
        counted, count_ps = sem("counted"), sem("count_ps")
        flags_ready, prefix_ps = sem("flags_ready"), sem("prefix_ps")
        block = ctx.enter_context(nc.Block())

        @block.sync
        def _(sp):
            weights.load(sp, 0, 0, 0)
            weights.load(sp, 0, 0, 1)

        @block.gpsimd
        def _(pool):
            nc.gpsimd.memset(restart[:], 1.0).then_inc(tables, 1)
            pool.wait_ge(tables, 1)
            nc.gpsimd.memset(restart[:, :, 0:1], 0.0).then_inc(tables, 1)
            nc.gpsimd.affine_select(out=before[:], in_=c["ones"][:], compare_op=ALU.is_gt, fill=0.0, base=0,
                                    pattern=[[1, P]], channel_multiplier=-1).then_inc(tables, 1)
            for t in range(weights.AHEAD):
                weights.split_lo(pool, 0, 0, t)

        @block.scalar
        def _(act):
            act.wait_ge(logits_shifted, 1)
            nc.scalar.activation(expo[:], shifted[:], ACT.Exp).then_inc(exped, 1)
            for t in range(weights.AHEAD):
                weights.split_hi(act, 0, 0, t)

        @block.tensor
        def _(pe):
            with pe.Fori(0, ROUNDS) as r:
                pe.wait_ge(counted, r + 1)
                for n in range(T):
                    mm = nc.tensor.matmul(ps_count[:, 0:E * RADIX], ones_bf[:],
                                          at_least[:, n].rearrange("p e j -> p (e j)"),
                                          start=(n == 0), stop=(n == T - 1))
                mm.then_inc(count_ps, 1)
            pe.wait_ge(tables, 3)
            pe.wait_ge(flags_ready, 2)
            f = flags[:].rearrange("p f e t -> p (f e t)")
            nc.tensor.matmul(ps_before[:, 0:2 * E * T], before[:], f, start=True, stop=True)
            nc.tensor.matmul(ps_count[:, 0:2 * E * T], c["ones"][:], f, start=True, stop=True).then_inc(prefix_ps, 1)
            slots.add_up(pe, 0, ps_slot)

        @block.vector
        def _(dve):
            steps = [0]

            def link(ins):
                steps[0] += 1
                ins.then_inc(cs, 1)
                dve.wait_ge(cs, steps[0])

            V = nc.vector

            def per_expert(ap):
                return ap.unsqueeze(2).broadcast_to([P, E, T])

            link(V.memset(beats[:], 0.0))
            for e in range(E):
                for js, op in ((slice(0, e), ALU.is_ge), (slice(e + 1, E), ALU.is_gt)):
                    n = js.stop - js.start
                    if n:
                        link(V.tensor_tensor(beats[:, :, e, js], logits[:, :, js],
                                             logits[:, :, e:e + 1].broadcast_to([P, T, n]), op))
            link(V.tensor_reduce(rank[:], beats[:], AX, ALU.add))
            link(V.tensor_scalar(assigned[:], rank[:], 2.0, None, ALU.is_lt))
            link(V.tensor_reduce(best[:], logits[:], AX, ALU.max))
            V.tensor_tensor(shifted[:], logits[:], best[:].unsqueeze(2).broadcast_to([P, T, E]),
                            ALU.subtract).then_inc(logits_shifted, 1)
            dve.wait_ge(exped, 1)
            link(V.tensor_tensor(expo[:], expo[:], assigned[:], ALU.mult))
            link(V.tensor_reduce(total[:], expo[:], AX, ALU.add))
            link(V.reciprocal(inv[:], total[:]))
            link(V.tensor_tensor(prob[:], expo[:], inv[:].unsqueeze(2).broadcast_to([P, T, E]), ALU.mult))
            link(V.tensor_scalar(unassigned[:], assigned[:], 1.0, None, ALU.subtract))
            link(V.tensor_tensor(score[:].rearrange("p e t -> p t e"), prob[:], unassigned[:], ALU.add))
            link(V.memset(kth[:], 0.0))
            link(V.memset(ones_bf[:], 1.0))

            base = steps[0]
            with dve.Fori(0, ROUNDS) as r:
                V.tensor_tensor(cand[:].bitcast(I32), kth[:].bitcast(I32).unsqueeze(2).broadcast_to([P, E, RADIX]),
                                digits[:, bass.ds(r, 1), :].broadcast_to([P, E, RADIX]),
                                ALU.bitwise_or).then_inc(cs, 1)
                dve.wait_ge(cs, 3 * r + base + 1)
                V.tensor_tensor(at_least[:], score[:].rearrange("p e t -> p t e").unsqueeze(3)
                                .broadcast_to([P, T, E, RADIX]),
                                cand[:].unsqueeze(1).broadcast_to([P, T, E, RADIX]), ALU.is_ge).then_inc(counted, 1)
                dve.wait_ge(count_ps, r + 1)
                V.scalar_tensor_tensor(out=kept[:], in0=ps_count[:, 0:E * RADIX].rearrange("p (e j) -> p e j", e=E),
                                       scalar=float(capacity), in1=cand[:], op0=ALU.is_ge,
                                       op1=ALU.mult).then_inc(cs, 1)
                dve.wait_ge(cs, 3 * r + base + 2)
                V.tensor_reduce(kth[:], kept[:], AX, ALU.max).then_inc(cs, 1)
                dve.wait_ge(cs, 3 * r + base + 3)
            steps[0] += 3 * ROUNDS

            for n, op in enumerate((ALU.is_gt, ALU.is_equal)):
                V.tensor_tensor(flags[:, n], score[:], per_expert(kth[:]), op).then_inc(flags_ready, 1)
            dve.wait_ge(tables, 3)
            dve.wait_ge(prefix_ps, 1)
            flat = lambda ap: ap[:].rearrange("p f e t -> p (f e t)")
            link(V.tensor_tensor_scan(flat(running), restart[:].rearrange("p f t -> p (f t)"),
                                      ps_count[:, 0:2 * E * T], 0.0, ALU.mult, ALU.add))
            link(V.tensor_tensor(flat(earlier), flat(running), ps_count[:, 0:2 * E * T], ALU.subtract))
            link(V.tensor_tensor(flat(earlier), flat(earlier), ps_before[:, 0:2 * E * T], ALU.add))
            link(V.tensor_scalar(wanted[:], running[:, 0, :, T - 1], -1.0, float(capacity), ALU.mult, ALU.add))
            link(V.tensor_tensor(ties[:], wanted[:], running[:, 1, :, T - 1], ALU.min))
            link(V.tensor_tensor(chosen_n[:], ties[:], running[:, 0, :, T - 1], ALU.add))
            link(V.tensor_tensor(fits[:], earlier[:, 1], per_expert(wanted[:]), ALU.is_lt))
            link(V.tensor_tensor(fits[:], fits[:], flags[:, 1], ALU.mult))
            link(V.tensor_tensor(chosen[:], flags[:, 0], fits[:], ALU.add))
            link(V.tensor_tensor(taken[:], earlier[:, 1], per_expert(wanted[:]), ALU.min))
            link(V.tensor_tensor(taken[:], taken[:], earlier[:, 0], ALU.add))
            link(V.tensor_tensor(other[:], token[:].unsqueeze(1).broadcast_to([P, E, T]), taken[:], ALU.subtract))
            link(V.tensor_tensor(other[:], other[:], per_expert(chosen_n[:]), ALU.add))
            link(V.tensor_tensor(slot[:], taken[:], other[:], ALU.subtract))
            link(V.tensor_tensor(slot[:], slot[:], chosen[:], ALU.mult))
            link(V.tensor_tensor(slot_i[:], slot[:], other[:], ALU.add))
            link(V.tensor_scalar(slot_hi_i[:], slot_i[:], DIGIT, None, ALU.logical_shift_right))
            link(V.tensor_scalar(slot_lo_i[:], slot_i[:], RADIX - 1, None, ALU.bitwise_and))
            link(V.tensor_copy(slots.hi[:], slot_hi_i[:]))
            link(V.tensor_copy(slot_lo[:], slot_lo_i[:]))
            link(V.tensor_tensor(weight[:, 0], chosen[:], prob[:].rearrange("p t e -> p e t"), ALU.mult))
            for n in range(3):
                link(V.tensor_copy(value[:, :, :, 2 + n], weight[:, n]))
                if n < 2:
                    link(V.tensor_tensor(weight[:, n + 1], weight[:, n], value[:, :, :, 2 + n], ALU.subtract))
            link(V.tensor_tensor(slots.hot_lo[:], slot_lo[:].unsqueeze(3).broadcast_to([P, E, T, B]),
                                 column[:, 0:B].unsqueeze(1).unsqueeze(1).broadcast_to([P, E, T, B]), ALU.is_equal))
            for n in range(slots.PIECES):
                slots.piece(dve, 0, n)
            slots.finish(dve, 0, ps_slot)


class ExpertWeights:
    GROUP = 4
    RING = 4
    AHEAD = 2

    def __init__(self, nc, ctx, w1, w2, tiles):
        E, D, H = w1.shape
        K, self.HT, self.tiles = D // P, H // P, tiles
        self.nc = nc
        self.w1_t = w1.rearrange("e (k p) h -> e p k h", p=P)
        self.w2_t = w2.rearrange("e (t p) d -> e p t d", p=P)

        def sb(name, shape, dt=F32):
            return ctx.enter_context(nc.sbuf_tensor(name, shape, dt))

        self.w1_raw = sb("w1_raw", [P, 2, K, self.GROUP * P])
        self.w2_raw = sb("w2_raw", [P, 2, self.GROUP, D])
        self.w1 = [sb("w1_hi", [P, self.RING, K, P], F32R), sb("w1_lo", [P, self.RING, K, P], F32R)]
        self.w2 = [sb("w2_hi", [P, self.RING, D], F32R), sb("w2_lo", [P, self.RING, D], F32R)]
        self.loaded = [ctx.enter_context(nc.semaphore(f"w_loaded{n}")) for n in range(2)]
        self.hi_done = ctx.enter_context(nc.semaphore("w_hi_done"))
        self.w1_lo_done = ctx.enter_context(nc.semaphore("w1_lo_done"))
        self.w2_lo_done = ctx.enter_context(nc.semaphore("w2_lo_done"))
        self.products = ctx.enter_context(nc.semaphore("y_done"))

    def load(self, sp, e, half, q):
        n, par = 8 * e + 4 * half + q, q % 2
        cols = slice(self.GROUP * P * q, self.GROUP * P * (q + 1))
        wait(sp, self.w1_lo_done, self.GROUP * (n - 1))
        wait(sp, self.w2_lo_done, self.GROUP * (n - 1))
        sp.dma_start(self.w1_raw[:, par], self.w1_t[bass.ds(e, 1), :, :, cols]
                     .rearrange("o p k h -> (o p) k h")).then_inc(self.loaded[par], 16)
        sp.dma_start(self.w2_raw[:, par], self.w2_t[bass.ds(e, 1), :, self.GROUP * q:self.GROUP * (q + 1), :]
                     .rearrange("o p t d -> (o p) t d")).then_inc(self.loaded[par], 16)

    def raw(self, t):
        par, j = (t // self.GROUP) % 2, t % self.GROUP
        return self.w1_raw[:, par, :, P * j:P * j + P], self.w2_raw[:, par, j, :]

    def split_hi(self, act, e, half, t):
        g, r = self.HT * (2 * e + half) + t, t % self.RING
        w1, w2 = self.raw(t)
        act.wait_ge(self.loaded[(t // self.GROUP) % 2], 32 * (4 * e + 2 * half + t // (2 * self.GROUP) + 1))
        wait(act, self.products, self.tiles * (g - self.RING + 1))
        self.nc.scalar.activation(self.w1[0][:, r], w1, ACT.Copy).then_inc(self.hi_done, 1)
        self.nc.scalar.activation(self.w2[0][:, r], w2, ACT.Copy).then_inc(self.hi_done, 1)

    def split_lo(self, pool, e, half, t):
        g, r = self.HT * (2 * e + half) + t, t % self.RING
        pool.wait_ge(self.hi_done, 2 * g + 1)
        self.nc.gpsimd.tensor_tensor(self.w1[1][:, r], self.raw(t)[0], self.w1[0][:, r],
                                     ALU.subtract).then_inc(self.w1_lo_done, 1)

    def split_w2_lo(self, dve, e, half, t):
        g, r = self.HT * (2 * e + half) + t, t % self.RING
        dve.wait_ge(self.hi_done, 2 * g + 2)
        self.nc.vector.tensor_tensor(self.w2[1][:, r], self.raw(t)[1], self.w2[0][:, r],
                                     ALU.subtract).then_inc(self.w2_lo_done, 1)


def experts(nc, c, weights, slots, E, D, xhat_d, out):
    K = D // P
    HT = weights.HT
    slot_token, slot_weight = slots.token, slots.weight
    I = slots.B // 2
    GROUP, RING, AHEAD = weights.GROUP, weights.RING, weights.AHEAD
    w1_s, w2_s, y_done = weights.w1, weights.w2, weights.products
    rows_out = row_major(out)
    with ExitStack() as ctx:
        def sb(name, shape, dt=F32):
            return ctx.enter_context(nc.sbuf_tensor(name, shape, dt))

        def sem(name):
            return ctx.enter_context(nc.semaphore(name))

        rows = sb("rows", [P, I, D])
        rows_t = [sb("rows_t_hi", [P, 2, K, D], F32R), sb("rows_t_lo", [P, 2, K, D], F32R)]
        hidden = sb("hidden", [P, 2, D])
        hid = [sb("hidden_hi", [P, 2, D], F32R), sb("hidden_lo", [P, 2, D], F32R)]
        scaled = sb("scaled", [P, I, D])
        gather_index = sb("gather_index", [P, I], U32)
        scatter_index = sb("scatter_index", [P, I], U32)
        factor = sb("factor", [P, I])
        ps_y = ctx.enter_context(nc.psum_tensor("ps_y", [P, I, 512], F32))
        ps_h = ctx.enter_context(nc.psum_tensor("ps_h", [P, 2, 512], F32))
        ps_t = ctx.enter_context(nc.psum_tensor("ps_t", [P, 2, I, P], F32))

        ps_slot = ps_t[:, 1].rearrange("p i s -> p (i s)")
        index_ready = sem("index_ready")
        factor_ready = sem("factor_ready")
        gathered = [sem(f"gathered{i}") for i in range(I)]
        rows_ps = sem("rows_ps")
        rows_hi, rows_lo = sem("rows_hi"), sem("rows_lo")
        h_ps, gelu_done = sem("h_ps"), sem("gelu_done")
        h_hi, h_lo = sem("h_hi"), sem("h_lo")
        y_out = sem("y_out")
        scattered = sem("scattered")
        block = ctx.enter_context(nc.Block())
        STEPS = 2 * HT

        def all_experts(eng, body):
            body(0, True)
            with eng.Fori(1, E - 1) as e:
                body(e, True)
            body(E - 1, False)

        def table_step(e, half, t):
            if isinstance(e, int) and e == 0 and 1 + (HT * half + t) // 8 < E:
                return 1 + (HT * half + t) // 8, t % 8
            return None, None

        def first(e, half):
            return isinstance(e, int) and e == 0 and half == 0

        @block.sync
        def _(sp):
            def body(e, more):
                for half in range(2):
                    for q in range(HT // GROUP):
                        if not (first(e, half) and q < 2):
                            weights.load(sp, e, half, q)

            all_experts(sp, body)

        def gather_wait(e, half):
            n = 2 * e + half
            nc.gpsimd.wait_ge(index_ready, n + 1)
            wait(nc.gpsimd, rows_ps, K * n)

        def gather():
            for i in range(I):
                nc.gpsimd.indirect_dma_start(
                    out=rows[:, i, :], out_offset=None, in_=xhat_d,
                    in_offset=bass.IndirectOffsetOnAxis(ap=gather_index[:, i:i + 1], axis=0)
                ).then_inc(gathered[i], 16)

        @block.gpsimd
        def _(pool):
            def split(e, half, t):
                weights.split_lo(pool, e, half, t)

            def scatter_wait(e, half, i):
                n = I * (2 * e + half) + i
                pool.wait_ge(y_out, n + 1)
                wait(pool, scattered, 16 * I * (2 * e + half))

            def scatter(i):
                nc.gpsimd.indirect_dma_start(
                    out=rows_out, out_offset=bass.IndirectOffsetOnAxis(
                        ap=scatter_index[:, i:i + 1], axis=0),
                    in_=scaled[:, i, :], in_offset=None, compute_op=ALU.add).then_inc(scattered, 16)

            gather_wait(0, 0)
            gather()

            def body(e, more):
                for half in range(2):
                    for t in range(HT):
                        i = (t - 3) // 2 if t in range(3, 3 + 2 * I, 2) and not first(e, half) else None
                        gathers = t == 1 and (half == 0 or more)
                        if i is not None:
                            scatter_wait(e if half else e - 1, 1 - half, i)
                        if gathers:
                            gather_wait(e + half, 1 - half)
                        if t + AHEAD < HT:
                            split(e, half, t + AHEAD)
                        elif half == 0:
                            split(e, 1, t + AHEAD - HT)
                        elif more:
                            split(e + 1, 0, t + AHEAD - HT)
                        if i is not None:
                            scatter(i)
                        if gathers:
                            gather()

            all_experts(pool, body)
            for i in range(I):
                scatter_wait(E - 1, 1, i)
                scatter(i)
            pool.wait_ge(scattered, 16 * 2 * E * I)

        @block.scalar
        def _(act):
            def split(e, half, t):
                weights.split_hi(act, e, half, t)

            def rows_part(e, half, k):
                n = K * (2 * e + half) + k
                act.wait_ge(rows_ps, n + 1)
                nc.scalar.activation(rows_t[0][:, half, k, :], ps_t[:, k % 2].rearrange("p i s -> p (i s)"),
                                     ACT.Copy).then_inc(rows_hi, 1)

            def gelu(e, half, t):
                g = STEPS * e + HT * half + t
                act.wait_ge(h_ps, g + 1)
                wait(act, h_lo, g - 1)
                nc.scalar.activation(hidden[:, t % 2, :], ps_h[:, t % 2, :], ACT.Gelu).then_inc(gelu_done, 1)

            for k in range(K):
                rows_part(0, 0, k)

            def body(e, more):
                for half in range(2):
                    for t in range(HT):
                        gelu(e, half, t)
                        if t + AHEAD < HT:
                            split(e, half, t + AHEAD)
                        elif half == 0:
                            split(e, 1, t + AHEAD - HT)
                        elif more:
                            split(e + 1, 0, t + AHEAD - HT)
                        if 8 <= t < 8 + K:
                            if half == 0:
                                rows_part(e, 1, t - 8)
                            elif more:
                                rows_part(e + 1, 0, t - 8)

            all_experts(act, body)

        @block.vector
        def _(dve):
            def rows_part(e, half, k):
                n = K * (2 * e + half) + k
                dve.wait_ge(rows_hi, n + 1)
                nc.vector.tensor_tensor(rows_t[1][:, half, k, :], ps_t[:, k % 2].rearrange("p i s -> p (i s)"),
                                        rows_t[0][:, half, k, :], ALU.subtract).then_inc(rows_lo, 1)

            def outputs(e, half):
                blk = 2 * e + half
                wait(dve, scattered, 16 * I * blk)
                cols = slice(I * half, I * half + I)
                nc.vector.tensor_copy(scatter_index[:].unsqueeze(1), slot_token[:, bass.ds(e, 1), cols]
                                      ).then_inc(factor_ready, 1)
                nc.vector.tensor_copy(factor[:].unsqueeze(1), slot_weight[:, bass.ds(e, 1), cols]
                                      ).then_inc(factor_ready, 1)
                dve.wait_ge(factor_ready, 2 * blk + 2)
                for i in range(I):
                    dve.wait_ge(y_done, I * (HT * (blk + 1) - 1) + i + 1)
                    nc.vector.tensor_scalar(scaled[:, i, :], ps_y[:, i, :], factor[:, i:i + 1], None,
                                            ALU.mult).then_inc(y_out, 1)

            def hidden_parts(e, half, t):
                g = STEPS * e + HT * half + t
                dve.wait_ge(gelu_done, g + 1)
                wait(dve, y_done, I * (g - 1))
                nc.vector.tensor_copy(hid[0][:, t % 2, :], hidden[:, t % 2, :]).then_inc(h_hi, 1)
                dve.wait_ge(h_hi, g + 1)
                nc.vector.tensor_tensor(hid[1][:, t % 2, :], hidden[:, t % 2, :], hid[0][:, t % 2, :],
                                        ALU.subtract).then_inc(h_lo, 1)

            def pick(e, half):
                n = 2 * e + half
                wait(dve, rows_ps, K * n)
                nc.vector.tensor_copy(gather_index[:].unsqueeze(1),
                                      slot_token[:, bass.ds(e, 1), I * half:I * half + I]).then_inc(index_ready, 1)

            pick(0, 0)
            for t in range(AHEAD):
                weights.split_w2_lo(dve, 0, 0, t)
            for k in range(K):
                rows_part(0, 0, k)

            def body(e, more):
                for half in range(2):
                    if half == 1:
                        outputs(e, 0)
                    elif not first(e, half):
                        outputs(e - 1, 1)
                    for t in range(HT):
                        if t == 0:
                            if half == 0:
                                pick(e, 1)
                            elif more:
                                pick(e + 1, 0)
                        hidden_parts(e, half, t)
                        if t + AHEAD < HT:
                            weights.split_w2_lo(dve, e, half, t + AHEAD)
                        elif half == 0:
                            weights.split_w2_lo(dve, e, 1, t + AHEAD - HT)
                        elif more:
                            weights.split_w2_lo(dve, e + 1, 0, t + AHEAD - HT)
                        other, n = table_step(e, half, t)
                        if other and n < slots.PIECES:
                            slots.piece(dve, other, n)
                        if other and n == 7:
                            slots.finish(dve, other, ps_slot)
                        if 8 <= t < 8 + K:
                            if half == 0:
                                rows_part(e, 1, t - 8)
                            elif more:
                                rows_part(e + 1, 0, t - 8)

            all_experts(dve, body)
            outputs(E - 1, 1)

        @block.tensor
        def _(pe):
            def transposes(e, half, k):
                n = K * (2 * e + half) + k
                if k == 0:
                    for i in range(I):
                        pe.wait_ge(gathered[i], 16 * (2 * e + half + 1))
                wait(pe, rows_lo, n - 1)
                if k == 1 and isinstance(e, int) and e * 2 + half in (1, 2):
                    pe.wait_ge(slots.copied, min(2 * (2 * e + half), E))
                for i in range(I):
                    mm = nc.tensor.transpose(ps_t[:, k % 2, i, :], rows[:, i, P * k:P * k + P], c["ident"][:])
                mm.then_inc(rows_ps, 1)

            def hidden_product(e, half, t):
                g, r = STEPS * e + HT * half + t, t % RING
                if t == 0:
                    pe.wait_ge(rows_lo, K * (2 * e + half) + K)
                pe.wait_ge(weights.w1_lo_done, g + 1)
                wait(pe, gelu_done, g - 1)
                for k in range(K):
                    for a, b in ((0, 0), (0, 1), (1, 0)):
                        mm = nc.tensor.matmul(ps_h[:, t % 2, :], w1_s[a][:, r, k, :], rows_t[b][:, half, k, :],
                                              start=(k == 0 and a == b), stop=(k == K - 1 and a == 1))
                mm.then_inc(h_ps, 1)

            def output_product(e, half, t):
                g, r = STEPS * e + HT * half + t, t % RING
                pe.wait_ge(h_lo, g + 1)
                pe.wait_ge(weights.w2_lo_done, g + 1)
                for i in range(I):
                    n = I * (2 * e + half) + i
                    if t == 0:
                        wait(pe, y_out, n - I + 1)
                    tok = slice(P * i, P * i + P)
                    for a, b in ((0, 0), (0, 1), (1, 0)):
                        mm = nc.tensor.matmul(ps_y[:, i, :], hid[a][:, t % 2, tok], w2_s[b][:, r],
                                              start=(t == 0 and a == b), stop=(t == HT - 1 and a == 1))
                    mm.then_inc(y_done, 1)

            for k in range(K):
                transposes(0, 0, k)

            def body(e, more):
                for half in range(2):
                    for t in range(HT):
                        hidden_product(e, half, t)
                        other, n = table_step(e, half, t)
                        if other and n == 6:
                            if t > 8:
                                pe.wait_ge(rows_lo, 2 * K)
                            slots.add_up(pe, other, ps_slot)
                        if t > 0:
                            output_product(e, half, t - 1)
                        if 8 <= t < 8 + K:
                            if half == 0:
                                transposes(e, 1, t - 8)
                            elif more:
                                transposes(e + 1, 0, t - 8)
                    output_product(e, half, HT - 1)

            all_experts(pe, body)


def program(nc, t, out):
    with ExitStack() as ctx:
        def sb(name, shape, dt=F32):
            return ctx.enter_context(nc.sbuf_tensor(name, shape, dt))

        B, S, D = t["x"].shape
        TOK, K = B * S, D // P
        E = t["L1_ffn_W1"].shape[0]
        CAPACITY = TOK // E
        logits = sb("logits", [P, TOK // P, E])
        xhat_d = nc.dram_tensor("xhat_d", (TOK, D), F32).ap()
        c = build_constants(nc, ctx, t["g_xattn"], t["g_ffn"], TOK // P, E)
        with ExitStack() as xctx:
            x_res = xctx.enter_context(nc.sbuf_tensor("x_res", [P, TOK // P, D], F32))
            raw = {n: xctx.enter_context(nc.sbuf_tensor(f"raw_{n}", [P, K, D], F32)) for n in ("up", "down")}
            raw_loaded = {n: xctx.enter_context(nc.semaphore(f"raw_{n}_loaded")) for n in raw}
            column_attention(nc, c, t["x"], t["ctx_2048"], xhat_d, x_res,
                             {n: t[f"L0_ffn_W_{n}"] for n in raw}, raw, raw_loaded)
            w = {n + part: xctx.enter_context(nc.sbuf_tensor("w_" + n + part, [P, K, cols], F32R))
                 for n, cols in (("up", D), ("down", D), ("expert", D)) for part in ("_hi", "_lo")}
            w["gate"] = xctx.enter_context(nc.sbuf_tensor("w_gate", [P, K, 2, t["L0_ffn_W_gate"].shape[0]], F32R))
            w["route"] = xctx.enter_context(nc.sbuf_tensor("w_route", [P, K, E], F32))
            w["route_bias"] = xctx.enter_context(nc.sbuf_tensor("w_route_bias", [P, E], F32))
            dense_and_memory(nc, c, w, t, raw, raw_loaded, x_res, xhat_d, out, logits)
        weights = ExpertWeights(nc, ctx, t["L1_ffn_W1"], t["L1_ffn_W2"], CAPACITY // P // 2)
        slots = SlotTables(nc, ctx, c, TOK // P, E, CAPACITY)
        route(nc, c, logits, CAPACITY, slots, weights)
        experts(nc, c, weights, slots, E, D, xhat_d, out)


_INS = ["x", "ctx_2048", "mask_BxS2_bk0", "g_xattn", "g_ffn", "L0_ffn_W_up", "L0_ffn_W_down", "L0_ffn_W_gate",
        "L0_ffn_W_expert", "L1_ffn_Wg", "L1_ffn_bg", "L1_ffn_W1", "L1_ffn_W2"]


def kernel(**inputs):
    import numpy as _np
    import concourse.bacc as _bacc
    from concourse import mybir as _mybir
    from concourse.bass_utils import run_bass_kernel_spmd as _run

    nc = _bacc.Bacc("TRN2", target_bir_lowering=False, num_devices=1)
    arrays, tensors = {}, {}
    for name in _INS:
        a = _np.ascontiguousarray(inputs[name])
        arrays[f"in_{name}"] = a
        tensors[name] = nc.dram_tensor(f"in_{name}", a.shape, _mybir.dt.from_np(a.dtype), kind="ExternalInput").ap()
    out = nc.dram_tensor("out_x", (16, 256, 512), _mybir.dt.float32, kind="ExternalOutput").ap()
    program(nc, tensors, out)
    r = _run(nc, [arrays], core_ids=[0])
    return r.results[0]["out_x"]
```
